# Optimizing a Trainium2 kernel written in Bass

```python
import numpy as np
import jax
import jax.numpy as jnp

def _softmax(x, axis=-1):
    return jax.nn.softmax(x, axis=axis)

def _gelu(x):
    return jax.nn.gelu(x, approximate=True)

def _silu(x):
    return jax.nn.silu(x)

def _sigmoid(x):
    return jax.nn.sigmoid(x)

def _layernorm(x, axis=-1, eps=1e-05):
    m = jnp.mean(x, axis=axis, keepdims=True)
    v = jnp.var(x, axis=axis, keepdims=True)
    return (x - m) / jnp.sqrt(v + eps)

def _scatter_add(tgt, idx, src, axis=0):
    return tgt.at[idx].add(src)

def _segment_sum(src, seg, n):
    return jax.ops.segment_sum(src, seg, n)
kernel_name = 'mk_flamingo_gated_d2_seqx_r4_9dbcd0'

def setup_inputs(seed: int=0):
    np.random.seed(seed)
    _w = jnp.asarray

    def _rec_inputs():
        import jax
        import jax.numpy as jnp
        _rk = jax.random.key(seed)
        x = 0.002226 + 0.9996 * jax.random.normal(jax.random.fold_in(_rk, 1), (8, 512, 256), jnp.float32)
        _lenS = 512 - jax.random.randint(jax.random.fold_in(_rk, 7), (8,), 0, max(1, 512 // 4) + 1, jnp.int32)
        _lenS2 = 512 - jax.random.randint(jax.random.fold_in(_rk, 8), (8,), 0, max(1, 512 // 4) + 1, jnp.int32)
        _ctx_1024P = jax.random.normal(jax.random.fold_in(_rk, 11), (8, 16, 256), jnp.float32)
        _ctx_1024c = jax.random.dirichlet(jax.random.fold_in(_rk, 511), 0.3 * jnp.ones((16,), jnp.float32), (8, 512))
        _ctx_1024t = jnp.einsum('bsk,bkd->bsd', _ctx_1024c, _ctx_1024P)
        _ctx_1024t = _ctx_1024t * jax.lax.rsqrt(jnp.mean(jnp.square(_ctx_1024t)) + 1e-12) * 0.953939
        ctx_1024 = -0.000125008 + 0.999885 * (_ctx_1024t + 0.3 * jax.random.normal(jax.random.fold_in(_rk, 611), (8, 512, 256), jnp.float32))
        _g = jax.random.normal(jax.random.fold_in(_rk, 9001), (2, 2), jnp.float32)
        _g = jnp.sign(_g) * jnp.maximum(jnp.abs(_g), 1.0) + (_g == 0) * 1.0
        g_xattn = _g[0]
        g_ffn = _g[1]
        return (x, ctx_1024, g_xattn, g_ffn)
    x, ctx_1024, g_xattn, g_ffn = _rec_inputs()

    def _L0_xattn_setup():
        import jax, jax.numpy as jnp
        import numpy as np
        B, M, N, DIM, DH, H = (8, 1024, 64, 256, 128, 8)
        INNER = DH * H
        EPS = 1e-05

        def _layernorm(x, g, b):
            mu = jnp.mean(x, axis=-1, keepdims=True)
            var = jnp.var(x, axis=-1, keepdims=True)
            return (x - mu) * jax.lax.rsqrt(var + EPS) * g + b
        key = jax.random.key(seed)
        ks = jax.random.split(key, 8)
        sd = 0.02
        return {'x': jax.random.normal(ks[0], (B, M, DIM), jnp.float32), 'latents': jax.random.normal(ks[1], (B, N, DIM), jnp.float32), 'gamma_media': jnp.ones((DIM,), jnp.float32), 'beta_media': jnp.zeros((DIM,), jnp.float32), 'gamma_lat': jnp.ones((DIM,), jnp.float32), 'beta_lat': jnp.zeros((DIM,), jnp.float32), 'Wq': jax.random.normal(ks[2], (DIM, INNER), jnp.float32) * sd, 'bq': jnp.zeros((INNER,), jnp.float32), 'Wkv': jax.random.normal(ks[3], (DIM, 2 * INNER), jnp.float32) * sd, 'bkv': jnp.zeros((2 * INNER,), jnp.float32), 'Wo': jax.random.normal(ks[4], (INNER, DIM), jnp.float32) * sd, 'bo': jnp.zeros((DIM,), jnp.float32)}
    _L0_xattn_all = _L0_xattn_setup()
    _L0_xattn_in = {k: v for k, v in _L0_xattn_all.items() if k in ('gamma_media', 'beta_media', 'gamma_lat', 'beta_lat', 'Wq', 'bq', 'Wkv', 'bkv', 'Wo', 'bo')}
    del _L0_xattn_all

    def _L0_ffn_setup():
        import jax, jax.numpy as jnp
        import numpy as np
        key = jax.random.key(seed)
        k1, k2, k3, k4 = jax.random.split(key, 4)
        B, T, M = (4, 512, 256)
        E, F = (16, 1024)
        x = jax.random.normal(k1, (B, T, M), dtype=jnp.float32) * 0.02
        Wg = jax.random.normal(k2, (M, E), dtype=jnp.float32) * 0.02
        w1 = jax.random.normal(k3, (E, M, F), dtype=jnp.float32) * 0.02
        w2 = jax.random.normal(k4, (E, F, M), dtype=jnp.float32) * 0.02
        return {'x': x, 'Wg': Wg, 'w1': w1, 'w2': w2}
    _L0_ffn_all = _L0_ffn_setup()
    _L0_ffn_in = {k: v for k, v in _L0_ffn_all.items() if k in ('Wg', 'w1', 'w2')}
    del _L0_ffn_all

    def _L1_xattn_setup():
        import jax, jax.numpy as jnp
        import numpy as np
        D_MODEL = 256
        N_HEADS = 16
        HEAD_DIM = D_MODEL // N_HEADS
        key = jax.random.key(seed)
        k1, k2, k3, k4, k5, k6 = jax.random.split(key, 6)
        B, T_q, T_kv = (4, 256, 1024)
        s = 1.0 / np.sqrt(D_MODEL)
        return {'query': jax.random.normal(k1, (B, T_q, D_MODEL), dtype=jnp.float32), 'kv_source': jax.random.normal(k2, (B, T_kv, D_MODEL), dtype=jnp.float32), 'w_q': jax.random.normal(k3, (D_MODEL, D_MODEL), dtype=jnp.float32) * s, 'w_k': jax.random.normal(k4, (D_MODEL, D_MODEL), dtype=jnp.float32) * s, 'w_v': jax.random.normal(k5, (D_MODEL, D_MODEL), dtype=jnp.float32) * s, 'w_o': jax.random.normal(k6, (D_MODEL, D_MODEL), dtype=jnp.float32) * s}
    _L1_xattn_all = _L1_xattn_setup()
    _L1_xattn_in = {k: v for k, v in _L1_xattn_all.items() if k in ('w_q', 'w_k', 'w_v', 'w_o')}
    del _L1_xattn_all

    def _L1_ffn_setup():
        import jax, jax.numpy as jnp
        import numpy as np
        DIM = 256
        INTER = 512
        E = 8
        TOPK = 2
        ROUTE_SCALE = 1.0

        def _mlp(x, w1, w2, w3):
            h = jax.nn.silu(x @ w1.T) * (x @ w3.T)
            return h @ w2.T
        key = jax.random.key(seed)
        ks = jax.random.split(key, 10)
        s_in = 0.02
        return {'x': jax.random.normal(ks[0], (4, 512, DIM), dtype=jnp.float32), 'gate_w': jax.random.normal(ks[1], (E, DIM), dtype=jnp.float32) * s_in, 'gate_bias': jax.random.normal(ks[2], (E,), dtype=jnp.float32) * 0.01, 'w1': jax.random.normal(ks[3], (E, INTER, DIM), dtype=jnp.float32) * s_in, 'w2': jax.random.normal(ks[4], (E, DIM, INTER), dtype=jnp.float32) * s_in, 'w3': jax.random.normal(ks[5], (E, INTER, DIM), dtype=jnp.float32) * s_in, 'sw1': jax.random.normal(ks[6], (INTER, DIM), dtype=jnp.float32) * s_in, 'sw2': jax.random.normal(ks[7], (DIM, INTER), dtype=jnp.float32) * s_in, 'sw3': jax.random.normal(ks[8], (INTER, DIM), dtype=jnp.float32) * s_in}
    _L1_ffn_all = _L1_ffn_setup()
    _L1_ffn_in = {k: v for k, v in _L1_ffn_all.items() if k in ('gate_w', 'gate_bias', 'w1', 'w2', 'w3', 'sw1', 'sw2', 'sw3')}
    del _L1_ffn_all
    return {'x': x, 'ctx_1024': ctx_1024, 'g_xattn': g_xattn, 'g_ffn': g_ffn, 'L0_xattn_gamma_media': _L0_xattn_in['gamma_media'], 'L0_xattn_beta_media': _L0_xattn_in['beta_media'], 'L0_xattn_gamma_lat': _L0_xattn_in['gamma_lat'], 'L0_xattn_beta_lat': _L0_xattn_in['beta_lat'], 'L0_xattn_Wq': _L0_xattn_in['Wq'], 'L0_xattn_bq': _L0_xattn_in['bq'], 'L0_xattn_Wkv': _L0_xattn_in['Wkv'], 'L0_xattn_bkv': _L0_xattn_in['bkv'], 'L0_xattn_Wo': _L0_xattn_in['Wo'], 'L0_xattn_bo': _L0_xattn_in['bo'], 'L0_ffn_Wg': _L0_ffn_in['Wg'], 'L0_ffn_w1': _L0_ffn_in['w1'], 'L0_ffn_w2': _L0_ffn_in['w2'], 'L1_xattn_w_q': _L1_xattn_in['w_q'], 'L1_xattn_w_k': _L1_xattn_in['w_k'], 'L1_xattn_w_v': _L1_xattn_in['w_v'], 'L1_xattn_w_o': _L1_xattn_in['w_o'], 'L1_ffn_gate_w': _L1_ffn_in['gate_w'], 'L1_ffn_gate_bias': _L1_ffn_in['gate_bias'], 'L1_ffn_w1': _L1_ffn_in['w1'], 'L1_ffn_w2': _L1_ffn_in['w2'], 'L1_ffn_w3': _L1_ffn_in['w3'], 'L1_ffn_sw1': _L1_ffn_in['sw1'], 'L1_ffn_sw2': _L1_ffn_in['sw2'], 'L1_ffn_sw3': _L1_ffn_in['sw3']}

def reference(x, ctx_1024, g_xattn, g_ffn, L0_xattn_gamma_media, L0_xattn_beta_media, L0_xattn_gamma_lat, L0_xattn_beta_lat, L0_xattn_Wq, L0_xattn_bq, L0_xattn_Wkv, L0_xattn_bkv, L0_xattn_Wo, L0_xattn_bo, L0_ffn_Wg, L0_ffn_w1, L0_ffn_w2, L1_xattn_w_q, L1_xattn_w_k, L1_xattn_w_v, L1_xattn_w_o, L1_ffn_gate_w, L1_ffn_gate_bias, L1_ffn_w1, L1_ffn_w2, L1_ffn_w3, L1_ffn_sw1, L1_ffn_sw2, L1_ffn_sw3):
    import jax
    import jax.numpy as jnp

    def _L0_xattn_ref(x, latents, gamma_media, beta_media, gamma_lat, beta_lat, Wq, bq, Wkv, bkv, Wo, bo):
        import jax, jax.numpy as jnp
        import numpy as np
        B, M, N, DIM, DH, H = (8, 1024, 64, 256, 128, 8)
        INNER = DH * H
        EPS = 1e-05

        def _layernorm(x, g, b):
            mu = jnp.mean(x, axis=-1, keepdims=True)
            var = jnp.var(x, axis=-1, keepdims=True)
            return (x - mu) * jax.lax.rsqrt(var + EPS) * g + b
        b = x.shape[0]
        xn = _layernorm(x, gamma_media, beta_media)
        ln = _layernorm(latents, gamma_lat, beta_lat)
        q = ln @ Wq + bq
        kv_input = jnp.concatenate([xn, ln], axis=1)
        kv = kv_input @ Wkv + bkv
        k, v = jnp.split(kv, 2, axis=-1)

        def to_heads(t):
            return t.reshape(b, t.shape[1], H, DH).transpose(0, 2, 1, 3)
        q, k, v = (to_heads(q), to_heads(k), to_heads(v))
        q = q * DH ** (-0.5)
        sim = jnp.einsum('bhid,bhjd->bhij', q, k)
        attn = jax.nn.softmax(sim, axis=-1)
        out = jnp.einsum('bhij,bhjd->bhid', attn, v)
        out = out.transpose(0, 2, 1, 3).reshape(b, -1, INNER)
        return out @ Wo + bo

    def _L0_ffn_ref(x, Wg, w1, w2):
        import jax, jax.numpy as jnp
        import numpy as np
        d = x.shape[-1]
        xr = x.reshape(-1, d)
        S = xr.shape[0]
        E = Wg.shape[1]
        C = (S + E - 1) // E
        gate = jax.nn.softmax(xr @ Wg, axis=-1)
        idx = jnp.argmax(gate, axis=1)
        gates_s = jnp.take_along_axis(gate, idx[:, None], axis=1)[:, 0]
        onehot = jax.nn.one_hot(idx, E, dtype=jnp.int32)
        loc = jnp.sum((jnp.cumsum(onehot, axis=0) - 1) * onehot, axis=1)
        valid = loc < C
        loc_pad = jnp.minimum(loc, C)
        dispatched = jnp.zeros((E, C + 1, d), dtype=x.dtype).at[idx, loc_pad].set(xr)
        dispatched = dispatched[:, :C]
        h = jax.nn.relu(jnp.einsum('ecm,emf->ecf', dispatched, w1))
        expert_out = jnp.einsum('ecf,efm->ecm', h, w2)
        gathered = expert_out[idx, jnp.minimum(loc, C - 1)]
        combined = gathered * (gates_s * valid.astype(x.dtype))[:, None]
        return combined.reshape(x.shape)

    def _L1_xattn_ref(query, kv_source, w_q, w_k, w_v, w_o):
        import jax, jax.numpy as jnp
        import numpy as np
        D_MODEL = 256
        N_HEADS = 16
        HEAD_DIM = D_MODEL // N_HEADS
        B, T_q, _ = query.shape
        T_kv = kv_source.shape[1]
        q = (query @ w_q.T).reshape(B, T_q, N_HEADS, HEAD_DIM)
        k = (kv_source @ w_k.T).reshape(B, T_kv, N_HEADS, HEAD_DIM)
        v = (kv_source @ w_v.T).reshape(B, T_kv, N_HEADS, HEAD_DIM)
        scale = HEAD_DIM ** (-0.5)
        attn = jax.nn.softmax(jnp.einsum('bqhd,bkhd->bhqk', q, k) * scale, axis=-1)
        out = jnp.einsum('bhqk,bkhd->bqhd', attn, v).reshape(B, T_q, D_MODEL)
        return out @ w_o.T

    def _L1_ffn_ref(x, gate_w, gate_bias, w1, w2, w3, sw1, sw2, sw3):
        import jax, jax.numpy as jnp
        import numpy as np
        DIM = 256
        INTER = 512
        E = 8
        TOPK = 2
        ROUTE_SCALE = 1.0

        def _mlp(x, w1, w2, w3):
            h = jax.nn.silu(x @ w1.T) * (x @ w3.T)
            return h @ w2.T
        shape = x.shape
        xt = x.reshape(-1, DIM)
        T = xt.shape[0]
        logits = xt @ gate_w.T
        scores = jax.nn.softmax(logits.astype(jnp.float32), axis=-1)
        original_scores = scores
        biased = scores + gate_bias
        _, indices = jax.lax.top_k(biased, TOPK)
        weights = jnp.take_along_axis(original_scores, indices, axis=1)
        weights = (weights * ROUTE_SCALE).astype(x.dtype)
        combine = (jax.nn.one_hot(indices, E, dtype=weights.dtype) * weights[..., None]).sum(axis=1)
        y = jnp.zeros_like(xt)
        for e in range(E):
            y = y + _mlp(xt, w1[e], w2[e], w3[e]) * combine[:, e:e + 1]
        z = _mlp(xt, sw1, sw2, sw3)
        return (y + z).reshape(shape)
    x = x + jnp.tanh(g_xattn[0]) * _L0_xattn_ref(ctx_1024, _layernorm(x, axis=-1), L0_xattn_gamma_media, L0_xattn_beta_media, L0_xattn_gamma_lat, L0_xattn_beta_lat, L0_xattn_Wq, L0_xattn_bq, L0_xattn_Wkv, L0_xattn_bkv, L0_xattn_Wo, L0_xattn_bo)
    x = x + jnp.tanh(g_ffn[0]) * _L0_ffn_ref(_layernorm(x, axis=-1), L0_ffn_Wg, L0_ffn_w1, L0_ffn_w2)
    x = x + jnp.tanh(g_xattn[1]) * _L1_xattn_ref(_layernorm(x, axis=-1), ctx_1024, L1_xattn_w_q, L1_xattn_w_k, L1_xattn_w_v, L1_xattn_w_o)
    x = x + jnp.tanh(g_ffn[1]) * _L1_ffn_ref(_layernorm(x, axis=-1), L1_ffn_gate_w, L1_ffn_gate_bias, L1_ffn_w1, L1_ffn_w2, L1_ffn_w3, L1_ffn_sw1, L1_ffn_sw2, L1_ffn_sw3)
    return x

_drawn_inputs = setup_inputs


def setup_inputs(seed=0):
    import zlib

    import numpy as np

    out = dict(_drawn_inputs(seed))
    spreads = {'g_ffn': (-1.0, 0.6),
     'L0_xattn_gamma_media': (1.0, 0.6),
     'L0_xattn_beta_media': (0.0, 0.8),
     'L0_xattn_gamma_lat': (1.0, 0.6),
     'L0_xattn_beta_lat': (0.0, 0.8),
     'L0_xattn_bq': (0.0, 0.8),
     'L0_xattn_bkv': (0.0, 0.1),
     'L0_xattn_bo': (0.0, 0.1)}
    factors = {'L0_xattn_Wq': 8.0,
     'L0_ffn_Wg': 5.686,
     'L0_ffn_w1': 6.641,
     'L0_ffn_w2': 5.517,
     'L1_ffn_gate_w': 8.0,
     'L1_ffn_gate_bias': 8.0,
     'L1_ffn_w1': 8.0,
     'L1_ffn_w2': 8.0,
     'L1_ffn_w3': 8.0,
     'L1_ffn_sw1': 3.278,
     'L1_ffn_sw2': 3.241,
     'L1_ffn_sw3': 3.23}
    for name, (base, spread) in spreads.items():
        noise = np.random.default_rng([zlib.crc32(name.encode()), seed]).standard_normal(out[name].shape)
        drawn = base * np.exp(spread * noise) if base else spread * noise
        out[name] = jnp.asarray(drawn.astype(out[name].dtype))
    for name, factor in factors.items():
        out[name] = (out[name] * factor).astype(out[name].dtype)
    return out
```

```python
from contextlib import ExitStack

import numpy as np
import concourse.bass as bass
from concourse import mybir

ALU = mybir.AluOpType
ACT = mybir.ActivationFunctionType
AX = mybir.AxisListType
F32 = mybir.dt.float32
F32R = mybir.dt.float32r
I32 = mybir.dt.int32

P = 128
B, S, D = 8, 512, 256
TB = S // P
NT = B * TB
DC = D // P
BANK = 512
EPS = 1e-5

H0, DH0 = 8, 128
INNER = H0 * DH0
KV0 = 2 * S
KT0 = KV0 // P


def mm3(pe, out, l_hi, l_lo, r_hi, r_lo, start, stop):
    pe.matmul(out, l_hi, r_hi, start=start, stop=False)
    pe.matmul(out, l_hi, r_lo, start=False, stop=False)
    return pe.matmul(out, l_lo, r_hi, start=False, stop=stop)


def known(v, value):
    return isinstance(v, int) and v == value


def flat(ap):
    n = len(ap.shape) - 1
    names = "abcd"[:n]
    return ap.rearrange(f"p {' '.join(names)} -> p ({' '.join(names)})") if n > 1 else ap


def pick(ap, i):
    one = ap[:, i:i + 1] if isinstance(i, int) else ap[:, bass.ds(i, 1)]
    return one.rearrange("p o n -> p (o n)")


def layer0_attention(nc, t_in, ident, tg, x1_dram):
    with ExitStack() as ctx:
        def sb(name, shape, dt=F32):
            return ctx.enter_context(nc.sbuf_tensor("a_" + name, shape, dt))

        def sem(name):
            return ctx.enter_context(nc.semaphore("a_" + name))

        w_stage = sb("w_stage", [P, 2, 2, DC, DH0])
        wqk = [sb("wqk_hi", [P, 2, 2, DC, DH0], F32R), sb("wqk_lo", [P, 2, 2, DC, DH0], F32R)]
        wv = [sb("wv_hi", [P, DC, INNER], F32R), sb("wv_lo", [P, DC, INNER], F32R)]
        wo = [sb("wo_hi", [P, H0, D], F32R), sb("wo_lo", [P, H0, D], F32R)]
        cols = sb("cols", [P, 4, DC])
        bias = sb("bias", [P, H0, 3])
        head_bias = sb("head_bias", [P, 2, 3])
        tbo = sb("tbo", [P, D])
        x_in = sb("x_in", [P, 2 * TB, D])
        y = sb("y", [P, 2 * TB, D])
        stats = sb("stats", [P, 2 * TB, 6])
        mv = sb("mv", [P, 2 * TB, 2])
        var = sb("var", [P, 2 * TB])
        rstd = sb("rstd", [P, 2 * TB])
        vtmp = sb("vtmp", [P, TB])
        consts = sb("consts", [P, 4])
        x_acc = sb("x_acc", [P, TB, D])
        kvT = [sb("kvT_hi", [P, DC, KV0], F32R), sb("kvT_lo", [P, DC, KV0], F32R)]
        qT = [sb("qT_hi", [P, S], F32R), sb("qT_lo", [P, S], F32R)]
        kT = [sb("kT_hi", [P, KV0], F32R), sb("kT_lo", [P, KV0], F32R)]
        v = [sb("v_hi", [P, KT0, 2 * DH0], F32R), sb("v_lo", [P, KT0, 2 * DH0], F32R)]
        neg_max = sb("neg_max", [P, TB])
        row_sum = sb("row_sum", [P, 2, TB])
        inv_sum = sb("inv_sum", [P, 2, TB])
        prob = sb("prob", [P, TB, KV0])
        pT = [sb("pT_hi", [P, KT0, S], F32R), sb("pT_lo", [P, KT0, S], F32R)]
        inv_row = sb("inv_row", [P, S])
        o_norm = sb("o_norm", [P, S])
        oT = [sb("oT_hi", [P, 2, S], F32R), sb("oT_lo", [P, 2, S], F32R)]

        pj = ctx.enter_context(nc.psum_tensor("a_pj", [P, 2, BANK], F32))
        ps_s = ctx.enter_context(nc.psum_tensor("a_scores", [P, 2, KV0], F32))
        ps_t = ctx.enter_context(nc.psum_tensor("a_probT", [P, 2, BANK], F32))

        loaded = sem("loaded")
        w_load = [sem("w_load_A"), sem("w_load_B")]
        w_split = sem("w_split")
        big_hi = sem("big_hi")
        big_lo = sem("big_lo")
        w_step = sem("w_step")
        consts_set = sem("consts_set")
        tanh_done = sem("tanh_done")
        bias_scaled = sem("bias_scaled")
        head_bias_set = sem("head_bias_set")
        x_load = sem("x_load")
        stats_ready = sem("stats_ready")
        rstd_ready = sem("rstd_ready")
        y_ready = sem("y_ready")
        ln_step = sem("ln_step")
        pj_full = sem("pj_full")
        pj_out = sem("pj_out")
        hi_done = sem("hi_done")
        s_full = sem("s_full")
        max_done = sem("max_done")
        exp_done = sem("exp_done")
        inv_done = sem("inv_done")
        t_full = sem("t_full")
        t_hi = sem("t_hi")
        t_out = sem("t_out")
        inv_row_done = sem("inv_row_done")
        affine_done = sem("affine_done")
        bn_done = sem("bn_done")
        aggr_done = sem("aggr_done")
        o_hi = sem("o_hi")
        o_lo = sem("o_lo")
        acc_init = sem("acc_init")
        stored = sem("stored")

        (x_d, ctx_d, g_x, g_f, gm, bm, gl, bl, wq_d, bq_d, wkv_d, bkv_d, wo_d, bo_d) = t_in
        xv = x_d.rearrange("b (t p) d -> p b t d", p=P)
        cv = ctx_d.rearrange("b (t p) d -> p b t d", p=P)
        x1v = x1_dram.rearrange("b (t p) d -> p b t d", p=P)
        wq_v = wq_d.rearrange("(c p) (h d) -> p h c d", p=P, d=DH0)
        wk_v = wkv_d[:, 0:INNER].rearrange("(c p) (h d) -> p h c d", p=P, d=DH0)
        wv_v = wkv_d[:, INNER:].rearrange("(c p) n -> p c n", p=P)
        wo_v = wo_d.rearrange("(h p) n -> p h n", p=DH0)
        N_CONST = 12

        def pj_start(b, hp):
            return 7 if known(b, 0) and known(hp, 0) else 3 + 68 * b + 16 * hp

        def hi_start(b, hp):
            return 7 + 44 * b + 10 * hp

        def at(v4, i):
            return v4[:, bass.ds(i, 1)].rearrange("p o t d -> p (o t) d")

        def at(v4, i):
            return v4[:, bass.ds(i, 1)].rearrange("p o t d -> p (o t) d")

        def whole(engine_pair, b0):
            pass

        block = ctx.enter_context(nc.Block())

        def batches(eng, pair):
            def batch(b):
                pair(b, 0)
                with eng.Fori(1, 3) as hp:
                    pair(b, hp)
                pair(b, 3)
            batch(0)
            with eng.Fori(1, B - 1) as b:
                batch(b)
            batch(B - 1)

        @block.sync
        def _(sp):
            dma = nc.sync.dma_start
            with nc.allow_non_contiguous_dma(reason="columns of biases, once"):
                for i, a in enumerate((gm, bm, gl, bl)):
                    dma(cols[:, i, :], a.rearrange("(c p) -> p c", p=P)).then_inc(loaded, 16)
                dma(bias[:, :, 0], bq_d.rearrange("(h p) -> p h", p=P)).then_inc(loaded, 16)
                dma(bias[:, :, 1], bkv_d[0:INNER].rearrange("(h p) -> p h", p=P)).then_inc(loaded, 16)
                dma(bias[:, :, 2], bkv_d[INNER:].rearrange("(h p) -> p h", p=P)).then_inc(loaded, 16)
            dma(tbo[:], bo_d.rearrange("(o d) -> o d", o=1).to_broadcast([P, D])).then_inc(loaded, 16)
            dma(tg[:, 0:2], g_x.rearrange("(o d) -> o d", o=1).to_broadcast([P, 2])).then_inc(loaded, 16)
            dma(tg[:, 2:4], g_f.rearrange("(o d) -> o d", o=1).to_broadcast([P, 2])).then_inc(loaded, 16)
            dma(prob[:, 0:2, :], wv_v).then_inc(loaded, 16)
            dma(prob[:, 2:4, :].rearrange("p a (h n) -> p (a h) n", n=D), wo_v).then_inc(loaded, 16)

            def load_tokens(b):
                dma(x_in[:, 0:TB, :], at(cv, b)).then_inc(x_load, 16)
                dma(x_in[:, TB:, :], at(xv, b)).then_inc(x_load, 16)

            def load_w(n, h, par):
                dma(w_stage[:, par, 0], at(wq_v, h)).then_inc(w_load[par], 16)
                dma(w_stage[:, par, 1], at(wk_v, h)).then_inc(w_load[par], 16)

            load_tokens(0)
            load_w(0, 0, 0)
            load_w(1, 1, 1)
            sp.wait_ge(w_split, 1)
            load_w(2, 2, 0)
            sp.wait_ge(w_split, 2)
            load_w(3, 3, 1)

            def batch(b):
                if not known(b, 0):
                    sp.wait_ge(pj_out, pj_start(b, 0) + 4)
                    dma(at(x1v, b - 1), x_acc[:]).then_inc(stored, 16)
                last = known(b, B - 1)
                if not last:
                    sp.wait_ge(acc_init, b + 1)
                    load_tokens(b + 1)
                for hp in range(2 if last else 4):
                    n, h = 8 * b + 2 * hp, (2 * hp + 4) % H0
                    sp.wait_ge(w_split, n + 3)
                    load_w(n + 4, h, 0)
                    sp.wait_ge(w_split, n + 4)
                    load_w(n + 5, h + 1, 1)
            batch(0)
            with sp.Fori(1, B - 1) as b:
                batch(b)
            batch(B - 1)
            sp.wait_ge(pj_out, pj_start(B - 1, 3) + 17)
            dma(x1v[:, B - 1], x_acc[:]).then_inc(stored, 16)
            sp.wait_ge(stored, 16 * B)

        @block.gpsimd
        def _(pool):
            g = nc.gpsimd
            for i, value in enumerate((-0.5, EPS, DH0 ** -0.5, 0.0)):
                g.memset(consts[:, i:i + 1], value).then_inc(consts_set, 1)

            def const(i, shape):
                return consts[:, i:i + 1].to_broadcast(shape)

            def split_w(n, par, after):
                pool.wait_ge(w_load[par], after)
                if not (isinstance(n, int) and n < 2):
                    pool.wait_ge(s_full, 4 * (n - 2) + 1)
                q, every, hi = flat(w_stage[:, par, 0]), flat(w_stage[:, par]), flat(wqk[0][:, par])
                g.tensor_tensor(q, q, const(2, [P, DC * DH0]), ALU.mult).then_inc(w_step, 1)
                pool.wait_ge(w_step, 2 * n + 1)
                g.tensor_tensor(hi, every, const(3, [P, 2 * DC * DH0]), ALU.add).then_inc(w_step, 1)
                pool.wait_ge(w_step, 2 * n + 2)
                g.tensor_tensor(flat(wqk[1][:, par]), every, hi.bitcast(F32), ALU.subtract).then_inc(w_split, 1)

            def inverse_std(b):
                lat = rstd[:, TB:]
                pool.wait_ge(stats_ready, 2 * b + 2)
                g.tensor_tensor(rstd[:], var[:], const(0, [P, 2 * TB]), ALU.pow).then_inc(ln_step, 1)
                pool.wait_ge(ln_step, 5 * b + 1)
                g.tensor_tensor(vtmp[:], lat, lat, ALU.mult).then_inc(ln_step, 1)
                pool.wait_ge(ln_step, 5 * b + 2)
                g.tensor_tensor(vtmp[:], vtmp[:], flat(mv[:, TB:, 1:2]), ALU.mult).then_inc(ln_step, 1)
                pool.wait_ge(ln_step, 5 * b + 3)
                g.tensor_tensor(vtmp[:], vtmp[:], const(1, [P, TB]), ALU.add).then_inc(ln_step, 1)
                pool.wait_ge(ln_step, 5 * b + 4)
                g.tensor_tensor(vtmp[:], vtmp[:], const(0, [P, TB]), ALU.pow).then_inc(ln_step, 1)
                pool.wait_ge(ln_step, 5 * b + 5)
                g.tensor_tensor(lat, lat, vtmp[:], ALU.mult).then_inc(rstd_ready, 1)

            pool.wait_ge(consts_set, 4)
            inverse_std(0)
            split_w(0, 0, 32)
            split_w(1, 1, 32)

            def pair(b, hp):
                n = 8 * b + 2 * hp
                i3 = known(hp, 3)
                if known(b, B - 1) and i3:
                    return
                if i3:
                    inverse_std(b + 1)
                turn = 4 * b + hp
                split_w(n + 2, 0, 32 * turn + 64)
                split_w(n + 3, 1, 32 * turn + 64)
            batches(pool, pair)

        @block.scalar
        def _(act):
            a = nc.scalar.activation
            act.wait_ge(loaded, 16 * N_CONST)
            a(tg[:], tg[:], ACT.Tanh).then_inc(tanh_done, 1)
            a(flat(wv[0][:]), flat(prob[:, 0:2, :]), ACT.Copy).then_inc(big_hi, 1)
            a(flat(wo[0][:]), flat(prob[:, 2:4, :]), ACT.Copy).then_inc(big_hi, 1)

            bank = [0]

            def prologue(u, b):
                for j in range(4):
                    c, half = j % 2, j // 2
                    act.wait_ge(pj_full, u + j + 1)
                    a(kvT[0][:, c, half * S:(half + 1) * S], pj[:, bank[0] % 2, :], ACT.Identity,
                      bias=cols[:, 2 * half + 1, c:c + 1], scale=cols[:, 2 * half, c:c + 1]).then_inc(hi_done, 1)
                    bank[0] += 1

            def qk(u, n, par):
                act.wait_ge(head_bias_set, n + 1)
                for j, (dst, i) in enumerate(((qT[0][:], 0), (kT[0][:, 0:S], 1), (kT[0][:, S:], 1))):
                    act.wait_ge(pj_full, u + j + 1)
                    a(dst, pj[:, bank[0] % 2, :], ACT.Identity, bias=head_bias[:, par, i:i + 1]).then_inc(hi_done, 1)
                    bank[0] += 1

            def values(u, j0):
                for j in (j0, j0 + 1):
                    act.wait_ge(pj_full, u + j - j0 + 1)
                    a(flat(v[0][:, 2 * j:2 * j + 2, :]), pj[:, bank[0] % 2, :], ACT.Copy).then_inc(hi_done, 1)
                    bank[0] += 1

            def prob_high(n, qt):
                for half in range(2):
                    act.wait_ge(t_full, 8 * n + 2 * qt + half + 1)
                    a(pT[0][:, 4 * half:4 * half + 4, qt * P:(qt + 1) * P],
                      ps_t[:, half, :].rearrange("p (k q) -> p k q", k=4), ACT.Copy).then_inc(t_hi, 1)

            def exp(n, qt, par):
                act.wait_ge(max_done, 4 * n + qt + 1)
                if not known(n, 0):
                    act.wait_ge(t_full, 8 * n + 2 * qt - 6)
                a(prob[:, qt, :], ps_s[:, qt % 2, :], ACT.Exp, bias=neg_max[:, qt:qt + 1],
                  accum_out=row_sum[:, par, qt:qt + 1]).then_inc(exp_done, 1)

            def finish_row(u):
                act.wait_ge(pj_full, u + 1)
                a(inv_row[:], pj[:, bank[0] % 2, :], ACT.Copy).then_inc(inv_row_done, 1)
                bank[0] += 2

            def finish_o(u, par):
                act.wait_ge(pj_out, u + 2)
                a(oT[0][:, par, :], o_norm[:], ACT.Identity, bias=head_bias[:, par, 2:3]).then_inc(o_hi, 1)

            prologue(0, 0)
            qk(4, 0, 0)

            def step(b, hp, par, u):
                n = 8 * b + 2 * hp + par
                first = known(n, 0)
                last = known(b, B - 1) and known(hp, 3)
                if not first:
                    prob_high(n - 1, 2)
                exp(n, 0, par)
                if not first:
                    prob_high(n - 1, 3)
                exp(n, 1, par)
                if not first:
                    finish_row(u)
                    finish_o(u, 1 - par)
                    u += 2
                exp(n, 2, par)
                prob_high(n, 0)
                if par == 0:
                    if not first:
                        u += 2
                        bank[0] += 2
                    values(u, 0)
                    u += 2
                elif known(hp, 3) and not last:
                    prologue(u, b + 1)
                    u += 4
                exp(n, 3, par)
                prob_high(n, 1)
                if par == 0:
                    values(u, 2)
                    u += 2
                if par == 0 or not last:
                    qk(u, n + 1, 1 - par)
                    u += 3
                return u

            def pair(b, hp):
                bank[0] = 1
                u = step(b, hp, 0, pj_start(b, hp))
                step(b, hp, 1, u)

            batches(act, pair)
            n, u = 8 * B - 1, pj_start(B - 1, 3) + 13
            prob_high(n, 2)
            prob_high(n, 3)
            bank[0] = u % 2
            finish_row(u)
            finish_o(u, 1)

        @block.vector
        def _(dve):
            ve = nc.vector
            bank = [0]

            def lo(out, ps, hi_ap, bias_ap=None):
                if bias_ap is None:
                    return ve.tensor_tensor(out, ps, hi_ap.bitcast(F32), ALU.subtract)
                return ve.scalar_tensor_tensor(out, ps, bias_ap, hi_ap.bitcast(F32), ALU.add, ALU.subtract)

            def prologue(k, b):
                for j in range(4):
                    c, half = j % 2, j // 2
                    dve.wait_ge(hi_done, k + j + 1)
                    ve.tensor_scalar(pj[:, bank[0] % 2, :], pj[:, bank[0] % 2, :], cols[:, 2 * half, c:c + 1],
                                     cols[:, 2 * half + 1, c:c + 1], ALU.mult, ALU.add).then_inc(affine_done, 1)
                    dve.wait_ge(affine_done, 4 * b + j + 1)
                    span = slice(half * S, (half + 1) * S)
                    lo(kvT[1][:, c, span], pj[:, bank[0] % 2, :], kvT[0][:, c, span]).then_inc(pj_out, 1)
                    bank[0] += 1

            def set_head_bias(h, par):
                ve.tensor_copy(head_bias[:, par, :], pick(bias[:], h)).then_inc(head_bias_set, 1)

            def qk(k, par):
                for j, (dst, src, i) in enumerate(((qT[1][:], qT[0][:], 0), (kT[1][:, 0:S], kT[0][:, 0:S], 1),
                                                   (kT[1][:, S:], kT[0][:, S:], 1))):
                    dve.wait_ge(hi_done, k + j + 1)
                    lo(dst, pj[:, bank[0] % 2, :], src, head_bias[:, par, i:i + 1]).then_inc(pj_out, 1)
                    bank[0] += 1

            def values(k, j0):
                for j in (j0, j0 + 1):
                    dve.wait_ge(hi_done, k + j - j0 + 1)
                    lo(flat(v[1][:, 2 * j:2 * j + 2, :]), pj[:, bank[0] % 2, :], flat(v[0][:, 2 * j:2 * j + 2, :])).then_inc(pj_out, 1)
                    bank[0] += 1

            def prob_low(n, qt):
                for half in range(2):
                    dve.wait_ge(t_hi, 8 * n + 2 * qt + half + 1)
                    dst = pT[1][:, 4 * half:4 * half + 4, qt * P:(qt + 1) * P]
                    src = pT[0][:, 4 * half:4 * half + 4, qt * P:(qt + 1) * P]
                    lo(dst, ps_t[:, half, :].rearrange("p (k q) -> p k q", k=4), src).then_inc(t_out, 1)

            def row_max(n, qt):
                dve.wait_ge(s_full, 4 * n + qt + 1)
                ve.tensor_reduce(neg_max[:, qt:qt + 1], ps_s[:, qt % 2, :], AX.X, ALU.max, negate=True).then_inc(max_done, 1)

            def invert_sums(n, par):
                dve.wait_ge(exp_done, 4 * n + 4)
                ve.reciprocal(inv_sum[:, par, :], row_sum[:, par, :]).then_inc(inv_done, 1)

            def norm_o(n, u):
                dve.wait_ge(inv_row_done, n + 1)
                dve.wait_ge(pj_full, u + 2)
                ve.tensor_tensor(o_norm[:], pj[:, (bank[0] + 1) % 2, :], inv_row[:], ALU.mult).then_inc(pj_out, 2)
                bank[0] += 2

            def o_low(n, par):
                dve.wait_ge(o_hi, n + 1)
                lo(oT[1][:, par, :], o_norm[:], oT[0][:, par, :], head_bias[:, par, 2:3]).then_inc(o_lo, 1)

            def add_out(u):
                for j in range(2):
                    dve.wait_ge(pj_full, u + j + 1)
                    if j == 0:
                        dve.wait_ge(pj_out, u)
                    part = flat(x_acc[:, 2 * j:2 * j + 2, :])
                    ve.scalar_tensor_tensor(part, pj[:, bank[0] % 2, :], tg[:, 0:1], part, ALU.mult, ALU.add).then_inc(pj_out, 1)
                    bank[0] += 1

            def statistics(b):
                dve.wait_ge(x_load, 32 * b + 32)
                T = 2 * TB
                for t in range(T):
                    if t:
                        dve.wait_ge(bn_done, T * b + t)
                    ve.bn_stats(stats[:, t, :], x_in[:, t, :]).then_inc(bn_done, 1)
                    if t:
                        ve.bn_aggr(mv[:, t - 1, :], stats[:, t - 1, :]).then_inc(aggr_done, 1)
                dve.wait_ge(bn_done, T * b + T)
                dve.wait_ge(aggr_done, T * b + T - 1)
                ve.tensor_scalar(var[:, 0:T - 1], flat(mv[:, 0:T - 1, 1:2]), EPS, None, ALU.add).then_inc(stats_ready, 1)
                ve.bn_aggr(mv[:, T - 1, :], stats[:, T - 1, :]).then_inc(aggr_done, 1)
                dve.wait_ge(aggr_done, T * b + T)
                ve.tensor_scalar(var[:, T - 1:], flat(mv[:, T - 1:, 1:2]), EPS, None, ALU.add).then_inc(stats_ready, 1)

            def normalise(b):
                dve.wait_ge(rstd_ready, b + 1)
                for t in range(2 * TB):
                    last = ve.tensor_scalar(y[:, t, :], x_in[:, t, :], mv[:, t, 0:1], rstd[:, t:t + 1], ALU.subtract, ALU.mult)
                    last.then_inc(y_ready, 1)

            def init_acc(b):
                if not known(b, 0):
                    dve.wait_ge(stored, 16 * b)
                ve.tensor_tensor(x_acc[:], x_in[:, TB:, :], tbo[:].rearrange("p (o d) -> p o d", o=1).to_broadcast([P, TB, D]), ALU.add).then_inc(acc_init, 1)
                dve.wait_ge(acc_init, b + 1)

            statistics(0)
            for i, (w, rows) in enumerate(((wv, slice(0, 2)), (wo, slice(2, 4)))):
                dve.wait_ge(big_hi, i + 1)
                ve.tensor_tensor(flat(w[1][:]), flat(prob[:, rows, :]), flat(w[0][:]).bitcast(F32), ALU.subtract).then_inc(big_lo, 1)
            dve.wait_ge(tanh_done, 1)
            ve.tensor_scalar(tbo[:], tbo[:], tg[:, 0:1], None, ALU.mult).then_inc(bias_scaled, 1)
            ve.tensor_scalar(bias[:, :, 0:1], bias[:, :, 0:1], DH0 ** -0.5, None, ALU.mult).then_inc(bias_scaled, 1)
            normalise(0)
            dve.wait_ge(bias_scaled, 2)
            set_head_bias(0, 0)
            prologue(0, 0)
            qk(4, 0)

            def step(b, hp, par, u, k):
                n = 8 * b + 2 * hp + par
                first = known(n, 0)
                pair0 = known(hp, 0)
                pair3 = known(hp, 3)
                last = known(b, B - 1) and pair3
                if not first:
                    invert_sums(n - 1, 1 - par)
                    prob_low(n - 1, 2)
                row_max(n, 0)
                if not first:
                    prob_low(n - 1, 3)
                row_max(n, 1)
                if par == 1 and pair0:
                    init_acc(b)
                if not first:
                    norm_o(n - 1, u)
                    u += 2
                row_max(n, 2)
                if not first:
                    o_low(n - 1, 1 - par)
                if not first:
                    dve.wait_ge(o_lo, n)
                prob_low(n, 0)
                if par == 0 or not last:
                    set_head_bias(2 * hp + 1 if par == 0 else (0 if pair3 else 2 * hp + 2), 1 - par)
                if par == 0:
                    if pair3 and not last:
                        statistics(b + 1)
                    if not first:
                        add_out(u)
                        u += 2
                    values(k, 0)
                    u, k = u + 2, k + 2
                elif pair3 and not last:
                    prologue(k, b + 1)
                    u, k = u + 4, k + 4
                row_max(n, 3)
                prob_low(n, 1)
                if par == 0:
                    values(k, 2)
                    u, k = u + 2, k + 2
                    if pair3 and not last:
                        normalise(b + 1)
                if par == 0 or not last:
                    qk(k, 1 - par)
                    u, k = u + 3, k + 3
                return u, k

            def pair(b, hp):
                bank[0] = 1
                u, k = step(b, hp, 0, pj_start(b, hp), hi_start(b, hp))
                step(b, hp, 1, u, k)

            batches(dve, pair)
            n, u = 8 * B - 1, pj_start(B - 1, 3) + 13
            invert_sums(n, 1)
            prob_low(n, 2)
            prob_low(n, 3)
            bank[0] = u % 2
            norm_o(n, u)
            o_low(n, 1)
            add_out(u + 2)

        @block.tensor
        def _(pe):
            t = nc.tensor
            bank = [0]

            def free_bank(u):
                if not (isinstance(u, int) and u < 2):
                    pe.wait_ge(pj_out, u - 1)

            def prologue(u, b):
                pe.wait_ge(y_ready, 8 * b + 8)
                for j in range(4):
                    c, half = j % 2, j // 2
                    free_bank(u + j)
                    for tt in range(TB):
                        last = t.transpose(pj[:, bank[0] % 2, tt * P:(tt + 1) * P], y[:, half * TB + tt, c * P:(c + 1) * P], ident[:])
                    last.then_inc(pj_full, 1)
                    bank[0] += 1

            def qk(u, n, par):
                pe.wait_ge(w_split, n + 1)
                for j, (i, span) in enumerate(((0, slice(S, KV0)), (1, slice(0, S)), (1, slice(S, KV0)))):
                    free_bank(u + j)
                    for c in range(DC):
                        last = mm3(t, pj[:, bank[0] % 2, :], wqk[0][:, par, i, c], wqk[1][:, par, i, c],
                                   kvT[0][:, c, span], kvT[1][:, c, span], c == 0, c == DC - 1)
                    last.then_inc(pj_full, 1)
                    bank[0] += 1

            def values(u, hp, j0):
                for j in (j0, j0 + 1):
                    free_bank(u + j - j0)
                    for kt in (2 * j, 2 * j + 1):
                        for c in range(DC):
                            cols_ = slice(hp * 256, hp * 256 + 256) if isinstance(hp, int) else bass.ds(hp * 256, 256)
                            last = mm3(t, pj[:, bank[0] % 2, (kt % 2) * 256:(kt % 2) * 256 + 256],
                                       kvT[0][:, c, kt * P:(kt + 1) * P], kvT[1][:, c, kt * P:(kt + 1) * P],
                                       wv[0][:, c, cols_], wv[1][:, c, cols_], c == 0, c == DC - 1)
                    last.then_inc(pj_full, 1)
                    bank[0] += 1

            def scores(n, qt):
                if not (isinstance(n, int) and 4 * n + qt < 2):
                    pe.wait_ge(exp_done, 4 * n + qt - 1)
                for half in range(2):
                    span = slice(half * S, (half + 1) * S)
                    q = slice(qt * P, (qt + 1) * P)
                    last = mm3(t, ps_s[:, qt % 2, span], qT[0][:, q], qT[1][:, q], kT[0][:, span], kT[1][:, span], True, True)
                last.then_inc(s_full, 1)

            def turn(n, qt):
                pe.wait_ge(exp_done, 4 * n + qt + 1)
                for half in range(2):
                    m = 8 * n + 2 * qt + half
                    if not (isinstance(m, int) and m < 2):
                        pe.wait_ge(t_out, m - 1)
                    for k in range(4):
                        kt = 4 * half + k
                        last = t.transpose(ps_t[:, half, k * P:(k + 1) * P], prob[:, qt, kt * P:(kt + 1) * P], ident[:])
                    last.then_inc(t_full, 1)

            def finish(n, par, u):
                pe.wait_ge(inv_done, n + 1)
                free_bank(u)
                for qt in range(TB):
                    last = t.matmul(pj[:, bank[0] % 2, qt * P:(qt + 1) * P], inv_sum[:, par, qt:qt + 1].to_broadcast([P, P]),
                                    ident[:], is_transpose=True)
                last.then_inc(pj_full, 1)
                bank[0] += 1
                free_bank(u + 1)
                pe.wait_ge(t_out, 8 * n + 8)
                for kt in range(KT0):
                    d = slice(par * DH0, (par + 1) * DH0)
                    last = mm3(t, pj[:, bank[0] % 2, :], v[0][:, kt, d], v[1][:, kt, d], pT[0][:, kt, :], pT[1][:, kt, :],
                               kt == 0, kt == KT0 - 1)
                last.then_inc(pj_full, 1)
                bank[0] += 1

            def output(u, n, hp):
                pe.wait_ge(o_lo, n + 1)
                for j in range(2):
                    free_bank(u + j)
                    for tt in (2 * j, 2 * j + 1):
                        for par in range(2):
                            h = 2 * hp + par
                            q = slice(tt * P, (tt + 1) * P)
                            last = mm3(t, pj[:, bank[0] % 2, (tt % 2) * D:(tt % 2) * D + D], oT[0][:, par, q], oT[1][:, par, q],
                                       pick(wo[0][:], h), pick(wo[1][:], h), par == 0, par == 1)
                    last.then_inc(pj_full, 1)
                    bank[0] += 1

            prologue(0, 0)
            pe.wait_ge(pj_out, 4)
            qk(4, 0, 0)

            def step(b, hp, par, u):
                n = 8 * b + 2 * hp + par
                first = known(n, 0)
                pair0 = known(hp, 0)
                pair3 = known(hp, 3)
                last = known(b, B - 1) and pair3
                if not first:
                    turn(n - 1, 2)
                pe.wait_ge(pj_out, u)
                scores(n, 0)
                if not first:
                    turn(n - 1, 3)
                scores(n, 1)
                if not first:
                    finish(n - 1, 1 - par, u)
                    u += 2
                scores(n, 2)
                turn(n, 0)
                if par == 0:
                    if not first:
                        output(u, n - 1, 3 if pair0 else hp - 1)
                        u += 2
                    values(u, hp, 0)
                    u += 2
                elif pair3 and not last:
                    prologue(u, b + 1)
                    u += 4
                scores(n, 3)
                turn(n, 1)
                if par == 0:
                    values(u, hp, 2)
                    u += 2
                if par == 1 and pair3 and not last:
                    pe.wait_ge(pj_out, u)
                if par == 0 or not last:
                    qk(u, n + 1, 1 - par)
                    u += 3
                return u

            def pair(b, hp):
                bank[0] = 1
                u = step(b, hp, 0, pj_start(b, hp))
                step(b, hp, 1, u)

            pe.wait_ge(big_lo, 2)
            batches(pe, pair)
            n, u = 8 * B - 1, pj_start(B - 1, 3) + 13
            turn(n, 2)
            turn(n, 3)
            bank[0] = u % 2
            finish(n, 1, u)
            output(u + 2, n, 3)


E0, F0 = 16, 1024
C0 = (B * S + E0 - 1) // E0
FT0 = F0 // P
CT0 = C0 // P
FAR = 1 << 20


def statistics(dve, ve, x, stats, mv, var, tiles, done, bn_done, aggr_done, stats_ready):
    T = tiles
    for t in range(T):
        if t:
            dve.wait_ge(bn_done, T * done + t)
        ve.bn_stats(stats[:, t, :], x[:, t, :]).then_inc(bn_done, 1)
        if t:
            ve.bn_aggr(mv[:, t - 1, :], stats[:, t - 1, :]).then_inc(aggr_done, 1)
    dve.wait_ge(bn_done, T * done + T)
    dve.wait_ge(aggr_done, T * done + T - 1)
    ve.tensor_scalar(var[:, 0:T - 1], flat(mv[:, 0:T - 1, 1:2]), EPS, None, ALU.add).then_inc(stats_ready, 1)
    ve.bn_aggr(mv[:, T - 1, :], stats[:, T - 1, :]).then_inc(aggr_done, 1)
    dve.wait_ge(aggr_done, T * done + T)
    ve.tensor_scalar(var[:, T - 1:T], flat(mv[:, T - 1:T, 1:2]), EPS, None, ALU.add).then_inc(stats_ready, 1)


def each_batch(eng, batch):
    batch(0)
    with eng.Fori(1, B) as b:
        batch(b)


def pick4(view, b):
    return view[:, bass.ds(b, 1)].rearrange("p o t d -> p (o t) d")


def pick_cols(table, b, n):
    return table[:, n * b:n * b + n] if isinstance(b, int) else table[:, bass.ds(n * b, n)]


def last_axis(ap, n):
    return ap.rearrange("p (a o) -> p a o", o=1).to_broadcast([ap.shape[0], ap.shape[1], n])


def mid_axis(ap, n):
    return ap.rearrange("p (o a) -> p o a", o=1).to_broadcast([ap.shape[0], n, ap.shape[1]])


def layer0_route(nc, x1_dram, wg_d, d_in, K, tg, route_row, route_w):
    with ExitStack() as ctx:
        def sb(name, shape, dt=F32):
            return ctx.enter_context(nc.sbuf_tensor("r_" + name, shape, dt))

        def sem(name):
            return ctx.enter_context(nc.semaphore("r_" + name))

        wg = sb("wg", [P, DC, E0])
        x = sb("x", [P, TB, D])
        y = sb("y", [P, TB, D])
        yT = sb("yT", [P, DC, S])
        stats, mv = sb("stats", [P, TB, 6]), sb("mv", [P, TB, 2])
        var, rstd = sb("var", [P, TB]), sb("rstd", [P, TB])
        neg_max, total, gate = sb("neg_max", [P, TB]), sb("total", [P, TB]), sb("gate", [P, TB])
        rel = sb("rel", [P, TB, E0])
        ex = sb("ex", [P, TB, E0])
        first = sb("first", [P, TB, E0])
        best = sb("best", [P, TB])
        chosen = sb("chosen", [P, TB, E0])
        place = sb("place", [P, TB, E0])
        carry = sb("carry", [P, E0])
        loc, valid, row, tmp = (sb(n, [P, TB]) for n in ("loc", "valid", "row", "tmp"))
        row_i = sb("row_i", [P, TB], I32)
        ps_t = ctx.enter_context(nc.psum_tensor("r_T", [P, 2, BANK], F32))
        ps_l = ctx.enter_context(nc.psum_tensor("r_logits", [P, BANK], F32))
        ps_c = ctx.enter_context(nc.psum_tensor("r_counts", [P, BANK], F32))
        ps_n = ctx.enter_context(nc.psum_tensor("r_counted", [P, BANK], F32))

        wg_load, x_load = sem("wg_load"), sem("x_load")
        bn_done, aggr_done, stats_ready, rstd_ready = sem("bn"), sem("aggr"), sem("stats_ready"), sem("rstd")
        y_ready, t_full, t_out, l_full = sem("y_ready"), sem("t_full"), sem("t_out"), sem("l_full")
        rel_ready, exp_done, chosen_ready, counted = sem("rel"), sem("exp"), sem("chosen"), sem("counted")
        carry_set, row_ready, scattered, step = sem("carry"), sem("row_ready"), sem("scattered"), sem("step")
        turn, weight_set = sem("turn"), sem("weight_set")
        STEPS = 15
        xv = x1_dram.rearrange("b (t p) d -> p b t d", p=P)
        block = ctx.enter_context(nc.Block())

        @block.sync
        def _(sp):
            nc.sync.dma_start(wg[:], wg_d.rearrange("(c p) e -> p c e", p=P)).then_inc(wg_load, 16)
            nc.sync.dma_start(x[:], xv[:, 0]).then_inc(x_load, 16)
            with sp.Fori(1, B) as b:
                sp.wait_ge(y_ready, TB * b)
                nc.sync.dma_start(x[:], pick4(xv, b)).then_inc(x_load, 16)

        @block.gpsimd
        def _(pool):
            def batch(b):
                pool.wait_ge(stats_ready, 2 * b + 2)
                nc.gpsimd.tensor_tensor(rstd[:], var[:], K.neg_half[:].to_broadcast([P, TB]), ALU.pow).then_inc(rstd_ready, 1)
                for t in range(TB):
                    if t == 0:
                        pool.wait_ge(row_ready, b + 1)
                        nc.gpsimd.tensor_tensor(K.pool_scratch[:], K.neg_half[:], K.neg_half[:], ALU.mult).then_inc(turn, 1)
                    nc.gpsimd.indirect_dma_start(d_in, bass.IndirectOffsetOnAxis(ap=row_i[:, t:t + 1], axis=0), y[:, t, :], None,
                                                 bounds_check=E0 * C0 - 1, oob_is_err=False).then_inc(scattered, 16)
            each_batch(pool, batch)
            pool.wait_ge(scattered, 16 * TB * B)

        @block.scalar
        def _(act):
            def batch(b):
                for c in range(DC):
                    act.wait_ge(t_full, DC * b + c + 1)
                    nc.scalar.activation(yT[:, c, :], ps_t[:, c, :], ACT.Copy).then_inc(t_out, 1)
                act.wait_ge(rel_ready, b + 1)
                nc.scalar.activation(flat(ex[:]), flat(rel[:]), ACT.Exp).then_inc(exp_done, 1)
            each_batch(act, batch)

        @block.tensor
        def _(pe):
            t_ = nc.tensor
            pe.wait_ge(wg_load, 16)
            def batch(b):
                pe.wait_ge(y_ready, TB * b + TB)
                for c in range(DC):
                    for t in range(TB):
                        last = t_.transpose(ps_t[:, c, t * P:(t + 1) * P], y[:, t, c * P:(c + 1) * P], K.ident[:])
                    last.then_inc(t_full, 1)
                pe.wait_ge(t_out, DC * b + DC)
                for t in range(TB):
                    for c in range(DC):
                        last = t_.matmul(ps_l[:, t * E0:(t + 1) * E0], yT[:, c, t * P:(t + 1) * P], wg[:, c, :],
                                         start=c == 0, stop=c == DC - 1)
                last.then_inc(l_full, 1)
                pe.wait_ge(chosen_ready, b + 1)
                for t in range(TB):
                    for u in range(t + 1):
                        t_.matmul(ps_c[:, t * E0:(t + 1) * E0], K.before[:] if u == t else K.ones[:], chosen[:, u, :],
                                  start=u == 0, stop=u == t)
                for t in range(TB):
                    last = t_.matmul(ps_n[:, 0:E0], K.ones[:], chosen[:, t, :], start=t == 0, stop=t == TB - 1)
                last.then_inc(counted, 1)
            each_batch(pe, batch)

        @block.vector
        def _(dve):
            ve = nc.vector
            ve.memset(carry[:], 0.0).then_inc(carry_set, 1)
            logits = ps_l[:, 0:TB * E0].rearrange("p (t e) -> p t e", e=E0)
            counts = ps_c[:, 0:TB * E0].rearrange("p (t e) -> p t e", e=E0)
            def batch(b):
                k = [0]

                def then(instruction):
                    k[0] += 1
                    instruction.then_inc(step, 1)
                    dve.wait_ge(step, STEPS * b + k[0])

                dve.wait_ge(x_load, 16 * b + 16)
                statistics(dve, ve, x, stats, mv, var, TB, b, bn_done, aggr_done, stats_ready)
                dve.wait_ge(rstd_ready, b + 1)
                if not known(b, 0):
                    dve.wait_ge(scattered, 16 * TB * b)
                for t in range(TB):
                    ve.tensor_scalar(y[:, t, :], x[:, t, :], mv[:, t, 0:1], rstd[:, t:t + 1], ALU.subtract, ALU.mult).then_inc(y_ready, 1)
                dve.wait_ge(l_full, b + 1)
                then(ve.tensor_reduce(neg_max[:], logits, AX.X, ALU.max, negate=True))
                ve.tensor_tensor(rel[:], logits, last_axis(neg_max[:], E0), ALU.add).then_inc(rel_ready, 1)
                dve.wait_ge(rel_ready, b + 1)
                then(ve.tensor_scalar(first[:], rel[:], 0.0, float(-FAR), ALU.is_equal, ALU.mult))
                then(ve.tensor_tensor(first[:], first[:], mid_axis(K.iota[:, 0:E0], TB), ALU.add))
                then(ve.tensor_reduce(best[:], first[:], AX.X, ALU.min))
                then(ve.tensor_scalar(best[:], best[:], float(FAR), None, ALU.add))
                ve.tensor_tensor(chosen[:], mid_axis(K.iota[:, 0:E0], TB), last_axis(best[:], E0), ALU.is_equal).then_inc(chosen_ready, 1)
                dve.wait_ge(exp_done, b + 1)
                then(ve.tensor_reduce(total[:], ex[:], AX.X, ALU.add))
                then(ve.reciprocal(gate[:], total[:]))
                dve.wait_ge(counted, b + 1)
                then(ve.tensor_tensor(place[:], counts, mid_axis(carry[:], TB), ALU.add))
                then(ve.tensor_tensor(place[:], place[:], chosen[:], ALU.mult))
                ve.tensor_tensor(carry[:], ps_n[:, 0:E0], carry[:], ALU.add).then_inc(carry_set, 1)
                then(ve.tensor_reduce(loc[:], place[:], AX.X, ALU.add))
                then(ve.tensor_scalar(valid[:], loc[:], float(C0), None, ALU.is_lt))
                then(ve.scalar_tensor_tensor(row[:], best[:], float(C0), loc[:], ALU.mult, ALU.add))
                then(ve.tensor_scalar(tmp[:], valid[:], float(-FAR), float(FAR), ALU.mult, ALU.add))
                ve.tensor_tensor(row_i[:], row[:], tmp[:], ALU.add).then_inc(row_ready, 1)
                then(ve.tensor_scalar(loc[:], loc[:], float(C0 - 1), None, ALU.min))
                ve.scalar_tensor_tensor(pick_cols(route_row, b, TB), best[:], float(C0), loc[:], ALU.mult, ALU.add).then_inc(step, 1)
                ve.scalar_tensor_tensor(pick_cols(route_w, b, TB), gate[:], tg[:, 2:3], valid[:], ALU.mult, ALU.mult).then_inc(weight_set, 1)
            each_batch(dve, batch)


def e_at(view, e):
    return view[:, e] if isinstance(e, int) else pick4(view, e)


def early(e, n):
    return isinstance(e, int) and e < n


def layer0_experts(nc, d_in, w1_d, w2_d, d_out, K):
    with ExitStack() as ctx:
        def sb(name, shape, dt=F32):
            return ctx.enter_context(nc.sbuf_tensor("e_" + name, shape, dt))

        def sem(name):
            return ctx.enter_context(nc.semaphore("e_" + name))

        def psum(name, banks):
            return ctx.enter_context(nc.psum_tensor("e_" + name, [P, banks, BANK], F32))

        HB = FT0 // 2
        w1_in, w2_in = sb("w1_in", [P, 2, DC, F0]), sb("w2_in", [P, 2, FT0, D])
        w1 = [sb("w1_hi", [P, 2, DC, F0], F32R), sb("w1_lo", [P, 2, DC, F0], F32R)]
        w2 = [sb("w2_hi", [P, 2, FT0, D], F32R), sb("w2_lo", [P, 2, FT0, D], F32R)]
        rows = sb("rows", [P, 2, CT0, D])
        rT = [sb("rT_hi", [P, 2, DC, C0], F32R), sb("rT_lo", [P, 2, DC, C0], F32R)]
        hT = [sb("hT_hi", [P, 2, FT0, C0], F32R), sb("hT_lo", [P, 2, FT0, C0], F32R)]
        res = sb("res", [P, 2, CT0, D])
        ps_h, ps_t, ps_o = psum("h", HB), psum("t", 1), psum("o", 1)

        w1_load, w2_load, row_load, stored = ([sem(f"{n}{p}") for p in range(2)] for n in ("w1_load", "w2_load", "row_load", "stored"))
        w1_hi, w1_lo, w2_hi, w2_lo = sem("w1_hi"), sem("w1_lo"), sem("w2_hi"), sem("w2_lo")
        t_full, t_hi, t_out = sem("t_full"), sem("t_hi"), sem("t_out")
        h_full, h_hi, h_out = sem("h_full"), sem("h_hi"), sem("h_out")
        o_full, o_out = sem("o_full"), sem("o_out")

        w1_v = w1_d.rearrange("e (c p) f -> p e c f", p=P)
        w2_v = w2_d.rearrange("e (k p) m -> p e k m", p=P)
        in_v = d_in.rearrange("(e t p) d -> p e t d", p=P, t=CT0)
        out_v = d_out.rearrange("(e t p) d -> p e t d", p=P, t=CT0)

        def steps(eng, step):
            step(0, 0, 0)
            step(1, 0, 1)
            with eng.Fori(1, E0 // 2 - 1) as i:
                step(2 * i, i, 0)
                step(2 * i + 1, i, 1)
            step(E0 - 2, E0 // 2 - 1, 0)
            step(E0 - 1, E0 // 2 - 1, 1)

        block = ctx.enter_context(nc.Block())

        @block.sync
        def _(sp):
            def step(e, i, par):
                if not early(e, 2):
                    sp.wait_ge(t_full, e - 1)
                nc.sync.dma_start(rows[:, par], e_at(in_v, e)).then_inc(row_load[par], 16)
                if not early(e, 2):
                    sp.wait_ge(w1_lo, e - 1)
                nc.sync.dma_start(w1_in[:, par], e_at(w1_v, e)).then_inc(w1_load[par], 16)
                if not early(e, 2):
                    sp.wait_ge(w2_lo, e - 1)
                nc.sync.dma_start(w2_in[:, par], e_at(w2_v, e)).then_inc(w2_load[par], 16)
            steps(sp, step)

        @block.gpsimd
        def _(pool):
            def store(e, par):
                pool.wait_ge(o_out, e + 1)
                nc.gpsimd.dma_start(e_at(out_v, e), res[:, par]).then_inc(stored[par], 16)

            def step(e, i, par):
                pool.wait_ge(w1_hi, e + 1)
                nc.gpsimd.tensor_tensor(flat(w1[1][:, par]), flat(w1_in[:, par]), flat(w1[0][:, par]).bitcast(F32), ALU.subtract).then_inc(w1_lo, 1)
                if not early(e, 2):
                    store(e - 2, par)
            steps(pool, step)
            store(E0 - 2, 0)
            store(E0 - 1, 1)
            pool.wait_ge(stored[0], 8 * E0)
            pool.wait_ge(stored[1], 8 * E0)

        @block.scalar
        def _(act):
            a = nc.scalar.activation

            def split_w1(e, i, par):
                act.wait_ge(w1_load[par], 16 * i + 16)
                if not early(e, 2):
                    act.wait_ge(h_full, HB * e - HB)
                a(flat(w1[0][:, par]), flat(w1_in[:, par]), ACT.Copy).then_inc(w1_hi, 1)

            def split_w2(e, i, par):
                act.wait_ge(w2_load[par], 16 * i + 16)
                if not early(e, 2):
                    act.wait_ge(o_full, e - 1)
                a(flat(w2[0][:, par]), flat(w2_in[:, par]), ACT.Copy).then_inc(w2_hi, 1)

            def rows_hi(e, par):
                act.wait_ge(t_full, e + 1)
                a(flat(rT[0][:, par]), ps_t[:, 0, :], ACT.Copy).then_inc(t_hi, 1)

            def step(e, i, par):
                if not early(e, 2):
                    act.wait_ge(o_full, e - 1)
                for j in range(HB):
                    act.wait_ge(h_full, HB * e + j + 1)
                    a(flat(hT[0][:, par, 2 * j:2 * j + 2]), ps_h[:, j, :], ACT.Relu).then_inc(h_hi, 1)
                if not known(e, E0 - 1):
                    rows_hi(e + 1, 1 - par)
                    split_w1(e + 1, i + par, 1 - par)
                split_w2(e, i, par)

            split_w1(0, 0, 0)
            rows_hi(0, 0)
            steps(act, step)

        @block.vector
        def _(dve):
            ve = nc.vector

            def rows_lo(e, par):
                dve.wait_ge(t_hi, e + 1)
                ve.tensor_tensor(flat(rT[1][:, par]), ps_t[:, 0, :], flat(rT[0][:, par]).bitcast(F32), ALU.subtract).then_inc(t_out, 1)

            def result(e, i, par):
                dve.wait_ge(o_full, e + 1)
                if not early(e, 2):
                    dve.wait_ge(stored[par], 16 * i)
                ve.tensor_copy(flat(res[:, par]), ps_o[:, 0, :]).then_inc(o_out, 1)

            def step(e, i, par):
                for j in range(HB):
                    dve.wait_ge(h_hi, HB * e + j + 1)
                    part = slice(2 * j, 2 * j + 2)
                    ve.scalar_tensor_tensor(flat(hT[1][:, par, part]), ps_h[:, j, :], 0.0, flat(hT[0][:, par, part]).bitcast(F32),
                                            ALU.max, ALU.subtract).then_inc(h_out, 1)
                if not known(e, E0 - 1):
                    rows_lo(e + 1, 1 - par)
                dve.wait_ge(w2_hi, e + 1)
                ve.tensor_tensor(flat(w2[1][:, par]), flat(w2_in[:, par]), flat(w2[0][:, par]).bitcast(F32), ALU.subtract).then_inc(w2_lo, 1)
                if not known(e, 0):
                    result(e - 1, i if par else i - 1, 1 - par)

            rows_lo(0, 0)
            steps(dve, step)
            result(E0 - 1, E0 // 2 - 1, 1)

        @block.tensor
        def _(pe):
            t_ = nc.tensor

            def turn_rows(e, i, par):
                pe.wait_ge(row_load[par], 16 * i + 16)
                if not known(e, 0):
                    pe.wait_ge(t_out, e)
                for c in range(DC):
                    for t in range(CT0):
                        last = t_.transpose(ps_t[:, 0, c * C0 + t * P:c * C0 + (t + 1) * P], rows[:, par, t, c * P:(c + 1) * P], K.ident[:])
                last.then_inc(t_full, 1)

            def first_product(e, par):
                pe.wait_ge(t_out, e + 1)
                pe.wait_ge(w1_lo, e + 1)
                for j in range(HB):
                    if not known(e, 0):
                        pe.wait_ge(h_out, HB * (e - 1) + j + 1)
                    for f in (2 * j, 2 * j + 1):
                        for c in range(DC):
                            fs = slice(f * P, (f + 1) * P)
                            last = mm3(t_, ps_h[:, j, (f % 2) * C0:(f % 2 + 1) * C0], w1[0][:, par, c, fs], w1[1][:, par, c, fs],
                                       rT[0][:, par, c], rT[1][:, par, c], c == 0, c == DC - 1)
                    last.then_inc(h_full, 1)

            def second_product(e, par):
                pe.wait_ge(h_out, HB * e + HB)
                pe.wait_ge(w2_lo, e + 1)
                if not known(e, 0):
                    pe.wait_ge(o_out, e)
                for t in range(CT0):
                    rs = slice(t * P, (t + 1) * P)
                    for f in range(FT0):
                        last = mm3(t_, ps_o[:, 0, t * D:(t + 1) * D], hT[0][:, par, f, rs], hT[1][:, par, f, rs],
                                   w2[0][:, par, f], w2[1][:, par, f], f == 0, f == FT0 - 1)
                last.then_inc(o_full, 1)

            def step(e, i, par):
                first_product(e, par)
                if not known(e, E0 - 1):
                    turn_rows(e + 1, i + par, 1 - par)
                if not known(e, 0):
                    second_product(e - 1, 1 - par)

            turn_rows(0, 0, 0)
            steps(pe, step)
            second_product(E0 - 1, 1)


H1, DH1 = 16, 16
G1 = H1 // 4
PAIRS = H1 // 2
KT1 = S // P
VPAD = H1 * P + P


def layer1_attention(nc, x1_dram, ctx_d, wqT_d, wkT_d, wvT_d, woT_d, route_row, route_w, d_out, tg, x3_dram, K):
    with ExitStack() as ctx:
        def sb(name, shape, dt=F32):
            return ctx.enter_context(nc.sbuf_tensor("c_" + name, shape, dt))

        def sem(name):
            return ctx.enter_context(nc.semaphore("c_" + name))

        w_in = sb("w_in", [P, 3, DC, D])
        w_qkv = [sb("w_hi", [P, 3, DC, D], F32R), sb("w_lo", [P, 3, DC, D], F32R)]
        w_o = [sb("wo_hi", [P, G1, D], F32R), sb("wo_lo", [P, G1, D], F32R)]
        x_in, c_in, y, fetched, x_acc = (sb(n, [P, TB, D]) for n in ("x_in", "c_in", "y", "fetched", "x_acc"))
        row_now, w_now = sb("row_now", [P, TB], I32), sb("w_now", [P, TB])
        stats, mv = sb("stats", [P, TB, 6]), sb("mv", [P, TB, 2])
        var, rstd = sb("var", [P, TB]), sb("rstd", [P, TB])
        tT = [sb("tT_hi", [P, DC, S], F32R), sb("tT_lo", [P, DC, S], F32R)]
        q_tok = sb("q_tok", [P, TB, H1, 4, DH1], F32R)
        k_tok = sb("k_tok", [P, TB, H1, 4, DH1], F32R)
        v_tok = sb("v_tok", [P, TB, H1, DH1])
        q_rows = sb("q_rows", [P, PAIRS, S], F32R)
        k_rows = sb("k_rows", [P, PAIRS, S], F32R)
        v_cols = sb("v_cols", [P, KT1, VPAD], F32R)
        neg_max = sb("neg_max", [P, TB])
        row_sum, inv_sum = sb("row_sum", [P, 2, TB, 4]), sb("inv_sum", [P, TB, 4])
        inv_wide = sb("inv_wide", [P, TB, 4, 2 * DH1])
        prob = sb("prob", [P, TB, S])
        pT = [sb("pT_hi", [P, KT1, S], F32R), sb("pT_lo", [P, KT1, S], F32R)]
        inv_row, o_norm = sb("inv_row", [P, S]), sb("o_norm", [P, S])
        oT = [sb("oT_hi", [P, G1, S], F32R), sb("oT_lo", [P, G1, S], F32R)]

        ps_s = ctx.enter_context(nc.psum_tensor("c_scores", [P, 2, 2, BANK], F32))
        ps_t = ctx.enter_context(nc.psum_tensor("c_probT", [P, 2, BANK], F32))
        ps_v = ctx.enter_context(nc.psum_tensor("c_values", [P, BANK], F32))
        pj = ctx.enter_context(nc.psum_tensor("c_pj", [P, BANK], F32))

        w_load, w_hi, w_lo, wo_load, wo_hi, wo_lo = (sem(n) for n in ("w_load", "w_hi", "w_lo", "wo_load", "wo_hi", "wo_lo"))
        cleared = sem("cleared")
        x_load, c_load, rows_set, fetch_done, x2_done = (sem(n) for n in ("x_load", "c_load", "rows_set", "fetch_done", "x2_done"))
        bn_done, aggr_done, stats_ready, rstd_ready, y_ready = (sem(n) for n in ("bn", "aggr", "stats", "rstd", "y"))
        pj_full = sem("pj_full")
        pj_hi = sem("pj_hi")
        pj_out = sem("pj_out")
        v_hi, v_lo = sem("v_hi"), sem("v_lo")
        s_full, max_done, exp_done = sem("s_full"), sem("max_done"), sem("exp_done")
        t_full, t_hi, t_out = sem("t_full"), sem("t_hi"), sem("t_out")
        inv_done, g_full, inv_row_done, o_norm_done, o_hi, o_lo = (
            sem(n) for n in ("inv_done", "g_full", "inv_row_done", "o_norm_done", "o_hi", "o_lo"))
        acc_set, stored, wide_done, w_scaled = sem("acc_set"), sem("stored"), sem("wide_done"), sem("w_scaled")

        xv = x1_dram.rearrange("b (t p) d -> p b t d", p=P)
        cv = ctx_d.rearrange("b (t p) d -> p b t d", p=P)
        x3v = x3_dram.rearrange("b (t p) d -> p b t d", p=P)

        PREP, ALL = 26, 32
        PREP_HI = 8

        def pj_start(b):
            return PREP if known(b, 0) else ALL * b + PREP - 3

        def b_at(view, b):
            return view[:, b] if isinstance(b, int) else pick4(view, b)

        def run(eng, batch):
            batch(0)
            with eng.Fori(1, B - 1) as b:
                batch(b)
            batch(B - 1)

        def diagonal(g, part):
            wide = v_cols[:, :, g * 4 * P:g * 4 * P + 4 * (P + 2 * DH1)].rearrange("p k (j c) -> p k j c", j=4)
            return wide[:, :, :, part * DH1:(part + 1) * DH1]

        block = ctx.enter_context(nc.Block())

        PAIR_STEP = {10: (0,), 11: (1, 2), 12: (3,), 13: (4, 5), 14: (6,), 15: (7,)}
        Q_HIGH, Q_LOW = slice(0, 4, 2), slice(1, 4, 2)
        K_HIGH, K_LOW = slice(0, 2), slice(2, 4)
        V_STEP = {10: 0, 11: 1, 14: 2}

        @block.sync
        def _(sp):
            dma = nc.sync.dma_start
            for i, w in enumerate((wqT_d, wkT_d, wvT_d)):
                dma(w_in[:, i], w.rearrange("(c p) n -> p c n", p=P)).then_inc(w_load, 16)
            dma(x_in[:], xv[:, 0]).then_inc(x_load, 16)
            dma(c_in[:], cv[:, 0]).then_inc(c_load, 16)
            sp.wait_ge(w_lo, 1)
            wo_v = woT_d.rearrange("(g j d) n -> j d g n", g=G1, j=4)
            stage = w_in[:].rearrange("p a c n -> p (a c) n")
            for j in range(4):
                for part in range(2):
                    dma(stage[32 * j + 16 * part:32 * j + 16 * part + 16, 0:G1, :], wo_v[j]).then_inc(wo_load, 16)

            def batch(b):
                if not known(b, B - 1):
                    sp.wait_ge(pj_full, 6 if known(b, 0) else pj_start(b - 1) + CTX_USE)
                    dma(c_in[:], b_at(cv, b + 1)).then_inc(c_load, 16)
                if not known(b, 0):
                    sp.wait_ge(pj_out, pj_start(b) + 3)
                    dma(b_at(x3v, b - 1), x_acc[:]).then_inc(stored, 16)
                if not known(b, B - 1):
                    sp.wait_ge(acc_set, b + 1)
                    dma(x_in[:], b_at(xv, b + 1)).then_inc(x_load, 16)
            CTX_USE = 3 + 1 + 6
            batch(0)
            batch(1)
            with sp.Fori(2, B - 1) as b:
                batch(b)
            batch(B - 1)
            sp.wait_ge(pj_out, pj_start(B - 1) + 3 + 3 + 3)
            dma(x3v[:, B - 1], x_acc[:]).then_inc(stored, 16)
            sp.wait_ge(stored, 16 * B)

        @block.gpsimd
        def _(pool):
            g = nc.gpsimd
            g.memset(v_cols[:].bitcast(F32), 0.0).then_inc(cleared, 1)

            def fetch(b):
                for t in range(TB):
                    if t == 0:
                        pool.wait_ge(rows_set, 2 * b + 2)
                        g.tensor_tensor(K.pool_scratch[:], K.neg_half[:], K.neg_half[:], ALU.mult).then_inc(cleared, 1)
                    g.indirect_dma_start(fetched[:, t, :], None, d_out, bass.IndirectOffsetOnAxis(ap=row_now[:, t:t + 1], axis=0)).then_inc(fetch_done, 16)
                pool.wait_ge(stats_ready, 2 * b + 2)
                g.tensor_tensor(rstd[:], var[:], K.neg_half[:].to_broadcast([P, TB]), ALU.pow).then_inc(rstd_ready, 1)
            each_batch(pool, fetch)

        @block.scalar
        def _(act):
            a = nc.scalar.activation

            def turn_tokens(u, dst, func=ACT.Copy):
                for c in range(DC):
                    act.wait_ge(pj_full, u + c + 1)
                    a(dst[:, c, :], pj[:], ACT.Copy).then_inc(pj_hi, 1)

            def project(u, dst, where):
                for i in range(2):
                    act.wait_ge(pj_full, u + i + 1)
                    for t in range(2):
                        src = pj[:, t * D:(t + 1) * D].rearrange("p (h o d) -> p h o d", h=H1, o=1).to_broadcast([P, H1, 2, DH1])
                        last = a(dst[:, 2 * i + t, :, where, :], src, ACT.Copy)
                    last.then_inc(pj_hi, 1)

            def project_v(u):
                for i in range(2):
                    act.wait_ge(pj_full, u + i + 1)
                    a(flat(v_tok[:, 2 * i:2 * i + 2]), pj[:], ACT.Copy).then_inc(pj_out, 1)

            def pair_rows(u, p):
                act.wait_ge(pj_full, u + 1)
                a(q_rows[:, p, :], pj[:], ACT.Copy).then_inc(pj_out, 1)

            def spread_v(m, g):
                act.wait_ge(cleared, 1)
                a(diagonal(g, 0), v_tok[:, :, 4 * g:4 * g + 4, :], ACT.Copy).then_inc(v_hi, 1)

            def exp(n, h, qt):
                act.wait_ge(max_done, 2 * n + qt // 2 + 1)
                if not known(n, 0):
                    act.wait_ge(t_full, 4 * n + qt - 3)
                a(prob[:, qt, :], ps_s[:, qt // 2, qt % 2, :], ACT.Exp, bias=neg_max[:, qt:qt + 1],
                  accum_out=row_sum[:, h // 4 % 2, qt, h % 4:h % 4 + 1]).then_inc(exp_done, 1)

            def prob_high(n, qt):
                act.wait_ge(t_full, 4 * n + qt + 1)
                a(pT[0][:, :, qt * P:(qt + 1) * P], ps_t[:, qt % 2, :].rearrange("p (k q) -> p k q", k=KT1), ACT.Copy).then_inc(t_hi, 1)

            def finish_group(u, m, g):
                act.wait_ge(pj_full, u + 1)
                a(inv_row[:], pj[:], ACT.Copy).then_inc(pj_out, 1)
                act.wait_ge(o_norm_done, m + 1)
                a(oT[0][:, g, :], o_norm[:], ACT.Copy).then_inc(o_hi, 1)

            act.wait_ge(w_scaled, 1)
            a(flat(w_qkv[0][:]), flat(w_in[:]), ACT.Copy).then_inc(w_hi, 1)
            act.wait_ge(wo_load, 16 * 8)
            stage = w_in[:].rearrange("p a c n -> p (a c) n")
            a(flat(w_o[0][:]), flat(stage[:, 0:G1, :]), ACT.Copy).then_inc(wo_hi, 1)
            turn_tokens(0, tT[0])
            project(2, q_tok, Q_HIGH)
            turn_tokens(4, tT[0])
            project(6, k_tok, K_HIGH)
            project_v(8)
            for p in range(PAIRS):
                pair_rows(10 + 2 * p, p)
            for g in range(3):
                spread_v(g, g)

            def batch(b):
                first, last = known(b, 0), known(b, B - 1)
                u = pj_start(b)
                for h in range(H1):
                    n = H1 * b + h
                    begin = first and h == 0
                    exp(n, h, 0)
                    exp(n, h, 1)
                    if not begin:
                        prob_high(n - 1, 2)
                        prob_high(n - 1, 3)
                    exp(n, h, 2)
                    exp(n, h, 3)
                    if h % 4 == 0 and not begin:
                        finish_group(u, G1 * b + h // 4 - 1, (h // 4 - 1) % G1)
                        u += 1
                    prob_high(n, 0)
                    prob_high(n, 1)
                    if h == 1:
                        spread_v(4 * b + 3, 3)
                        if not first:
                            u += 2
                    if last:
                        continue
                    if h == 5:
                        turn_tokens(u, tT[0])
                        u += 2
                    elif h == 6:
                        project(u, q_tok, Q_HIGH)
                        u += 2
                    elif h == 7:
                        turn_tokens(u, tT[0])
                        u += 2
                    elif h == 8:
                        project(u, k_tok, K_HIGH)
                        u += 2
                    elif h == 9:
                        project_v(u)
                        u += 2
                    for p in PAIR_STEP.get(h, ()):
                        pair_rows(u, p)
                        u += 2
                    if h in V_STEP:
                        spread_v(4 * b + 4 + V_STEP[h], V_STEP[h])
                return u

            u = [0]

            def keep(b):
                u[0] = batch(b)
            run(act, keep)
            n = H1 * B - 1
            prob_high(n, 2)
            prob_high(n, 3)
            finish_group(u[0], G1 * B - 1, 3)

        @block.vector
        def _(dve):
            ve = nc.vector

            def lo(out, ps, hi):
                return ve.tensor_tensor(out, ps, hi.bitcast(F32), ALU.subtract)

            def set_rows(b):
                ve.tensor_copy(row_now[:], pick_cols(route_row, b, TB)).then_inc(rows_set, 1)
                ve.tensor_copy(w_now[:], pick_cols(route_w, b, TB)).then_inc(rows_set, 1)

            def add_experts(b):
                dve.wait_ge(x_load, 16 * b + 16)
                dve.wait_ge(fetch_done, 16 * TB * (b + 1))
                for t in range(TB):
                    ve.scalar_tensor_tensor(x_in[:, t, :], fetched[:, t, :], w_now[:, t:t + 1], x_in[:, t, :], ALU.mult, ALU.add).then_inc(x2_done, 1)
                dve.wait_ge(x2_done, TB * b + TB)
                statistics(dve, ve, x_in, stats, mv, var, TB, b, bn_done, aggr_done, stats_ready)

            def normalise(b):
                dve.wait_ge(rstd_ready, b + 1)
                for t in range(TB):
                    ve.tensor_scalar(y[:, t, :], x_in[:, t, :], mv[:, t, 0:1], rstd[:, t:t + 1], ALU.subtract, ALU.mult).then_inc(y_ready, 1)

            def turn_tokens(k, t):
                for c in range(DC):
                    dve.wait_ge(pj_hi, k + c + 1)
                    lo(t[1][:, c, :], pj[:], t[0][:, c, :]).then_inc(pj_out, 1)

            def project(k, dst, high):
                low = Q_LOW if high == Q_HIGH else K_LOW
                for i in range(2):
                    dve.wait_ge(pj_hi, k + i + 1)
                    for t in range(2):
                        src = pj[:, t * D:(t + 1) * D].rearrange("p (h o d) -> p h o d", h=H1, o=1).to_broadcast([P, H1, 2, DH1])
                        last = lo(dst[:, 2 * i + t, :, low, :], src, dst[:, 2 * i + t, :, high, :])
                    last.then_inc(pj_out, 1)

            def pair_rows(u, p):
                dve.wait_ge(pj_full, u + 2)
                ve.tensor_copy(k_rows[:, p, :], pj[:]).then_inc(pj_out, 1)

            def spread_v(m, g):
                dve.wait_ge(v_hi, m + 1)
                lo(diagonal(g, 1), v_tok[:, :, 4 * g:4 * g + 4, :], diagonal(g, 0)).then_inc(v_lo, 1)

            def row_max(n, pr):
                dve.wait_ge(s_full, 2 * n + pr + 1)
                ve.tensor_reduce(neg_max[:, 2 * pr:2 * pr + 2], ps_s[:, pr], AX.X, ALU.max, negate=True).then_inc(max_done, 1)

            def prob_low(n, qt):
                dve.wait_ge(t_hi, 4 * n + qt + 1)
                q = slice(qt * P, (qt + 1) * P)
                lo(pT[1][:, :, q], ps_t[:, qt % 2, :].rearrange("p (k q) -> p k q", k=KT1), pT[0][:, :, q]).then_inc(t_out, 1)

            def invert_sums(n, m, par):
                dve.wait_ge(exp_done, 4 * n + 4)
                ve.reciprocal(flat(inv_sum[:]), flat(row_sum[:, par])).then_inc(inv_done, 1)
                dve.wait_ge(inv_done, m + 1)
                ve.tensor_copy(inv_wide[:].rearrange("p t j c -> p (t j) c"), last_axis(flat(inv_sum[:]), 2 * DH1)).then_inc(wide_done, 1)

            def finish_group(u, m):
                dve.wait_ge(g_full, m + 1)
                dve.wait_ge(pj_out, u + 1)
                if not known(m, 0):
                    dve.wait_ge(o_lo, m)
                ve.tensor_tensor(o_norm[:], ps_v[:], inv_row[:], ALU.mult).then_inc(o_norm_done, 1)

            def group_low(m, g):
                dve.wait_ge(o_hi, m + 1)
                lo(oT[1][:, g, :], o_norm[:], oT[0][:, g, :]).then_inc(o_lo, 1)

            def add_out(u, b):
                for i in range(2):
                    dve.wait_ge(pj_full, u + i + 1)
                    if i == 0:
                        dve.wait_ge(acc_set, b + 1)
                    part = flat(x_acc[:, 2 * i:2 * i + 2, :])
                    ve.scalar_tensor_tensor(part, pj[:], tg[:, 1:2], part, ALU.mult, ALU.add).then_inc(pj_out, 1)

            def keep_x2(b):
                if not known(b, 0):
                    dve.wait_ge(stored, 16 * b)
                ve.tensor_copy(x_acc[:], x_in[:]).then_inc(acc_set, 1)

            dve.wait_ge(w_load, 48)
            ve.tensor_scalar(flat(w_in[:, 1]), flat(w_in[:, 1]), DH1 ** -0.5, None, ALU.mult).then_inc(w_scaled, 1)
            dve.wait_ge(w_hi, 1)
            lo(flat(w_qkv[1][:]), flat(w_in[:]), flat(w_qkv[0][:])).then_inc(w_lo, 1)
            set_rows(0)
            add_experts(0)
            normalise(0)
            dve.wait_ge(wo_hi, 1)
            stage = w_in[:].rearrange("p a c n -> p (a c) n")
            lo(flat(w_o[1][:]), flat(stage[:, 0:G1, :]), flat(w_o[0][:])).then_inc(wo_lo, 1)
            turn_tokens(0, tT)
            project(2, q_tok, Q_HIGH)
            turn_tokens(4, tT)
            project(6, k_tok, K_HIGH)
            for p in range(PAIRS):
                pair_rows(10 + 2 * p, p)
            for g in range(3):
                spread_v(g, g)

            def batch(b):
                first, last = known(b, 0), known(b, B - 1)
                u, k = pj_start(b), PREP_HI * b + PREP_HI
                for h in range(H1):
                    n = H1 * b + h
                    begin = first and h == 0
                    group_end = h % 4 == 0 and not begin
                    m = G1 * b + h // 4 - 1
                    if group_end:
                        invert_sums(n - 1, m, (h // 4 - 1) % 2)
                    row_max(n, 0)
                    if not begin:
                        prob_low(n - 1, 2)
                        prob_low(n - 1, 3)
                    row_max(n, 1)
                    if group_end:
                        finish_group(u, m)
                        u += 1
                    prob_low(n, 0)
                    if group_end:
                        group_low(m, (h // 4 - 1) % G1)
                    prob_low(n, 1)
                    if h == 1:
                        spread_v(4 * b + 3, 3)
                        if not first:
                            add_out(u, b - 1)
                            u += 2
                    elif h == 2:
                        keep_x2(b)
                    if last:
                        continue
                    if h == 0:
                        set_rows(b + 1)
                    elif h == 4:
                        add_experts(b + 1)
                        normalise(b + 1)
                    elif h == 5:
                        turn_tokens(k, tT)
                        u, k = u + 2, k + 2
                    elif h == 6:
                        project(k, q_tok, Q_HIGH)
                        u, k = u + 2, k + 2
                    elif h == 7:
                        turn_tokens(k, tT)
                        u, k = u + 2, k + 2
                    elif h == 8:
                        project(k, k_tok, K_HIGH)
                        u, k = u + 2, k + 2
                    elif h == 9:
                        u += 2
                    for p in PAIR_STEP.get(h, ()):
                        pair_rows(u, p)
                        u += 2
                    if h in V_STEP:
                        spread_v(4 * b + 4 + V_STEP[h], V_STEP[h])
                return u

            u = [0]

            def keep(b):
                u[0] = batch(b)
            run(dve, keep)
            n = H1 * B - 1
            invert_sums(n, G1 * B - 1, 1)
            prob_low(n, 2)
            prob_low(n, 3)
            finish_group(u[0], G1 * B - 1)
            group_low(G1 * B - 1, 3)
            add_out(u[0] + 1, B - 1)

        @block.tensor
        def _(pe):
            t_ = nc.tensor

            def free(u):
                if not known(u, 0):
                    pe.wait_ge(pj_out, u)

            def turn_tokens(u, src):
                for c in range(DC):
                    free(u + c)
                    for t in range(TB):
                        last = t_.transpose(pj[:, t * P:(t + 1) * P], src[:, t, c * P:(c + 1) * P], K.ident[:])
                    last.then_inc(pj_full, 1)

            def project(u, i):
                free(u)
                for half in range(2):
                    free(u + half)
                    for t in range(2):
                        rows = slice((2 * half + t) * P, (2 * half + t + 1) * P)
                        for c in range(DC):
                            last = mm3(t_, pj[:, t * D:(t + 1) * D], tT[0][:, c, rows], tT[1][:, c, rows],
                                       w_qkv[0][:, i, c], w_qkv[1][:, i, c], c == 0, c == DC - 1)
                    last.then_inc(pj_full, 1)

            def pair_rows(u, p):
                free(u)
                for t in range(TB):
                    last = t_.transpose(pj[:, t * P:(t + 1) * P].bitcast(F32R), flat(q_tok[:, t, 2 * p:2 * p + 2]), K.ident_r[:])
                last.then_inc(pj_full, 1)
                free(u + 1)
                for t in range(TB):
                    last = t_.transpose(pj[:, t * P:(t + 1) * P].bitcast(F32R), flat(k_tok[:, t, 2 * p:2 * p + 2]), K.ident_r[:])
                last.then_inc(pj_full, 1)

            def scores(n, h, pr):
                if not known(n, 0):
                    pe.wait_ge(exp_done, 4 * n + 2 * pr - 2)
                rows = slice(64 * (h % 2), 64 * (h % 2) + 64)
                for i in range(2):
                    qt = 2 * pr + i
                    last = t_.matmul(ps_s[:, pr, i, :], q_rows[rows, h // 2, qt * P:(qt + 1) * P], k_rows[rows, h // 2, :], start=True, stop=True)
                last.then_inc(s_full, 1)

            def turn(n, qt):
                pe.wait_ge(exp_done, 4 * n + qt + 1)
                if not (isinstance(n, int) and 4 * n + qt < 2):
                    pe.wait_ge(t_out, 4 * n + qt - 1)
                for k in range(KT1):
                    last = t_.transpose(ps_t[:, qt % 2, k * P:(k + 1) * P], prob[:, qt, k * P:(k + 1) * P], K.ident[:])
                last.then_inc(t_full, 1)

            def values(n, h, m):
                pe.wait_ge(t_out, 4 * n + 4)
                if h % 4 == 0 and not known(m, 0):
                    pe.wait_ge(o_norm_done, m)
                for kt in range(KT1):
                    for part in range(2):
                        last = t_.matmul(ps_v[:], v_cols[:, kt, h * P:(h + 1) * P], pT[part][:, kt, :],
                                         start=h % 4 == 0 and kt == 0 and part == 0, stop=h % 4 == 3 and kt == KT1 - 1 and part == 1)
                if h % 4 == 3:
                    last.then_inc(g_full, 1)

            def sums(u, m):
                pe.wait_ge(wide_done, m + 1)
                free(u)
                for qt in range(TB):
                    inv = flat(inv_wide[:, qt])
                    last = t_.matmul(pj[:, qt * P:(qt + 1) * P], inv, K.ident[:], is_transpose=True)
                last.then_inc(pj_full, 1)

            def output(u, b):
                pe.wait_ge(o_lo, G1 * b + G1)
                for half in range(2):
                    free(u + half)
                    for t in range(2):
                        q = slice((2 * half + t) * P, (2 * half + t + 1) * P)
                        for g in range(G1):
                            last = mm3(t_, pj[:, t * D:(t + 1) * D], oT[0][:, g, q], oT[1][:, g, q], w_o[0][:, g], w_o[1][:, g], g == 0, g == G1 - 1)
                    last.then_inc(pj_full, 1)

            pe.wait_ge(y_ready, TB)
            turn_tokens(0, y)
            pe.wait_ge(w_lo, 1)
            project(2, 0)
            pe.wait_ge(c_load, 16)
            turn_tokens(4, c_in)
            project(6, 1)
            project(8, 2)
            for p in range(PAIRS):
                pair_rows(10 + 2 * p, p)
            pe.wait_ge(wo_lo, 1)
            free(PREP)
            pe.wait_ge(v_lo, 3)

            def batch(b):
                first, last = known(b, 0), known(b, B - 1)
                u = pj_start(b)
                for h in range(H1):
                    n = H1 * b + h
                    begin = first and h == 0
                    group_end = h % 4 == 0 and not begin
                    m = G1 * b + h // 4 - 1
                    if h == 0:
                        free(u)
                    scores(n, h, 0)
                    if not begin:
                        turn(n - 1, 2)
                        turn(n - 1, 3)
                        if group_end:
                            sums(u, m)
                            u += 1
                        if h == 13:
                            pe.wait_ge(v_lo, 4 * b + 4)
                        elif h == 1:
                            pe.wait_ge(v_lo, 4 * b + 3)
                        values(n - 1, (h - 1) % H1, G1 * b + (h - 1) // 4 if h else m)
                    scores(n, h, 1)
                    turn(n, 0)
                    turn(n, 1)
                    if h == 1 and not first:
                        output(u, b - 1)
                        u += 2
                    if last:
                        continue
                    if h == 5:
                        pe.wait_ge(y_ready, TB * b + 2 * TB)
                        turn_tokens(u, y)
                        u += 2
                    elif h == 6:
                        project(u, 0)
                        u += 2
                    elif h == 7:
                        pe.wait_ge(c_load, 16 * b + 32)
                        turn_tokens(u, c_in)
                        u += 2
                    elif h == 8:
                        project(u, 1)
                        u += 2
                    elif h == 9:
                        project(u, 2)
                        u += 2
                    for p in PAIR_STEP.get(h, ()):
                        if p == 0:
                            free(u)
                        pair_rows(u, p)
                        u += 2
                return u

            u = [0]

            def keep(b):
                u[0] = batch(b)
            run(pe, keep)
            n = H1 * B - 1
            turn(n, 2)
            turn(n, 3)
            sums(u[0], G1 * B - 1)
            values(n, H1 - 1, G1 * B - 1)
            output(u[0] + 1, B - 1)


E1, F1 = 8, 512
EA = E1 + 1
FT1 = F1 // P


def layer1_gate(nc, x3_dram, wg_d, bias_d, K, tg, zT, weight):
    with ExitStack() as ctx:
        def sb(name, shape, dt=F32):
            return ctx.enter_context(nc.sbuf_tensor("g_" + name, shape, dt))

        def sem(name):
            return ctx.enter_context(nc.semaphore("g_" + name))

        wg = sb("wg", [P, DC, E1])
        gate_bias = sb("gate_bias", [P, E1])
        x = sb("x", [P, TB, D])
        y = sb("y", [P, TB, D])
        yT = sb("yT", [P, DC, S])
        stats, mv = sb("stats", [P, TB, 6]), sb("mv", [P, TB, 2])
        var, rstd = sb("var", [P, TB]), sb("rstd", [P, TB])
        neg_max, total, inverse, best = (sb(n, [P, TB]) for n in ("neg_max", "total", "inverse", "best"))
        rel, ex, scores, biased, first, one, two = (sb(n, [P, TB, E1]) for n in ("rel", "ex", "scores", "biased", "first", "one", "two"))
        ps_t = ctx.enter_context(nc.psum_tensor("g_T", [P, 2, DC, BANK], F32))
        ps_l = ctx.enter_context(nc.psum_tensor("g_logits", [P, BANK], F32))

        loaded, x_load = sem("loaded"), sem("x_load")
        bn_done, aggr_done, stats_ready, rstd_ready = sem("bn"), sem("aggr"), sem("stats_ready"), sem("rstd")
        y_ready, t_full, t_out, l_full = sem("y_ready"), sem("t_full"), sem("t_out"), sem("l_full")
        rel_ready, exp_done, z_hi, z_lo, step = sem("rel"), sem("exp"), sem("z_hi"), sem("z_lo"), sem("step")
        weight_set = sem("weight_set")
        STEPS = 21
        xv = x3_dram.rearrange("b (t p) d -> p b t d", p=P)
        block = ctx.enter_context(nc.Block())

        @block.sync
        def _(sp):
            nc.sync.dma_start(x[:], xv[:, 0]).then_inc(x_load, 16)
            nc.sync.dma_start(wg[:], wg_d.rearrange("(c p) e -> p c e", p=P)).then_inc(loaded, 16)
            nc.sync.dma_start(gate_bias[:], bias_d.rearrange("(o d) -> o d", o=1).to_broadcast([P, E1])).then_inc(loaded, 16)
            with sp.Fori(1, B) as b:
                sp.wait_ge(y_ready, TB * b)
                nc.sync.dma_start(x[:], pick4(xv, b)).then_inc(x_load, 16)

        @block.gpsimd
        def _(pool):
            def batch(b):
                pool.wait_ge(stats_ready, 2 * b + 2)
                nc.gpsimd.tensor_tensor(rstd[:], var[:], K.neg_half[:].to_broadcast([P, TB]), ALU.pow).then_inc(rstd_ready, 1)
            each_batch(pool, batch)

        @block.scalar
        def _(act):
            def batch(b):
                if not known(b, 0):
                    act.wait_ge(z_lo, b)
                for c in range(DC):
                    act.wait_ge(t_full, DC * b + c + 1)
                    nc.scalar.activation(yT[:, c, :], ps_t[:, 0, c, :], ACT.Copy).then_inc(t_out, 1)
                act.wait_ge(rel_ready, b + 1)
                nc.scalar.activation(flat(ex[:]), flat(rel[:]), ACT.Exp).then_inc(exp_done, 1)
            each_batch(act, batch)

        @block.tensor
        def _(pe):
            t_ = nc.tensor
            pe.wait_ge(loaded, 32)
            def batch(b):
                pe.wait_ge(y_ready, TB * b + TB)
                for c in range(DC):
                    for t in range(TB):
                        last = t_.transpose(ps_t[:, 0, c, t * P:(t + 1) * P], y[:, t, c * P:(c + 1) * P], K.ident[:])
                    last.then_inc(t_full, 1)
                pe.wait_ge(t_out, DC * b + DC)
                for t in range(TB):
                    for c in range(DC):
                        last = t_.matmul(ps_l[:, t * E1:(t + 1) * E1], yT[:, c, t * P:(t + 1) * P], wg[:, c, :],
                                         start=c == 0, stop=c == DC - 1)
                last.then_inc(l_full, 1)
            each_batch(pe, batch)

        @block.vector
        def _(dve):
            ve = nc.vector
            ve.tensor_copy(weight[:, E1, :], tg[:, 3:4].to_broadcast([P, NT])).then_inc(weight_set, 1)
            logits = ps_l[:, 0:TB * E1].rearrange("p (t e) -> p t e", e=E1)
            dve.wait_ge(loaded, 32)
            def batch(b):
                k = [0]

                def then(instruction):
                    k[0] += 1
                    instruction.then_inc(step, 1)
                    dve.wait_ge(step, STEPS * b + k[0])

                def first_maximum(values, hot):
                    then(ve.tensor_reduce(neg_max[:], values[:], AX.X, ALU.max, negate=True))
                    then(ve.tensor_tensor(first[:], values[:], last_axis(neg_max[:], E1), ALU.add))
                    then(ve.tensor_scalar(first[:], first[:], 0.0, float(-FAR), ALU.is_equal, ALU.mult))
                    then(ve.tensor_tensor(first[:], first[:], mid_axis(K.iota[:, 0:E1], TB), ALU.add))
                    then(ve.tensor_reduce(best[:], first[:], AX.X, ALU.min))
                    then(ve.tensor_scalar(best[:], best[:], float(FAR), None, ALU.add))
                    then(ve.tensor_tensor(hot[:], mid_axis(K.iota[:, 0:E1], TB), last_axis(best[:], E1), ALU.is_equal))

                dve.wait_ge(x_load, 16 * b + 16)
                statistics(dve, ve, x, stats, mv, var, TB, b, bn_done, aggr_done, stats_ready)
                dve.wait_ge(rstd_ready, b + 1)
                for t in range(TB):
                    ve.tensor_scalar(y[:, t, :], x[:, t, :], mv[:, t, 0:1], rstd[:, t:t + 1], ALU.subtract, ALU.mult).then_inc(y_ready, 1)
                dve.wait_ge(t_out, DC * b + DC)
                part = bass.ds(S * b, S) if not isinstance(b, int) else slice(S * b, S * b + S)
                ve.tensor_scalar(zT[0][:, :, part], yT[:], 1.0, None, ALU.mult).then_inc(z_hi, 1)
                dve.wait_ge(z_hi, b + 1)
                ve.tensor_tensor(zT[1][:, :, part], yT[:], zT[0][:, :, part].bitcast(F32), ALU.subtract).then_inc(z_lo, 1)
                dve.wait_ge(l_full, b + 1)
                then(ve.tensor_reduce(neg_max[:], logits, AX.X, ALU.max, negate=True))
                ve.tensor_tensor(rel[:], logits, last_axis(neg_max[:], E1), ALU.add).then_inc(rel_ready, 1)
                dve.wait_ge(exp_done, b + 1)
                then(ve.tensor_reduce(total[:], ex[:], AX.X, ALU.add))
                then(ve.reciprocal(inverse[:], total[:]))
                then(ve.tensor_tensor(scores[:], ex[:], last_axis(inverse[:], E1), ALU.mult))
                then(ve.tensor_tensor(biased[:], scores[:], mid_axis(gate_bias[:], TB), ALU.add))
                first_maximum(biased, one)
                then(ve.scalar_tensor_tensor(biased[:], one[:], -3.0e38, biased[:], ALU.mult, ALU.add))
                first_maximum(biased, two)
                then(ve.tensor_tensor(one[:], one[:], two[:], ALU.add))
                cols = weight[:, 0:E1, pick_range(b, TB)]
                ve.scalar_tensor_tensor(cols, one[:].rearrange("p t e -> p e t"), tg[:, 3:4],
                                        scores[:].rearrange("p t e -> p e t"), ALU.mult, ALU.mult).then_inc(weight_set, 1)
                assert k[0] == STEPS, k[0]
            each_batch(dve, batch)


def pick_range(b, n):
    return slice(n * b, n * b + n) if isinstance(b, int) else bass.ds(n * b, n)


def layer1_experts(nc, x3_dram, w1_d, w3_d, w2_d, zT, weight, out_dram):
    with ExitStack() as ctx:
        def sb(name, shape, dt=F32):
            return ctx.enter_context(nc.sbuf_tensor("m_" + name, shape, dt))

        def sem(name):
            return ctx.enter_context(nc.semaphore("m_" + name))

        w_in = sb("w_in", [P, 3, DC * F1])
        w = [sb("w_hi", [P, 2, 3, DC * F1], F32R), sb("w_lo", [P, 2, 3, DC * F1], F32R)]
        acc = sb("acc", [P, NT, D])
        act_h = sb("act_h", [P, 2, S])
        g = sb("g", [P, 2, S])
        hT = [sb("hT_hi", [P, 2, FT1, S], F32R), sb("hT_lo", [P, 2, FT1, S], F32R)]
        ps_h = ctx.enter_context(nc.psum_tensor("m_h", [P, 2, 2, BANK], F32))
        ps_o = ctx.enter_context(nc.psum_tensor("m_o", [P, TB, D], F32))

        x_load, w_load, w_hi, w_lo = sem("x_load"), sem("w_load"), sem("w_hi"), sem("w_lo")
        h_full, silu_done = sem("h_full"), sem("silu_done")
        g_ready = sem("g_ready")
        h_out = sem("h_out")
        o_full, acc_done, stored = sem("o_full"), sem("acc_done"), sem("stored")

        views = [w1_d.rearrange("e (c p) f -> p e c f", p=P), w3_d.rearrange("e (c p) f -> p e c f", p=P),
                 w2_d.rearrange("e (k p) m -> p e k m", p=P)]

        def experts(eng, expert):
            expert(0, 0)
            with eng.Fori(0, E1 // 2) as k:
                expert(2 * k + 1, 1)
                expert(2 * k + 2, 0)

        def batches(eng, e, slot, step):
            step(e, 0, 0, slot)
            step(e, 1, 1, slot)
            with eng.Fori(1, B // 2) as i:
                step(e, 2 * i, 0, slot)
                step(e, 2 * i + 1, 1, slot)

        block = ctx.enter_context(nc.Block())

        @block.sync
        def _(sp):
            def load(e):
                for j in range(3):
                    view = views[j]
                    src = view[:, e] if isinstance(e, int) else pick4(view, e)
                    n = src.shape[1]
                    nc.sync.dma_start(w_in[:, j].rearrange("p (c f) -> p c f", c=n), src).then_inc(w_load, 16)
            load(0)
            nc.sync.dma_start(acc[:], x3_dram.rearrange("b (t p) d -> p (b t) d", p=P)).then_inc(x_load, 16)
            with sp.Fori(1, EA) as e:
                sp.wait_ge(w_lo, 3 * e)
                load(e)
            ov = out_dram.rearrange("b (t p) d -> p b t d", p=P)
            for b in range(B):
                sp.wait_ge(acc_done, TB * (B * E1 + b + 1))
                nc.sync.dma_start(ov[:, b], acc[:, TB * b:TB * b + TB, :]).then_inc(stored, 16)
            sp.wait_ge(stored, 16 * B)

        @block.scalar
        def _(act):
            def split(e, slot):
                for j in range(3):
                    act.wait_ge(w_load, 48 * e + 48)
                    if not known(e, 0) and not known(e, 1):
                        act.wait_ge(o_full, B * e - B)
                    nc.scalar.activation(w[0][:, slot, j], w_in[:, j], ACT.Copy).then_inc(w_hi, 1)

            def step(e, b, par, slot):
                n = B * e + b
                for f in range(FT1):
                    act.wait_ge(h_full, FT1 * n + f + 1)
                    if not known(n, 0) or f >= 2:
                        act.wait_ge(g_ready, 2 * (FT1 * n + f - 1))
                    nc.scalar.activation(act_h[:, f % 2], ps_h[:, f % 2, 0], ACT.Silu).then_inc(silu_done, 1)

            split(0, 0)
            expert_s(act, step, split, 0, 0)
            with act.Fori(0, E1 // 2 - 1) as k:
                expert_s(act, step, split, 2 * k + 1, 1)
                expert_s(act, step, split, 2 * k + 2, 0)
            expert_s(act, step, split, E1 - 1, 1)
            expert_s(act, step, None, E1, 0)

        @block.gpsimd
        def _(pool):
            def lows(e, slot):
                for j in range(3):
                    pool.wait_ge(w_hi, 3 * e + j + 1)
                    nc.gpsimd.tensor_tensor(w[1][:, slot, j], w_in[:, j], w[0][:, slot, j].bitcast(F32), ALU.subtract).then_inc(w_lo, 1)

            def step(e, b, par, slot):
                n = B * e + b
                for f in range(FT1):
                    pool.wait_ge(g_ready, 2 * (FT1 * n + f + 1))
                    nc.gpsimd.tensor_tensor(hT[1][:, par, f], g[:, f % 2], hT[0][:, par, f].bitcast(F32), ALU.subtract).then_inc(h_out, 1)
            lows(0, 0)
            expert_s(pool, step, lows, 0, 0)
            with pool.Fori(0, E1 // 2 - 1) as k:
                expert_s(pool, step, lows, 2 * k + 1, 1)
                expert_s(pool, step, lows, 2 * k + 2, 0)
            expert_s(pool, step, lows, E1 - 1, 1)
            expert_s(pool, step, None, E1, 0)

        @block.vector
        def _(dve):
            ve = nc.vector
            dve.wait_ge(x_load, 16)

            def combine(e, b, n):
                dve.wait_ge(o_full, n + 1)
                if not known(n, 0):
                    dve.wait_ge(acc_done, TB * n)
                for t in range(TB):
                    at = TB * b + t
                    ve.scalar_tensor_tensor(pick(acc[:], at), ps_o[:, t, :], pick_cols(weight_flat, NT * e + at, 1), pick(acc[:], at),
                                            ALU.mult, ALU.add).then_inc(acc_done, 1)

            weight_flat = flat(weight[:])

            def step(e, b, par, slot):
                n = B * e + b
                for f in range(FT1):
                    dve.wait_ge(silu_done, FT1 * n + f + 1)
                    if f == 0 and not early(n, 2):
                        dve.wait_ge(o_full, n - 1)
                    ve.tensor_tensor(hT[0][:, par, f], act_h[:, f % 2], ps_h[:, f % 2, 1], ALU.mult).then_inc(g_ready, 1)
                    if not known(n, 0) or f >= 2:
                        dve.wait_ge(h_out, FT1 * n + f - 1)
                    ve.tensor_tensor(g[:, f % 2], act_h[:, f % 2], ps_h[:, f % 2, 1], ALU.mult).then_inc(g_ready, 1)
                if not known(n, 0):
                    if known(b, 0):
                        combine(e - 1, B - 1, n - 1)
                    else:
                        combine(e, b - 1, n - 1)

            experts(dve, lambda e, slot: batches(dve, e, slot, step))
            combine(E1, B - 1, B * EA - 1)

        @block.tensor
        def _(pe):
            t_ = nc.tensor

            def first_products(e, b, slot):
                n = B * e + b
                if known(b, 0):
                    pe.wait_ge(w_lo, 3 * e + 3)
                for f in range(FT1):
                    if not known(n, 0) or f >= 2:
                        pe.wait_ge(g_ready, 2 * (FT1 * n + f - 1))
                    for j in range(2):
                        for c in range(DC):
                            ws = slice(c * F1 + f * P, c * F1 + (f + 1) * P)
                            z = [part[:, c, pick_range(b, S)] for part in zT]
                            last = mm3(t_, ps_h[:, f % 2, j], w[0][:, slot, j, ws], w[1][:, slot, j, ws], z[0], z[1],
                                       c == 0, c == DC - 1)
                    last.then_inc(h_full, 1)

            def second_product(n, par, slot):
                pe.wait_ge(h_out, FT1 * n + FT1)
                if not known(n, 0):
                    pe.wait_ge(acc_done, TB * n)
                for t in range(TB):
                    rs = slice(t * P, (t + 1) * P)
                    for f in range(FT1):
                        last = mm3(t_, ps_o[:, t, :], hT[0][:, par, f, rs], hT[1][:, par, f, rs],
                                   w[0][:, slot, 2, f * D:(f + 1) * D], w[1][:, slot, 2, f * D:(f + 1) * D], f == 0, f == FT1 - 1)
                last.then_inc(o_full, 1)

            def step(e, b, par, slot):
                first_products(e, b, slot)
                n = B * e + b
                if not known(n, 0):
                    second_product(n - 1, 1 - par, 1 - slot if known(b, 0) else slot)

            experts(pe, lambda e, slot: batches(pe, e, slot, step))
            second_product(B * EA - 1, 1, 0)


def expert_s(eng, step, split, e, slot):
    step(e, 0, 0, slot)
    step(e, 1, 1, slot)
    if split:
        split(e + 1, 1 - slot)
    with eng.Fori(1, B // 2) as i:
        step(e, 2 * i, 0, slot)
        step(e, 2 * i + 1, 1, slot)


class Constants:

    def __init__(self, nc, ctx):
        def sb(name, shape, dt=F32):
            return ctx.enter_context(nc.sbuf_tensor("k_" + name, shape, dt))

        self.ident = sb("ident", [P, P])
        self.ident_r = sb("ident_r", [P, P], F32R)
        self.ones = sb("ones", [P, P])
        self.before = sb("before", [P, P])
        self.iota = sb("iota", [P, 32])
        self.neg_half = sb("neg_half", [P, 1])
        self.pool_scratch = sb("pool_scratch", [P, 1])
        self.iota_i = sb("iota_i", [P, 32], I32)

    def fill(self, nc, ctx):
        step = ctx.enter_context(nc.semaphore("k_step"))
        with nc.Block() as block:
            @block.gpsimd
            def _(pool):
                g = nc.gpsimd
                g.memset(self.ident[:], 0.0).then_inc(step, 1)
                g.memset(self.ones[:], 1.0).then_inc(step, 1)
                g.memset(self.before[:], 1.0).then_inc(step, 1)
                g.memset(self.neg_half[:], -0.5).then_inc(step, 1)
                g.iota(self.iota_i[:], pattern=[[1, 32]], base=0, channel_multiplier=0).then_inc(step, 1)
                pool.wait_ge(step, 5)
                g.affine_select(out=self.ident[:], in_=self.ident[:], compare_op=ALU.not_equal, fill=1.0, base=0,
                                pattern=[[-1, P]], channel_multiplier=1).then_inc(step, 1)
                g.affine_select(out=self.before[:], in_=self.before[:], compare_op=ALU.is_gt, fill=0.0, base=0,
                                pattern=[[1, P]], channel_multiplier=-1).then_inc(step, 1)
                g.tensor_copy(self.iota[:], self.iota_i[:]).then_inc(step, 1)
                pool.wait_ge(step, 8)
                g.tensor_copy(self.ident_r[:], self.ident[:]).then_inc(step, 1)
                pool.wait_ge(step, 9)


def clear(nc, tables):
    with ExitStack() as ctx:
        zero = ctx.enter_context(nc.sbuf_tensor("z_zero", [P, 4096], F32))
        z, done = ctx.enter_context(nc.semaphore("z_z")), ctx.enter_context(nc.semaphore("z_done"))
        with nc.Block() as block:
            @block.vector
            def _(dve):
                nc.vector.memset(zero[:], 0.0).then_inc(z, 1)

            @block.sync
            def _(sp):
                sp.wait_ge(z, 1)
                n = 0
                for table in tables:
                    v = table.rearrange("(p r) d -> p (r d)", p=P)
                    for at in range(0, v.shape[1], 4096):
                        w = min(4096, v.shape[1] - at)
                        nc.sync.dma_start(v[:, at:at + w], zero[:, 0:w]).then_inc(done, 16)
                        n += 16
                sp.wait_ge(done, n)


def load_gates(nc, g_xattn, g_ffn, tg):
    with ExitStack() as ctx:
        loaded, done = ctx.enter_context(nc.semaphore("t_loaded")), ctx.enter_context(nc.semaphore("t_done"))
        with nc.Block() as block:
            @block.sync
            def _(sp):
                nc.sync.dma_start(tg[:, 0:2], g_xattn.rearrange("(o d) -> o d", o=1).to_broadcast([P, 2])).then_inc(loaded, 16)
                nc.sync.dma_start(tg[:, 2:4], g_ffn.rearrange("(o d) -> o d", o=1).to_broadcast([P, 2])).then_inc(loaded, 16)

            @block.scalar
            def _(act):
                act.wait_ge(loaded, 32)
                nc.scalar.activation(tg[:], tg[:], ACT.Tanh).then_inc(done, 1)
                act.wait_ge(done, 1)


def flamingo(nc, t_in, out):
    with ExitStack() as ctx:
        def dram(name, shape):
            return nc.dram_tensor(name, shape, F32).ap()

        K = Constants(nc, ctx)
        tg = ctx.enter_context(nc.sbuf_tensor("tg", [P, 4], F32))
        x1, x3 = dram("x1_dram", (B, S, D)), dram("x3_dram", (B, S, D))
        rows_in, rows_out = dram("rows_in_dram", (E0 * C0, D)), dram("rows_out_dram", (E0 * C0, D))
        K.fill(nc, ctx)
        clear(nc, [rows_in])
        layer0_attention(nc, tuple(t_in[n] for n in (
            "x", "ctx_1024", "g_xattn", "g_ffn", "L0_xattn_gamma_media", "L0_xattn_beta_media", "L0_xattn_gamma_lat",
            "L0_xattn_beta_lat", "L0_xattn_Wq", "L0_xattn_bq", "L0_xattn_Wkv", "L0_xattn_bkv", "L0_xattn_Wo", "L0_xattn_bo")),
            K.ident, tg, x1)
        with ExitStack() as routed:
            route_row = routed.enter_context(nc.sbuf_tensor("route_row", [P, NT], I32))
            route_w = routed.enter_context(nc.sbuf_tensor("route_w", [P, NT], F32))
            layer0_route(nc, x1, t_in["L0_ffn_Wg"], rows_in, K, tg, route_row, route_w)
            layer0_experts(nc, rows_in, t_in["L0_ffn_w1"], t_in["L0_ffn_w2"], rows_out, K)
            layer1_attention(nc, x1, t_in["ctx_1024"], t_in["L1_xattn_w_q"], t_in["L1_xattn_w_k"], t_in["L1_xattn_w_v"],
                             t_in["L1_xattn_w_o"], route_row, route_w, rows_out, tg, x3, K)
        zT = [ctx.enter_context(nc.sbuf_tensor("zT_hi", [P, DC, B * S], F32R)),
              ctx.enter_context(nc.sbuf_tensor("zT_lo", [P, DC, B * S], F32R))]
        weight = ctx.enter_context(nc.sbuf_tensor("weight", [P, EA, NT], F32))
        layer1_gate(nc, x3, t_in["L1_ffn_gate_w"], t_in["L1_ffn_gate_bias"], K, tg, zT, weight)
        layer1_experts(nc, x3, t_in["w1_all"], t_in["w3_all"], t_in["w2_all"], zT, weight, out)



def kernel(**inputs):
    import concourse.bacc as bacc
    from concourse.bass_utils import run_bass_kernel_spmd

    arrays = {k: np.asarray(v) for k, v in inputs.items()}
    for j in (1, 2, 3):
        experts, shared = arrays.pop(f"L1_ffn_w{j}"), arrays.pop(f"L1_ffn_sw{j}")
        arrays[f"w{j}_all"] = np.concatenate([experts, shared[None]]).transpose(0, 2, 1)
    for name in ("L1_xattn_w_q", "L1_xattn_w_k", "L1_xattn_w_v", "L1_xattn_w_o", "L1_ffn_gate_w"):
        arrays[name] = arrays[name].T
    arrays = {k: np.ascontiguousarray(v) for k, v in arrays.items()}

    nc = bacc.Bacc("TRN2", target_bir_lowering=False, num_devices=1)
    t_in = {k: nc.dram_tensor(k + "_in", v.shape, mybir.dt.from_np(v.dtype), kind="ExternalInput").ap() for k, v in arrays.items()}
    out = nc.dram_tensor("out", (B, S, D), F32, kind="ExternalOutput").ap()
    flamingo(nc, t_in, out)
    r = run_bass_kernel_spmd(nc, [{k + "_in": v for k, v in arrays.items()}], core_ids=[0])
    return r.results[0]["out"]
```

```python
from contextlib import ExitStack

import numpy as np
import concourse.bass as bass
from concourse import mybir

ALU = mybir.AluOpType
ACT = mybir.ActivationFunctionType
AX = mybir.AxisListType
F32 = mybir.dt.float32
F32R = mybir.dt.float32r
I32 = mybir.dt.int32

P = 128
B, S, D = 8, 512, 256
TB = S // P
NT = B * TB
DC = D // P
BANK = 512
EPS = 1e-5

H0, DH0 = 8, 128
INNER = H0 * DH0
KV0 = 2 * S
KT0 = KV0 // P


def mm3(pe, out, l_hi, l_lo, r_hi, r_lo, start, stop):
    pe.matmul(out, l_hi, r_hi, start=start, stop=False)
    pe.matmul(out, l_hi, r_lo, start=False, stop=False)
    return pe.matmul(out, l_lo, r_hi, start=False, stop=stop)


def known(v, value):
    return isinstance(v, int) and v == value


def flat(ap):
    n = len(ap.shape) - 1
    names = "abcd"[:n]
    return ap.rearrange(f"p {' '.join(names)} -> p ({' '.join(names)})") if n > 1 else ap


def pick(ap, i):
    one = ap[:, i:i + 1] if isinstance(i, int) else ap[:, bass.ds(i, 1)]
    return one.rearrange("p o n -> p (o n)")


def layer0_attention(nc, t_in, ident, tg, x1_dram):
    with ExitStack() as ctx:
        def sb(name, shape, dt=F32):
            return ctx.enter_context(nc.sbuf_tensor("a_" + name, shape, dt))

        def sem(name):
            return ctx.enter_context(nc.semaphore("a_" + name))

        w_stage = sb("w_stage", [P, 2, 2, DC, DH0])
        wqk = [sb("wqk_hi", [P, 2, 2, DC, DH0], F32R), sb("wqk_lo", [P, 2, 2, DC, DH0], F32R)]
        wv = [sb("wv_hi", [P, DC, INNER], F32R), sb("wv_lo", [P, DC, INNER], F32R)]
        wo = [sb("wo_hi", [P, H0, D], F32R), sb("wo_lo", [P, H0, D], F32R)]
        cols = sb("cols", [P, 4, DC])
        bias = sb("bias", [P, H0, 3])
        qk_bias = sb("qk_bias", [P, 2, 2])
        v_bias = sb("v_bias", [P, 1])
        tbo = sb("tbo", [P, D])
        x_in = sb("x_in", [P, 2 * TB, D])
        y = sb("y", [P, 2 * TB, D])
        stats = sb("stats", [P, 2 * TB, 6])
        mv = sb("mv", [P, 2 * TB, 2])
        var = sb("var", [P, 2 * TB])
        rstd = sb("rstd", [P, 2 * TB])
        vtmp = sb("vtmp", [P, TB])
        consts = sb("consts", [P, 4])
        x_acc = sb("x_acc", [P, TB, D])
        kvT = [sb("kvT_hi", [P, DC, KV0], F32R), sb("kvT_lo", [P, DC, KV0], F32R)]
        qT = [sb("qT_hi", [P, 2, S], F32R), sb("qT_lo", [P, 2, S], F32R)]
        kT = [sb("kT_hi", [P, 2, KV0], F32R), sb("kT_lo", [P, 2, KV0], F32R)]
        v = [sb("v_hi", [P, KT0, 2 * DH0], F32R), sb("v_lo", [P, KT0, 2 * DH0], F32R)]
        neg_max = sb("neg_max", [P, TB])
        row_sum = sb("row_sum", [P, 2, TB])
        inv_sum = sb("inv_sum", [P, 2, TB])
        prob = sb("prob", [P, TB, KV0])
        pT = [sb("pT_hi", [P, KT0, S], F32R), sb("pT_lo", [P, KT0, S], F32R)]
        inv_row = sb("inv_row", [P, S])
        o_norm = sb("o_norm", [P, S])
        oT = [sb("oT_hi", [P, 2, S], F32R), sb("oT_lo", [P, 2, S], F32R)]

        pj = ctx.enter_context(nc.psum_tensor("a_pj", [P, 2, BANK], F32))
        ps_s = ctx.enter_context(nc.psum_tensor("a_scores", [P, 2, KV0], F32))
        ps_t = ctx.enter_context(nc.psum_tensor("a_probT", [P, 2, BANK], F32))

        loaded = sem("loaded")
        w_load = [sem("w_load_A"), sem("w_load_B")]
        w_split = sem("w_split")
        big_hi = sem("big_hi")
        big_lo = sem("big_lo")
        w_step = sem("w_step")
        consts_set = sem("consts_set")
        tanh_done = sem("tanh_done")
        bias_scaled = sem("bias_scaled")
        qk_bias_set = sem("qk_bias_set")
        v_bias_set = sem("v_bias_set")
        x_load = sem("x_load")
        stats_ready = sem("stats_ready")
        rstd_ready = sem("rstd_ready")
        y_ready = sem("y_ready")
        ln_step = sem("ln_step")
        pj_full = sem("pj_full")
        pj_out = sem("pj_out")
        hi_done = sem("hi_done")
        s_full = sem("s_full")
        max_done = sem("max_done")
        exp_done = sem("exp_done")
        inv_done = sem("inv_done")
        t_full = sem("t_full")
        t_hi = sem("t_hi")
        t_out = sem("t_out")
        inv_row_done = sem("inv_row_done")
        affine_done = sem("affine_done")
        bn_done = sem("bn_done")
        aggr_done = sem("aggr_done")
        o_hi = sem("o_hi")
        o_lo = sem("o_lo")
        acc_init = sem("acc_init")
        stored = sem("stored")

        (x_d, ctx_d, g_x, g_f, gm, bm, gl, bl, wq_d, bq_d, wkv_d, bkv_d, wo_d, bo_d) = t_in
        xv = x_d.rearrange("b (t p) d -> p b t d", p=P)
        cv = ctx_d.rearrange("b (t p) d -> p b t d", p=P)
        x1v = x1_dram.rearrange("b (t p) d -> p b t d", p=P)
        wq_v = wq_d.rearrange("(c p) (h d) -> p h c d", p=P, d=DH0)
        wk_v = wkv_d[:, 0:INNER].rearrange("(c p) (h d) -> p h c d", p=P, d=DH0)
        wv_v = wkv_d[:, INNER:].rearrange("(c p) n -> p c n", p=P)
        wo_v = wo_d.rearrange("(h p) n -> p h n", p=DH0)
        N_CONST = 12

        def pj_start(b, hp):
            return 7 if known(b, 0) and known(hp, 0) else 3 + 68 * b + 16 * hp

        def hi_start(b, hp):
            return 7 + 44 * b + 10 * hp

        def at(v4, i):
            return v4[:, bass.ds(i, 1)].rearrange("p o t d -> p (o t) d")

        FIN = ("fin", 0)

        def plan(b, hp, par):
            def some(kind, *js):
                return [(kind, j) for j in js]

            if par == 0:
                return [some("qk", 0, 1), [] if known(b, 0) and known(hp, 0) else [FIN], some("qk", 2) + some("v", 0, 1), some("v", 2, 3)]
            out = [] if known(b, 0) and known(hp, 0) else some("out", 0, 1)
            if not known(hp, 3):
                return [out, [FIN], some("qk", 0, 1), some("qk", 2)]
            if known(b, B - 1):
                return [out, [FIN], [], []]
            return [out + some("pro", 0, 1), [FIN], some("pro", 2, 3), some("qk", 0, 1, 2)]

        SCORES = ((0,), (1, 2), (3,), ())

        def width(use):
            return 2 if use == FIN else 1

        def highs(use):
            return use[0] in ("qk", "v", "pro")

        def qk_dst(part, j, par):
            if j == 0:
                return qT[part][:, par]
            return kT[part][:, par, (j - 1) * S:j * S]

        block = ctx.enter_context(nc.Block())

        def batches(eng, pair):
            def batch(b):
                pair(b, 0)
                with eng.Fori(1, 3) as hp:
                    pair(b, hp)
                pair(b, 3)
            batch(0)
            with eng.Fori(1, B - 1) as b:
                batch(b)
            batch(B - 1)

        @block.sync
        def _(sp):
            dma = nc.sync.dma_start
            with nc.allow_non_contiguous_dma(reason="columns of biases, once"):
                for i, a in enumerate((gm, bm, gl, bl)):
                    dma(cols[:, i, :], a.rearrange("(c p) -> p c", p=P)).then_inc(loaded, 16)
                dma(bias[:, :, 0], bq_d.rearrange("(h p) -> p h", p=P)).then_inc(loaded, 16)
                dma(bias[:, :, 1], bkv_d[0:INNER].rearrange("(h p) -> p h", p=P)).then_inc(loaded, 16)
                dma(bias[:, :, 2], bkv_d[INNER:].rearrange("(h p) -> p h", p=P)).then_inc(loaded, 16)
            dma(tbo[:], bo_d.rearrange("(o d) -> o d", o=1).to_broadcast([P, D])).then_inc(loaded, 16)
            dma(tg[:, 0:2], g_x.rearrange("(o d) -> o d", o=1).to_broadcast([P, 2])).then_inc(loaded, 16)
            dma(tg[:, 2:4], g_f.rearrange("(o d) -> o d", o=1).to_broadcast([P, 2])).then_inc(loaded, 16)
            dma(prob[:, 0:2, :], wv_v).then_inc(loaded, 16)
            dma(prob[:, 2:4, :].rearrange("p a (h n) -> p (a h) n", n=D), wo_v).then_inc(loaded, 16)

            def load_tokens(b):
                dma(x_in[:, 0:TB, :], at(cv, b)).then_inc(x_load, 16)
                dma(x_in[:, TB:, :], at(xv, b)).then_inc(x_load, 16)

            def load_w(n, h, par):
                dma(w_stage[:, par, 0], at(wq_v, h)).then_inc(w_load[par], 16)
                dma(w_stage[:, par, 1], at(wk_v, h)).then_inc(w_load[par], 16)

            load_tokens(0)
            load_w(0, 0, 0)
            load_w(1, 1, 1)
            sp.wait_ge(w_split, 1)
            load_w(2, 2, 0)
            sp.wait_ge(w_split, 2)
            load_w(3, 3, 1)

            def batch(b):
                if not known(b, 0):
                    sp.wait_ge(pj_out, pj_start(b, 0) + 11)
                    dma(at(x1v, b - 1), x_acc[:]).then_inc(stored, 16)
                last = known(b, B - 1)
                if not last:
                    sp.wait_ge(acc_init, b + 1)
                    load_tokens(b + 1)
                for hp in range(2 if last else 4):
                    n, h = 8 * b + 2 * hp, (2 * hp + 4) % H0
                    sp.wait_ge(w_split, n + 3)
                    load_w(n + 4, h, 0)
                    sp.wait_ge(w_split, n + 4)
                    load_w(n + 5, h + 1, 1)
            batch(0)
            with sp.Fori(1, B - 1) as b:
                batch(b)
            batch(B - 1)
            sp.wait_ge(pj_out, pj_start(B - 1, 3) + 17)
            dma(x1v[:, B - 1], x_acc[:]).then_inc(stored, 16)
            sp.wait_ge(stored, 16 * B)

        @block.gpsimd
        def _(pool):
            g = nc.gpsimd
            for i, value in enumerate((-0.5, EPS, DH0 ** -0.5, 0.0)):
                g.memset(consts[:, i:i + 1], value).then_inc(consts_set, 1)

            def const(i, shape):
                return consts[:, i:i + 1].to_broadcast(shape)

            def split_w(n, par, after):
                pool.wait_ge(w_load[par], after)
                if not (isinstance(n, int) and n < 2):
                    pool.wait_ge(s_full, 4 * (n - 2) + 1)
                q, every, hi = flat(w_stage[:, par, 0]), flat(w_stage[:, par]), flat(wqk[0][:, par])
                g.tensor_tensor(q, q, const(2, [P, DC * DH0]), ALU.mult).then_inc(w_step, 1)
                pool.wait_ge(w_step, 2 * n + 1)
                g.tensor_tensor(hi, every, const(3, [P, 2 * DC * DH0]), ALU.add).then_inc(w_step, 1)
                pool.wait_ge(w_step, 2 * n + 2)
                g.tensor_tensor(flat(wqk[1][:, par]), every, hi.bitcast(F32), ALU.subtract).then_inc(w_split, 1)

            def inverse_std(b):
                lat = rstd[:, TB:]
                pool.wait_ge(stats_ready, 2 * b + 2)
                g.tensor_tensor(rstd[:], var[:], const(0, [P, 2 * TB]), ALU.pow).then_inc(ln_step, 1)
                pool.wait_ge(ln_step, 5 * b + 1)
                g.tensor_tensor(vtmp[:], lat, lat, ALU.mult).then_inc(ln_step, 1)
                pool.wait_ge(ln_step, 5 * b + 2)
                g.tensor_tensor(vtmp[:], vtmp[:], flat(mv[:, TB:, 1:2]), ALU.mult).then_inc(ln_step, 1)
                pool.wait_ge(ln_step, 5 * b + 3)
                g.tensor_tensor(vtmp[:], vtmp[:], const(1, [P, TB]), ALU.add).then_inc(ln_step, 1)
                pool.wait_ge(ln_step, 5 * b + 4)
                g.tensor_tensor(vtmp[:], vtmp[:], const(0, [P, TB]), ALU.pow).then_inc(ln_step, 1)
                pool.wait_ge(ln_step, 5 * b + 5)
                g.tensor_tensor(lat, lat, vtmp[:], ALU.mult).then_inc(rstd_ready, 1)

            pool.wait_ge(consts_set, 4)
            inverse_std(0)
            split_w(0, 0, 32)
            split_w(1, 1, 32)

            def pair(b, hp):
                n = 8 * b + 2 * hp
                i3 = known(hp, 3)
                if known(b, B - 1) and i3:
                    return
                if i3:
                    inverse_std(b + 1)
                turn = 4 * b + hp
                split_w(n + 2, 0, 32 * turn + 64)
                split_w(n + 3, 1, 32 * turn + 64)
            batches(pool, pair)

        @block.scalar
        def _(act):
            a = nc.scalar.activation
            act.wait_ge(loaded, 16 * N_CONST)
            a(tg[:], tg[:], ACT.Tanh).then_inc(tanh_done, 1)
            a(flat(wv[0][:]), flat(prob[:, 0:2, :]), ACT.Copy).then_inc(big_hi, 1)
            a(flat(wo[0][:]), flat(prob[:, 2:4, :]), ACT.Copy).then_inc(big_hi, 1)

            def use_bank(use, u, bank, n, par):
                kind, j = use
                src = pj[:, bank, :]
                if kind == "out":
                    return
                if kind == "qk" and j == 0:
                    act.wait_ge(qk_bias_set, n + 2)
                act.wait_ge(pj_full, u + 1)
                if kind == "qk":
                    i = min(j, 1)
                    a(qk_dst(0, j, 1 - par), src, ACT.Identity, bias=qk_bias[:, 1 - par, i:i + 1]).then_inc(hi_done, 1)
                elif kind == "v":
                    a(flat(v[0][:, 2 * j:2 * j + 2, :]), src, ACT.Copy).then_inc(hi_done, 1)
                elif kind == "pro":
                    c, half = j % 2, j // 2
                    a(kvT[0][:, c, half * S:(half + 1) * S], src, ACT.Identity,
                      bias=cols[:, 2 * half + 1, c:c + 1], scale=cols[:, 2 * half, c:c + 1]).then_inc(hi_done, 1)
                else:
                    a(inv_row[:], src, ACT.Copy).then_inc(inv_row_done, 1)

            def prob_high(n, qt):
                for half in range(2):
                    act.wait_ge(t_full, 8 * n + 2 * qt + half + 1)
                    a(pT[0][:, 4 * half:4 * half + 4, qt * P:(qt + 1) * P],
                      ps_t[:, half, :].rearrange("p (k q) -> p k q", k=4), ACT.Copy).then_inc(t_hi, 1)

            def exp(n, qt, par):
                act.wait_ge(max_done, 4 * n + qt + 1)
                if not known(n, 0):
                    act.wait_ge(t_full, 8 * n + 2 * qt - 6)
                a(prob[:, qt, :], ps_s[:, qt % 2, :], ACT.Exp, bias=neg_max[:, qt:qt + 1],
                  accum_out=row_sum[:, par, qt:qt + 1]).then_inc(exp_done, 1)

            def finish_o(n, par, u):
                act.wait_ge(pj_out, u)
                act.wait_ge(v_bias_set, n + 1)
                a(oT[0][:, par, :], o_norm[:], ACT.Identity, bias=v_bias[:]).then_inc(o_hi, 1)

            for j in range(4):
                use_bank(("pro", j), j, j % 2, 0, 0)
            for j in range(3):
                use_bank(("qk", j), 4 + j, j % 2, -1, 1)

            def step(b, hp, par, u, bank):
                n = 8 * b + 2 * hp + par
                first = known(n, 0)
                for q, todo in enumerate(plan(b, hp, par)):
                    if q == 2 and not first:
                        finish_o(n - 1, 1 - par, u)
                    for i, qt in enumerate(SCORES[q]):
                        if i and not first:
                            use_bank(FIN, u, bank, n, par)
                        exp(n, qt, par)
                    for use in todo:
                        if use != FIN:
                            use_bank(use, u, bank, n, par)
                        u, bank = u + width(use), (bank + width(use)) % 2
                    if q:
                        prob_high(n, q - 1)
                    elif not first:
                        prob_high(n - 1, 3)
                return u, bank

            def pair(b, hp):
                u, bank = step(b, hp, 0, pj_start(b, hp), 1)
                step(b, hp, 1, u, bank)

            batches(act, pair)
            n, u = 8 * B - 1, pj_start(B - 1, 3) + 13
            prob_high(n, 3)
            use_bank(FIN, u, u % 2, n, 1)
            finish_o(n, 1, u + 2)

        @block.vector
        def _(dve):
            ve = nc.vector

            def lo(out, ps, hi_ap, bias_ap=None):
                if bias_ap is None:
                    return ve.tensor_tensor(out, ps, hi_ap.bitcast(F32), ALU.subtract)
                return ve.scalar_tensor_tensor(out, ps, bias_ap, hi_ap.bitcast(F32), ALU.add, ALU.subtract)

            def use_bank(use, u, k, bank, n, par, b):
                kind, j = use
                src = pj[:, bank, :]
                if highs(use):
                    dve.wait_ge(hi_done, k + 1)
                elif kind == "out":
                    dve.wait_ge(pj_full, u + 1)
                if kind == "qk":
                    i = min(j, 1)
                    lo(qk_dst(1, j, 1 - par), src, qk_dst(0, j, 1 - par), qk_bias[:, 1 - par, i:i + 1]).then_inc(pj_out, 1)
                elif kind == "v":
                    lo(flat(v[1][:, 2 * j:2 * j + 2, :]), src, flat(v[0][:, 2 * j:2 * j + 2, :])).then_inc(pj_out, 1)
                elif kind == "pro":
                    c, half = j % 2, j // 2
                    ve.tensor_scalar(src, src, cols[:, 2 * half, c:c + 1],
                                     cols[:, 2 * half + 1, c:c + 1], ALU.mult, ALU.add).then_inc(affine_done, 1)
                    dve.wait_ge(affine_done, 4 * b + j + 1)
                    span = slice(half * S, (half + 1) * S)
                    lo(kvT[1][:, c, span], src, kvT[0][:, c, span]).then_inc(pj_out, 1)
                elif kind == "out":
                    if j == 0:
                        dve.wait_ge(pj_out, u)
                        dve.wait_ge(acc_init, b)
                    part = flat(x_acc[:, 2 * j:2 * j + 2, :])
                    ve.scalar_tensor_tensor(part, src, tg[:, 0:1], part, ALU.mult, ALU.add).then_inc(pj_out, 1)
                else:
                    dve.wait_ge(inv_row_done, n)
                    dve.wait_ge(pj_full, u + 2)
                    ve.tensor_tensor(o_norm[:], pj[:, 1 - bank, :], inv_row[:], ALU.mult).then_inc(pj_out, 2)

            def set_qk_bias(h, par):
                ve.tensor_copy(qk_bias[:, par, :], pick(bias[:], h)[:, 0:2]).then_inc(qk_bias_set, 1)

            def set_v_bias(h):
                ve.tensor_copy(v_bias[:], pick(bias[:], h)[:, 2:3]).then_inc(v_bias_set, 1)

            def prob_low(n, qt):
                for half in range(2):
                    dve.wait_ge(t_hi, 8 * n + 2 * qt + half + 1)
                    dst = pT[1][:, 4 * half:4 * half + 4, qt * P:(qt + 1) * P]
                    src = pT[0][:, 4 * half:4 * half + 4, qt * P:(qt + 1) * P]
                    lo(dst, ps_t[:, half, :].rearrange("p (k q) -> p k q", k=4), src).then_inc(t_out, 1)

            def row_max(n, qt):
                dve.wait_ge(s_full, 4 * n + qt + 1)
                ve.tensor_reduce(neg_max[:, qt:qt + 1], ps_s[:, qt % 2, :], AX.X, ALU.max, negate=True).then_inc(max_done, 1)

            def invert_sums(n, par):
                dve.wait_ge(exp_done, 4 * n + 4)
                ve.reciprocal(inv_sum[:, par, :], row_sum[:, par, :]).then_inc(inv_done, 1)

            def o_low(n, par):
                dve.wait_ge(o_hi, n + 1)
                lo(oT[1][:, par, :], o_norm[:], oT[0][:, par, :], v_bias[:]).then_inc(o_lo, 1)

            def statistics(b):
                dve.wait_ge(x_load, 32 * b + 32)
                T = 2 * TB
                for t in range(T):
                    if t:
                        dve.wait_ge(bn_done, T * b + t)
                    ve.bn_stats(stats[:, t, :], x_in[:, t, :]).then_inc(bn_done, 1)
                    if t:
                        ve.bn_aggr(mv[:, t - 1, :], stats[:, t - 1, :]).then_inc(aggr_done, 1)
                dve.wait_ge(bn_done, T * b + T)
                dve.wait_ge(aggr_done, T * b + T - 1)
                ve.tensor_scalar(var[:, 0:T - 1], flat(mv[:, 0:T - 1, 1:2]), EPS, None, ALU.add).then_inc(stats_ready, 1)
                ve.bn_aggr(mv[:, T - 1, :], stats[:, T - 1, :]).then_inc(aggr_done, 1)
                dve.wait_ge(aggr_done, T * b + T)
                ve.tensor_scalar(var[:, T - 1:], flat(mv[:, T - 1:, 1:2]), EPS, None, ALU.add).then_inc(stats_ready, 1)

            def normalise(b):
                dve.wait_ge(rstd_ready, b + 1)
                for t in range(2 * TB):
                    last = ve.tensor_scalar(y[:, t, :], x_in[:, t, :], mv[:, t, 0:1], rstd[:, t:t + 1], ALU.subtract, ALU.mult)
                    last.then_inc(y_ready, 1)

            def init_acc(b):
                if not known(b, 0):
                    dve.wait_ge(stored, 16 * b)
                ve.tensor_tensor(x_acc[:], x_in[:, TB:, :], tbo[:].rearrange("p (o d) -> p o d", o=1).to_broadcast([P, TB, D]), ALU.add).then_inc(acc_init, 1)

            statistics(0)
            for i, (w, rows) in enumerate(((wv, slice(0, 2)), (wo, slice(2, 4)))):
                dve.wait_ge(big_hi, i + 1)
                ve.tensor_tensor(flat(w[1][:]), flat(prob[:, rows, :]), flat(w[0][:]).bitcast(F32), ALU.subtract).then_inc(big_lo, 1)
            dve.wait_ge(tanh_done, 1)
            ve.tensor_scalar(tbo[:], tbo[:], tg[:, 0:1], None, ALU.mult).then_inc(bias_scaled, 1)
            ve.tensor_scalar(bias[:, :, 0:1], bias[:, :, 0:1], DH0 ** -0.5, None, ALU.mult).then_inc(bias_scaled, 1)
            normalise(0)
            dve.wait_ge(bias_scaled, 2)
            set_qk_bias(0, 0)
            for j in range(4):
                use_bank(("pro", j), j, j, j % 2, 0, 0, 0)
            for j in range(3):
                use_bank(("qk", j), 4 + j, 4 + j, j % 2, -1, 1, 0)

            def step(b, hp, par, u, k, bank):
                n = 8 * b + 2 * hp + par
                first = known(n, 0)
                pair3 = known(hp, 3)
                last = known(b, B - 1) and pair3
                if par == 0 or not last:
                    set_qk_bias(2 * hp + 1 if par == 0 else (0 if pair3 else 2 * hp + 2), 1 - par)
                if not first:
                    if not known(n, 1):
                        dve.wait_ge(o_lo, n - 1)
                    set_v_bias((H0 - 1 if known(hp, 0) else 2 * hp - 1) if par == 0 else 2 * hp)
                    invert_sums(n - 1, 1 - par)
                for q, todo in enumerate(plan(b, hp, par)):
                    for qt in SCORES[q]:
                        row_max(n, qt)
                    if q == 2 and not first:
                        o_low(n - 1, 1 - par)
                    for use in todo:
                        use_bank(use, u, k, bank, n, par, b if known(hp, 0) and use[0] == "out" else b + 1)
                        u, k, bank = u + width(use), k + highs(use), (bank + width(use)) % 2
                    if q:
                        prob_low(n, q - 1)
                    elif not first:
                        prob_low(n - 1, 3)
                    if par == 0 and pair3 and not last:
                        if q == 1:
                            statistics(b + 1)
                        elif q == 3:
                            normalise(b + 1)
                if par == 1 and known(hp, 0):
                    init_acc(b)
                return u, k, bank

            def pair(b, hp):
                u, k, bank = step(b, hp, 0, pj_start(b, hp), hi_start(b, hp), 1)
                step(b, hp, 1, u, k, bank)

            batches(dve, pair)
            n, u = 8 * B - 1, pj_start(B - 1, 3) + 13
            dve.wait_ge(o_lo, n)
            set_v_bias(H0 - 1)
            invert_sums(n, 1)
            prob_low(n, 3)
            use_bank(FIN, u, 0, u % 2, n + 1, 0, 0)
            o_low(n, 1)
            for j in range(2):
                use_bank(("out", j), u + 2 + j, 0, (u + j) % 2, n, 1, B)

        @block.tensor
        def _(pe):
            t = nc.tensor

            def free_bank(u):
                if not (isinstance(u, int) and u < 2):
                    pe.wait_ge(pj_out, u - 1)

            def finish(n, par, u, bank, between=None):
                pe.wait_ge(inv_done, n + 1)
                for qt in range(TB):
                    last = t.matmul(pj[:, bank, qt * P:(qt + 1) * P], inv_sum[:, par, qt:qt + 1].to_broadcast([P, P]),
                                    ident[:], is_transpose=True)
                last.then_inc(pj_full, 1)
                free_bank(u + 1)
                pe.wait_ge(t_out, 8 * n + 8)
                for kt in range(KT0):
                    if kt == KT0 // 2 and between:
                        between()
                    d = slice(par * DH0, (par + 1) * DH0)
                    last = mm3(t, pj[:, 1 - bank, :], v[0][:, kt, d], v[1][:, kt, d], pT[0][:, kt, :], pT[1][:, kt, :],
                               kt == 0, kt == KT0 - 1)
                last.then_inc(pj_full, 1)

            def use_bank(use, u, bank, n, par, b, hp, between=None):
                kind, j = use
                dst = pj[:, bank, :]
                if kind == "qk" and j == 0:
                    pe.wait_ge(w_split, n + 2)
                elif kind == "out" and j == 0:
                    pe.wait_ge(o_lo, n - 1)
                elif kind == "pro" and j == 0:
                    pe.wait_ge(y_ready, 8 * b + 8)
                free_bank(u)
                if kind == "qk":
                    span = (slice(S, KV0), slice(0, S), slice(S, KV0))[j]
                    for c in range(DC):
                        last = mm3(t, dst, wqk[0][:, 1 - par, min(j, 1), c], wqk[1][:, 1 - par, min(j, 1), c],
                                   kvT[0][:, c, span], kvT[1][:, c, span], c == 0, c == DC - 1)
                elif kind == "v":
                    for kt in (2 * j, 2 * j + 1):
                        for c in range(DC):
                            two = slice(hp * 256, hp * 256 + 256) if isinstance(hp, int) else bass.ds(hp * 256, 256)
                            last = mm3(t, dst[:, (kt % 2) * 256:(kt % 2) * 256 + 256],
                                       kvT[0][:, c, kt * P:(kt + 1) * P], kvT[1][:, c, kt * P:(kt + 1) * P],
                                       wv[0][:, c, two], wv[1][:, c, two], c == 0, c == DC - 1)
                elif kind == "pro":
                    c, half = j % 2, j // 2
                    for tt in range(TB):
                        last = t.transpose(dst[:, tt * P:(tt + 1) * P], y[:, half * TB + tt, c * P:(c + 1) * P], ident[:])
                elif kind == "out":
                    for tt in (2 * j, 2 * j + 1):
                        for head in range(2):
                            h = 2 * (hp - 1) + head if not known(hp, 0) else H0 - 2 + head
                            q = slice(tt * P, (tt + 1) * P)
                            last = mm3(t, dst[:, (tt % 2) * D:(tt % 2) * D + D], oT[0][:, head, q], oT[1][:, head, q],
                                       pick(wo[0][:], h), pick(wo[1][:], h), head == 0, head == 1)
                else:
                    return finish(n - 1, 1 - par, u, bank, between)
                last.then_inc(pj_full, 1)

            def scores(n, qt, par):
                if not (isinstance(n, int) and 4 * n + qt < 2):
                    pe.wait_ge(exp_done, 4 * n + qt - 1)
                for half in range(2):
                    span = slice(half * S, (half + 1) * S)
                    q = slice(qt * P, (qt + 1) * P)
                    last = mm3(t, ps_s[:, qt % 2, span], qT[0][:, par, q], qT[1][:, par, q], kT[0][:, par, span], kT[1][:, par, span], True, True)
                last.then_inc(s_full, 1)

            def turn(n, qt):
                pe.wait_ge(exp_done, 4 * n + qt + 1)
                for half in range(2):
                    m = 8 * n + 2 * qt + half
                    if not (isinstance(m, int) and m < 2):
                        pe.wait_ge(t_out, m - 1)
                    for k in range(4):
                        kt = 4 * half + k
                        last = t.transpose(ps_t[:, half, k * P:(k + 1) * P], prob[:, qt, kt * P:(kt + 1) * P], ident[:])
                    last.then_inc(t_full, 1)

            for j in range(4):
                use_bank(("pro", j), j, j % 2, 0, 0, 0, 0)
            pe.wait_ge(pj_out, 4)
            for j in range(3):
                use_bank(("qk", j), 4 + j, j % 2, -1, 1, 0, 0)

            def step(b, hp, par, u, bank):
                n = 8 * b + 2 * hp + par
                first = known(n, 0)
                pe.wait_ge(pj_out, u - 4 * par)
                for q, todo in enumerate(plan(b, hp, par)):
                    for qt in SCORES[q][:1 if todo == [FIN] else 2]:
                        scores(n, qt, par)
                    if q == 3 and ("qk", 0) in todo:
                        pe.wait_ge(pj_out, u)
                    for use in todo:
                        use_bank(use, u, bank, n, par, b + 1, hp, lambda: scores(n, 2, par))
                        u, bank = u + width(use), (bank + width(use)) % 2
                    if q:
                        turn(n, q - 1)
                    elif not first:
                        turn(n - 1, 3)
                return u, bank

            def pair(b, hp):
                u, bank = step(b, hp, 0, pj_start(b, hp), 1)
                step(b, hp, 1, u, bank)

            pe.wait_ge(big_lo, 2)
            batches(pe, pair)
            n, u = 8 * B - 1, pj_start(B - 1, 3) + 13
            turn(n, 3)
            free_bank(u)
            finish(n, 1, u, u % 2)
            pe.wait_ge(o_lo, n + 1)
            for j in range(2):
                use_bank(("out", j), u + 2 + j, (u + j) % 2, n, 1, B, 4)


E0, F0 = 16, 1024
C0 = (B * S + E0 - 1) // E0
FT0 = F0 // P
CT0 = C0 // P
FAR = 1 << 20


def statistics(dve, ve, x, stats, mv, var, tiles, done, bn_done, aggr_done, stats_ready):
    T = tiles
    for t in range(T):
        if t:
            dve.wait_ge(bn_done, T * done + t)
        ve.bn_stats(stats[:, t, :], x[:, t, :]).then_inc(bn_done, 1)
        if t:
            ve.bn_aggr(mv[:, t - 1, :], stats[:, t - 1, :]).then_inc(aggr_done, 1)
    dve.wait_ge(bn_done, T * done + T)
    dve.wait_ge(aggr_done, T * done + T - 1)
    ve.tensor_scalar(var[:, 0:T - 1], flat(mv[:, 0:T - 1, 1:2]), EPS, None, ALU.add).then_inc(stats_ready, 1)
    ve.bn_aggr(mv[:, T - 1, :], stats[:, T - 1, :]).then_inc(aggr_done, 1)
    dve.wait_ge(aggr_done, T * done + T)
    ve.tensor_scalar(var[:, T - 1:T], flat(mv[:, T - 1:T, 1:2]), EPS, None, ALU.add).then_inc(stats_ready, 1)


def each_batch(eng, batch):
    batch(0)
    with eng.Fori(1, B) as b:
        batch(b)


def pick4(view, b):
    return view[:, bass.ds(b, 1)].rearrange("p o t d -> p (o t) d")


def pick_cols(table, b, n):
    return table[:, n * b:n * b + n] if isinstance(b, int) else table[:, bass.ds(n * b, n)]


def last_axis(ap, n):
    return ap.rearrange("p (a o) -> p a o", o=1).to_broadcast([ap.shape[0], ap.shape[1], n])


def mid_axis(ap, n):
    return ap.rearrange("p (o a) -> p o a", o=1).to_broadcast([ap.shape[0], n, ap.shape[1]])


def layer0_route(nc, x1_dram, wg_d, d_in, K, tg, route_row, route_w):
    with ExitStack() as ctx:
        def sb(name, shape, dt=F32):
            return ctx.enter_context(nc.sbuf_tensor("r_" + name, shape, dt))

        def sem(name):
            return ctx.enter_context(nc.semaphore("r_" + name))

        wg = sb("wg", [P, DC, E0])
        x = sb("x", [P, TB, D])
        y = sb("y", [P, TB, D])
        yT = sb("yT", [P, DC, S])
        stats, mv = sb("stats", [P, TB, 6]), sb("mv", [P, TB, 2])
        var, rstd = sb("var", [P, TB]), sb("rstd", [P, TB])
        neg_max, total, gate = sb("neg_max", [P, TB]), sb("total", [P, TB]), sb("gate", [P, TB])
        rel = sb("rel", [P, TB, E0])
        ex = sb("ex", [P, TB, E0])
        first = sb("first", [P, TB, E0])
        best = sb("best", [P, TB])
        chosen = sb("chosen", [P, TB, E0])
        place = sb("place", [P, TB, E0])
        carry = sb("carry", [P, E0])
        loc, valid, row, tmp = (sb(n, [P, TB]) for n in ("loc", "valid", "row", "tmp"))
        row_i = sb("row_i", [P, TB], I32)
        ps_t = ctx.enter_context(nc.psum_tensor("r_T", [P, 2, BANK], F32))
        ps_l = ctx.enter_context(nc.psum_tensor("r_logits", [P, BANK], F32))
        ps_c = ctx.enter_context(nc.psum_tensor("r_counts", [P, BANK], F32))
        ps_n = ctx.enter_context(nc.psum_tensor("r_counted", [P, BANK], F32))

        wg_load, x_load = sem("wg_load"), sem("x_load")
        bn_done, aggr_done, stats_ready, rstd_ready = sem("bn"), sem("aggr"), sem("stats_ready"), sem("rstd")
        y_ready, t_full, t_out, l_full = sem("y_ready"), sem("t_full"), sem("t_out"), sem("l_full")
        rel_ready, exp_done, chosen_ready, counted = sem("rel"), sem("exp"), sem("chosen"), sem("counted")
        carry_set, row_ready, scattered, step = sem("carry"), sem("row_ready"), sem("scattered"), sem("step")
        turn, weight_set = sem("turn"), sem("weight_set")
        STEPS = 15
        xv = x1_dram.rearrange("b (t p) d -> p b t d", p=P)
        block = ctx.enter_context(nc.Block())

        @block.sync
        def _(sp):
            nc.sync.dma_start(wg[:], wg_d.rearrange("(c p) e -> p c e", p=P)).then_inc(wg_load, 16)
            nc.sync.dma_start(x[:], xv[:, 0]).then_inc(x_load, 16)
            with sp.Fori(1, B) as b:
                sp.wait_ge(y_ready, TB * b)
                nc.sync.dma_start(x[:], pick4(xv, b)).then_inc(x_load, 16)

        @block.gpsimd
        def _(pool):
            def batch(b):
                pool.wait_ge(stats_ready, 2 * b + 2)
                nc.gpsimd.tensor_tensor(rstd[:], var[:], K.neg_half[:].to_broadcast([P, TB]), ALU.pow).then_inc(rstd_ready, 1)
                for t in range(TB):
                    if t == 0:
                        pool.wait_ge(row_ready, b + 1)
                        nc.gpsimd.tensor_tensor(K.pool_scratch[:], K.neg_half[:], K.neg_half[:], ALU.mult).then_inc(turn, 1)
                    nc.gpsimd.indirect_dma_start(d_in, bass.IndirectOffsetOnAxis(ap=row_i[:, t:t + 1], axis=0), y[:, t, :], None,
                                                 bounds_check=E0 * C0 - 1, oob_is_err=False).then_inc(scattered, 16)
            each_batch(pool, batch)
            pool.wait_ge(scattered, 16 * TB * B)

        @block.scalar
        def _(act):
            def batch(b):
                for c in range(DC):
                    act.wait_ge(t_full, DC * b + c + 1)
                    nc.scalar.activation(yT[:, c, :], ps_t[:, c, :], ACT.Copy).then_inc(t_out, 1)
                act.wait_ge(rel_ready, b + 1)
                nc.scalar.activation(flat(ex[:]), flat(rel[:]), ACT.Exp).then_inc(exp_done, 1)
            each_batch(act, batch)

        @block.tensor
        def _(pe):
            t_ = nc.tensor
            pe.wait_ge(wg_load, 16)
            def batch(b):
                pe.wait_ge(y_ready, TB * b + TB)
                for c in range(DC):
                    for t in range(TB):
                        last = t_.transpose(ps_t[:, c, t * P:(t + 1) * P], y[:, t, c * P:(c + 1) * P], K.ident[:])
                    last.then_inc(t_full, 1)
                pe.wait_ge(t_out, DC * b + DC)
                for t in range(TB):
                    for c in range(DC):
                        last = t_.matmul(ps_l[:, t * E0:(t + 1) * E0], yT[:, c, t * P:(t + 1) * P], wg[:, c, :],
                                         start=c == 0, stop=c == DC - 1)
                last.then_inc(l_full, 1)
                pe.wait_ge(chosen_ready, b + 1)
                for t in range(TB):
                    for u in range(t + 1):
                        t_.matmul(ps_c[:, t * E0:(t + 1) * E0], K.before[:] if u == t else K.ones[:], chosen[:, u, :],
                                  start=u == 0, stop=u == t)
                for t in range(TB):
                    last = t_.matmul(ps_n[:, 0:E0], K.ones[:], chosen[:, t, :], start=t == 0, stop=t == TB - 1)
                last.then_inc(counted, 1)
            each_batch(pe, batch)

        @block.vector
        def _(dve):
            ve = nc.vector
            ve.memset(carry[:], 0.0).then_inc(carry_set, 1)
            logits = ps_l[:, 0:TB * E0].rearrange("p (t e) -> p t e", e=E0)
            counts = ps_c[:, 0:TB * E0].rearrange("p (t e) -> p t e", e=E0)
            def batch(b):
                k = [0]

                def then(instruction):
                    k[0] += 1
                    instruction.then_inc(step, 1)
                    dve.wait_ge(step, STEPS * b + k[0])

                dve.wait_ge(x_load, 16 * b + 16)
                statistics(dve, ve, x, stats, mv, var, TB, b, bn_done, aggr_done, stats_ready)
                dve.wait_ge(rstd_ready, b + 1)
                if not known(b, 0):
                    dve.wait_ge(scattered, 16 * TB * b)
                for t in range(TB):
                    ve.tensor_scalar(y[:, t, :], x[:, t, :], mv[:, t, 0:1], rstd[:, t:t + 1], ALU.subtract, ALU.mult).then_inc(y_ready, 1)
                dve.wait_ge(l_full, b + 1)
                then(ve.tensor_reduce(neg_max[:], logits, AX.X, ALU.max, negate=True))
                ve.tensor_tensor(rel[:], logits, last_axis(neg_max[:], E0), ALU.add).then_inc(rel_ready, 1)
                dve.wait_ge(rel_ready, b + 1)
                then(ve.tensor_scalar(first[:], rel[:], 0.0, float(-FAR), ALU.is_equal, ALU.mult))
                then(ve.tensor_tensor(first[:], first[:], mid_axis(K.iota[:, 0:E0], TB), ALU.add))
                then(ve.tensor_reduce(best[:], first[:], AX.X, ALU.min))
                then(ve.tensor_scalar(best[:], best[:], float(FAR), None, ALU.add))
                ve.tensor_tensor(chosen[:], mid_axis(K.iota[:, 0:E0], TB), last_axis(best[:], E0), ALU.is_equal).then_inc(chosen_ready, 1)
                dve.wait_ge(exp_done, b + 1)
                then(ve.tensor_reduce(total[:], ex[:], AX.X, ALU.add))
                then(ve.reciprocal(gate[:], total[:]))
                dve.wait_ge(counted, b + 1)
                then(ve.tensor_tensor(place[:], counts, mid_axis(carry[:], TB), ALU.add))
                then(ve.tensor_tensor(place[:], place[:], chosen[:], ALU.mult))
                ve.tensor_tensor(carry[:], ps_n[:, 0:E0], carry[:], ALU.add).then_inc(carry_set, 1)
                then(ve.tensor_reduce(loc[:], place[:], AX.X, ALU.add))
                then(ve.tensor_scalar(valid[:], loc[:], float(C0), None, ALU.is_lt))
                then(ve.scalar_tensor_tensor(row[:], best[:], float(C0), loc[:], ALU.mult, ALU.add))
                then(ve.tensor_scalar(tmp[:], valid[:], float(-FAR), float(FAR), ALU.mult, ALU.add))
                ve.tensor_tensor(row_i[:], row[:], tmp[:], ALU.add).then_inc(row_ready, 1)
                then(ve.tensor_scalar(loc[:], loc[:], float(C0 - 1), None, ALU.min))
                ve.scalar_tensor_tensor(pick_cols(route_row, b, TB), best[:], float(C0), loc[:], ALU.mult, ALU.add).then_inc(step, 1)
                ve.scalar_tensor_tensor(pick_cols(route_w, b, TB), gate[:], tg[:, 2:3], valid[:], ALU.mult, ALU.mult).then_inc(weight_set, 1)
            each_batch(dve, batch)


def e_at(view, e):
    return view[:, e] if isinstance(e, int) else pick4(view, e)


def early(e, n):
    return isinstance(e, int) and e < n


def layer0_experts(nc, d_in, w1_d, w2_d, d_out, K):
    with ExitStack() as ctx:
        def sb(name, shape, dt=F32):
            return ctx.enter_context(nc.sbuf_tensor("e_" + name, shape, dt))

        def sem(name):
            return ctx.enter_context(nc.semaphore("e_" + name))

        def psum(name, banks):
            return ctx.enter_context(nc.psum_tensor("e_" + name, [P, banks, BANK], F32))

        HB = FT0 // 2
        w1_in, w2_in = sb("w1_in", [P, 2, DC, F0]), sb("w2_in", [P, 2, FT0, D])
        w1 = [sb("w1_hi", [P, 2, DC, F0], F32R), sb("w1_lo", [P, 2, DC, F0], F32R)]
        w2 = [sb("w2_hi", [P, 2, FT0, D], F32R), sb("w2_lo", [P, 2, FT0, D], F32R)]
        rows = sb("rows", [P, 2, CT0, D])
        rT = [sb("rT_hi", [P, 2, DC, C0], F32R), sb("rT_lo", [P, 2, DC, C0], F32R)]
        hT = [sb("hT_hi", [P, 2, FT0, C0], F32R), sb("hT_lo", [P, 2, FT0, C0], F32R)]
        res = sb("res", [P, 2, CT0, D])
        ps_h, ps_t, ps_o = psum("h", HB), psum("t", 1), psum("o", 1)

        w1_load, w2_load, row_load, stored = ([sem(f"{n}{p}") for p in range(2)] for n in ("w1_load", "w2_load", "row_load", "stored"))
        w1_hi, w1_lo, w2_hi, w2_lo = sem("w1_hi"), sem("w1_lo"), sem("w2_hi"), sem("w2_lo")
        t_full, t_hi, t_out = sem("t_full"), sem("t_hi"), sem("t_out")
        h_full, h_hi, h_out = sem("h_full"), sem("h_hi"), sem("h_out")
        o_full, o_out = sem("o_full"), sem("o_out")

        w1_v = w1_d.rearrange("e (c p) f -> p e c f", p=P)
        w2_v = w2_d.rearrange("e (k p) m -> p e k m", p=P)
        in_v = d_in.rearrange("(e t p) d -> p e t d", p=P, t=CT0)
        out_v = d_out.rearrange("(e t p) d -> p e t d", p=P, t=CT0)

        def steps(eng, step):
            step(0, 0, 0)
            step(1, 0, 1)
            with eng.Fori(1, E0 // 2 - 1) as i:
                step(2 * i, i, 0)
                step(2 * i + 1, i, 1)
            step(E0 - 2, E0 // 2 - 1, 0)
            step(E0 - 1, E0 // 2 - 1, 1)

        block = ctx.enter_context(nc.Block())

        @block.sync
        def _(sp):
            def step(e, i, par):
                if not early(e, 2):
                    sp.wait_ge(t_full, e - 1)
                nc.sync.dma_start(rows[:, par], e_at(in_v, e)).then_inc(row_load[par], 16)
                if not early(e, 2):
                    sp.wait_ge(w1_lo, e - 1)
                nc.sync.dma_start(w1_in[:, par], e_at(w1_v, e)).then_inc(w1_load[par], 16)
                if not early(e, 2):
                    sp.wait_ge(w2_lo, e - 1)
                nc.sync.dma_start(w2_in[:, par], e_at(w2_v, e)).then_inc(w2_load[par], 16)
            steps(sp, step)

        @block.gpsimd
        def _(pool):
            def store(e, par):
                pool.wait_ge(o_out, e + 1)
                nc.gpsimd.dma_start(e_at(out_v, e), res[:, par]).then_inc(stored[par], 16)

            def step(e, i, par):
                pool.wait_ge(w1_hi, e + 1)
                nc.gpsimd.tensor_tensor(flat(w1[1][:, par]), flat(w1_in[:, par]), flat(w1[0][:, par]).bitcast(F32), ALU.subtract).then_inc(w1_lo, 1)
                if not early(e, 2):
                    store(e - 2, par)
            steps(pool, step)
            store(E0 - 2, 0)
            store(E0 - 1, 1)
            pool.wait_ge(stored[0], 8 * E0)
            pool.wait_ge(stored[1], 8 * E0)

        @block.scalar
        def _(act):
            a = nc.scalar.activation

            def split_w1(e, i, par):
                act.wait_ge(w1_load[par], 16 * i + 16)
                if not early(e, 2):
                    act.wait_ge(h_full, HB * e - HB)
                a(flat(w1[0][:, par]), flat(w1_in[:, par]), ACT.Copy).then_inc(w1_hi, 1)

            def split_w2(e, i, par):
                act.wait_ge(w2_load[par], 16 * i + 16)
                if not early(e, 2):
                    act.wait_ge(o_full, e - 1)
                a(flat(w2[0][:, par]), flat(w2_in[:, par]), ACT.Copy).then_inc(w2_hi, 1)

            def rows_hi(e, par):
                act.wait_ge(t_full, e + 1)
                a(flat(rT[0][:, par]), ps_t[:, 0, :], ACT.Copy).then_inc(t_hi, 1)

            def step(e, i, par):
                if not early(e, 2):
                    act.wait_ge(o_full, e - 1)
                for j in range(HB):
                    act.wait_ge(h_full, HB * e + j + 1)
                    a(flat(hT[0][:, par, 2 * j:2 * j + 2]), ps_h[:, j, :], ACT.Relu).then_inc(h_hi, 1)
                if not known(e, E0 - 1):
                    rows_hi(e + 1, 1 - par)
                    split_w1(e + 1, i + par, 1 - par)
                split_w2(e, i, par)

            split_w1(0, 0, 0)
            rows_hi(0, 0)
            steps(act, step)

        @block.vector
        def _(dve):
            ve = nc.vector

            def rows_lo(e, par):
                dve.wait_ge(t_hi, e + 1)
                ve.tensor_tensor(flat(rT[1][:, par]), ps_t[:, 0, :], flat(rT[0][:, par]).bitcast(F32), ALU.subtract).then_inc(t_out, 1)

            def result(e, i, par):
                dve.wait_ge(o_full, e + 1)
                if not early(e, 2):
                    dve.wait_ge(stored[par], 16 * i)
                ve.tensor_copy(flat(res[:, par]), ps_o[:, 0, :]).then_inc(o_out, 1)

            def step(e, i, par):
                for j in range(HB):
                    dve.wait_ge(h_hi, HB * e + j + 1)
                    part = slice(2 * j, 2 * j + 2)
                    ve.scalar_tensor_tensor(flat(hT[1][:, par, part]), ps_h[:, j, :], 0.0, flat(hT[0][:, par, part]).bitcast(F32),
                                            ALU.max, ALU.subtract).then_inc(h_out, 1)
                if not known(e, E0 - 1):
                    rows_lo(e + 1, 1 - par)
                dve.wait_ge(w2_hi, e + 1)
                ve.tensor_tensor(flat(w2[1][:, par]), flat(w2_in[:, par]), flat(w2[0][:, par]).bitcast(F32), ALU.subtract).then_inc(w2_lo, 1)
                if not known(e, 0):
                    result(e - 1, i if par else i - 1, 1 - par)

            rows_lo(0, 0)
            steps(dve, step)
            result(E0 - 1, E0 // 2 - 1, 1)

        @block.tensor
        def _(pe):
            t_ = nc.tensor

            def turn_rows(e, i, par):
                pe.wait_ge(row_load[par], 16 * i + 16)
                if not known(e, 0):
                    pe.wait_ge(t_out, e)
                for c in range(DC):
                    for t in range(CT0):
                        last = t_.transpose(ps_t[:, 0, c * C0 + t * P:c * C0 + (t + 1) * P], rows[:, par, t, c * P:(c + 1) * P], K.ident[:])
                last.then_inc(t_full, 1)

            def first_product(e, par):
                pe.wait_ge(t_out, e + 1)
                pe.wait_ge(w1_lo, e + 1)
                for j in range(HB):
                    if not known(e, 0):
                        pe.wait_ge(h_out, HB * (e - 1) + j + 1)
                    for f in (2 * j, 2 * j + 1):
                        for c in range(DC):
                            fs = slice(f * P, (f + 1) * P)
                            last = mm3(t_, ps_h[:, j, (f % 2) * C0:(f % 2 + 1) * C0], w1[0][:, par, c, fs], w1[1][:, par, c, fs],
                                       rT[0][:, par, c], rT[1][:, par, c], c == 0, c == DC - 1)
                    last.then_inc(h_full, 1)

            def second_product(e, par):
                pe.wait_ge(h_out, HB * e + HB)
                pe.wait_ge(w2_lo, e + 1)
                if not known(e, 0):
                    pe.wait_ge(o_out, e)
                for t in range(CT0):
                    rs = slice(t * P, (t + 1) * P)
                    for f in range(FT0):
                        last = mm3(t_, ps_o[:, 0, t * D:(t + 1) * D], hT[0][:, par, f, rs], hT[1][:, par, f, rs],
                                   w2[0][:, par, f], w2[1][:, par, f], f == 0, f == FT0 - 1)
                last.then_inc(o_full, 1)

            def step(e, i, par):
                first_product(e, par)
                if not known(e, E0 - 1):
                    turn_rows(e + 1, i + par, 1 - par)
                if not known(e, 0):
                    second_product(e - 1, 1 - par)

            turn_rows(0, 0, 0)
            steps(pe, step)
            second_product(E0 - 1, 1)


H1, DH1 = 16, 16
G1 = H1 // 4
PAIRS = H1 // 2
KT1 = S // P
VPAD = H1 * P + P
AHEAD = 5


def layer1_attention(nc, x1_dram, ctx_d, wqT_d, wkT_d, wvT_d, woT_d, route_row, route_w, d_out, tg, x3_dram, K):
    with ExitStack() as ctx:
        def sb(name, shape, dt=F32):
            return ctx.enter_context(nc.sbuf_tensor("c_" + name, shape, dt))

        def sem(name):
            return ctx.enter_context(nc.semaphore("c_" + name))

        prob = sb("prob", [P, KT1, S])
        w_in = prob[:, 0:3, :].rearrange("p a (c n) -> p a c n", c=DC)
        w_qkv = [sb("w_hi", [P, 3, DC, D], F32R), sb("w_lo", [P, 3, DC, D], F32R)]
        w_o = [sb("wo_hi", [P, G1, D], F32R), sb("wo_lo", [P, G1, D], F32R)]
        x_in, x_acc = sb("x_in", [P, TB, D]), sb("x_acc", [P, TB, D])
        y = sb("y", [P, TB, D])
        c_in = sb("c_in", [P, TB, D])
        v_tok = c_in[:].rearrange("p t (h d) -> p t h d", h=H1)
        row_now, w_now = sb("row_now", [P, TB], I32), sb("w_now", [P, TB])
        stats, mv = sb("stats", [P, TB, 6]), sb("mv", [P, TB, 2])
        var, rstd = sb("var", [P, TB]), sb("rstd", [P, TB])
        tT = [sb("tT_hi", [P, DC, S], F32R), sb("tT_lo", [P, DC, S], F32R)]
        q_tok = sb("q_tok", [P, TB, H1, 4, DH1], F32R)
        k_tok = sb("k_tok", [P, TB, H1, 4, DH1], F32R)
        q_rows = sb("q_rows", [P, PAIRS, S], F32R)
        k_rows = sb("k_rows", [P, PAIRS, S], F32R)
        v_cols = sb("v_cols", [P, KT1, VPAD], F32R)
        neg_max = sb("neg_max", [P, 2, TB, 4])
        max_parts = sb("max_parts", [P, TB, 2, 4], F32R)
        max_rows = sb("max_rows", [40, S], F32R)
        select = sb("select", [40, 4, P], F32R)
        one_cols = sb("one_cols", [P, 7 * 32], F32R)
        pT = [sb("pT_hi", [P, 2, KT1, S], F32R), sb("pT_lo", [P, 2, KT1, S], F32R)]
        o_norm = sb("o_norm", [P, S])
        oT = [sb("oT_hi", [P, G1, S], F32R), sb("oT_lo", [P, G1, S], F32R)]

        ps_m = ctx.enter_context(nc.psum_tensor("c_max", [P, 2, BANK], F32))
        ps_s = ctx.enter_context(nc.psum_tensor("c_scores", [P, 2, BANK], F32))
        ps_v = ctx.enter_context(nc.psum_tensor("c_values", [P, 2, BANK], F32))
        ps_z = ctx.enter_context(nc.psum_tensor("c_sums", [P, BANK], F32))
        pj = ctx.enter_context(nc.psum_tensor("c_pj", [P, BANK], F32))

        w_load, w_hi, w_lo, wo_load, wo_hi, wo_lo = (sem(n) for n in ("w_load", "w_hi", "w_lo", "wo_load", "wo_hi", "wo_lo"))
        cleared, tables = sem("cleared"), sem("tables")
        x_load, c_load, rows_set, fetch_done, x2_done = (sem(n) for n in ("x_load", "c_load", "rows_set", "fetch_done", "x2_done"))
        bn_done, aggr_done, stats_ready, rstd_ready, y_ready = (sem(n) for n in ("bn", "aggr", "stats", "rstd", "y"))
        pj_full = sem("pj_full")
        pj_hi = sem("pj_hi")
        pj_out = sem("pj_out")
        pj_out_act = sem("pj_out_act")
        v_hi, v_lo = sem("v_hi"), sem("v_lo")
        m_full, max_done, parts_hi, parts_lo = sem("m_full"), sem("max_done"), sem("parts_hi"), sem("parts_lo")
        s_full, exp_done, p_hi, p_lo = sem("s_full"), sem("exp_done"), sem("p_hi"), sem("p_lo")
        values_done, sums_out, inv_done, o_norm_done, o_hi, o_lo = (
            sem(n) for n in ("values_done", "sums_out", "inv_done", "o_norm_done", "o_hi", "o_lo"))
        acc_set, stored, w_scaled = sem("acc_set"), sem("stored"), sem("w_scaled")

        xv = x1_dram.rearrange("b (t p) d -> p b t d", p=P)
        cv = ctx_d.rearrange("b (t p) d -> p b t d", p=P)
        x3v = x3_dram.rearrange("b (t p) d -> p b t d", p=P)

        PLAN = {3: [("ctx", 0), ("ctx", 1)], 4: [("k", 0), ("k", 1)], 5: [("v", 0), ("v", 1)],
                6: [("y", 0), ("y", 1)], 7: [("q", 0), ("q", 1)]}
        PLAN.update({8 + p: [("q_rows", p), ("k_rows", p)] for p in range(PAIRS)})
        PREPARE = [use for h in sorted(PLAN) for use in PLAN[h]]
        HIGHS = [use for use in PREPARE if use[0] in ("ctx", "k", "y", "q")]
        BY_ACT = ("v", "q_rows", "k_rows")
        ACT_USES = sum(use[0] in BY_ACT for use in PREPARE)
        V_STEP = {10: 0, 11: 1, 14: 2}

        def uses(b, h):
            found = [("max", (h // 4 + 1) % 2)] if h % 4 == 3 and not (known(b, B - 1) and h == H1 - 1) else []
            if h == 2 and not known(b, 0):
                found += [("out", 0), ("out", 1)]
            return found + ([] if known(b, B - 1) else PLAN.get(h, []))

        ALL = len(PREPARE) + G1 + 2

        def pj_start(b):
            return len(PREPARE) + 1 if known(b, 0) else ALL * b + len(PREPARE) + 1 - 2

        def dve_start(b):
            return len(PREPARE) + 1 - ACT_USES if known(b, 0) else (ALL - ACT_USES) * b + len(PREPARE) + 1 - 2 - ACT_USES

        def halves(todo):
            first = 0 if todo and todo[0][0] == "out" else 1
            return todo[:first], todo[first:first + 1], todo[first + 1:]

        def whole(b):
            return [use for h in range(H1) for use in uses(b, h)]

        def out_of_bank(eng, b, i):
            seq = PREPARE if b is None else whole(b)
            by_act = sum(use[0] in BY_ACT for use in seq[:i + 1])
            if seq[i][0] in BY_ACT if i >= 0 else not known(b, 0):
                eng.wait_ge(pj_out_act, by_act if b is None else ACT_USES * b + (ACT_USES + by_act))
            else:
                eng.wait_ge(pj_out, i + 1 - by_act if b is None else dve_start(b) + (i + 1 - by_act))

        V_USE = max(i for i, use in enumerate(PREPARE) if use[0] == "v")

        def hi_index(use, b):
            return len(HIGHS) * b + HIGHS.index(use)

        def b_at(view, b):
            return view[:, b] if isinstance(b, int) else pick4(view, b)

        def run(eng, batch):
            batch(0)
            with eng.Fori(1, B - 1) as b:
                batch(b)
            batch(B - 1)

        def diagonal(g, part):
            wide = v_cols[:, :, g * 4 * P:g * 4 * P + 4 * (P + 2 * DH1)].rearrange("p k (j c) -> p k j c", j=4)
            return wide[:, :, :, part * DH1:(part + 1) * DH1]

        block = ctx.enter_context(nc.Block())

        Q_HIGH, Q_LOW = slice(0, 4, 2), slice(1, 4, 2)
        K_HIGH, K_LOW = slice(0, 2), slice(2, 4)

        def twice(two_tiles, t):
            return two_tiles[:, t * D:(t + 1) * D].rearrange("p (h o d) -> p h o d", h=H1, o=1).to_broadcast([P, H1, 2, DH1])

        @block.sync
        def _(sp):
            dma = nc.sync.dma_start
            for i, w in enumerate((wqT_d, wkT_d, wvT_d)):
                dma(w_in[:, i], w.rearrange("(c p) n -> p c n", p=P)).then_inc(w_load, 16)
            dma(x_in[:], xv[:, 0]).then_inc(x_load, 16)
            dma(c_in[:], cv[:, 0]).then_inc(c_load, 16)
            sp.wait_ge(w_lo, 1)
            wo_v = woT_d.rearrange("(g j d) n -> j d g n", g=G1, j=4)
            stage = w_in.rearrange("p a c n -> p (a c) n")
            for j in range(4):
                for part in range(2):
                    dma(stage[32 * j + 16 * part:32 * j + 16 * part + 16, 0:G1, :], wo_v[j]).then_inc(wo_load, 16)

            def batch(b):
                if not known(b, B - 1):
                    sp.wait_ge(v_lo, G1 * b + G1)
                    dma(c_in[:], b_at(cv, b + 1)).then_inc(c_load, 16)
                if not known(b, 0):
                    out_of_bank(sp, b, 1)
                    dma(b_at(x3v, b - 1), x_acc[:]).then_inc(stored, 16)
                if not known(b, B - 1):
                    sp.wait_ge(acc_set, b + 1)
                    dma(x_in[:], b_at(xv, b + 1)).then_inc(x_load, 16)
            run(sp, batch)
            sp.wait_ge(pj_out, dve_start(B - 1) + len(whole(B - 1)) + 2)
            dma(x3v[:, B - 1], x_acc[:]).then_inc(stored, 16)
            sp.wait_ge(stored, 16 * B)

        @block.gpsimd
        def _(pool):
            g = nc.gpsimd
            g.memset(v_cols[:].bitcast(F32), 0.0).then_inc(cleared, 1)

            def fetch(b):
                for t in range(TB):
                    if t == 0:
                        pool.wait_ge(rows_set, 2 * b + 2)
                        g.tensor_tensor(K.pool_scratch[:], K.neg_half[:], K.neg_half[:], ALU.mult).then_inc(cleared, 1)
                    g.indirect_dma_start(y[:, t, :], None, d_out, bass.IndirectOffsetOnAxis(ap=row_now[:, t:t + 1], axis=0)).then_inc(fetch_done, 16)
                pool.wait_ge(stats_ready, 2 * b + 2)
                g.tensor_tensor(rstd[:], var[:], K.neg_half[:].to_broadcast([P, TB]), ALU.pow).then_inc(rstd_ready, 1)
            each_batch(pool, fetch)

        @block.scalar
        def _(act):
            a = nc.scalar.activation

            def side(use, u, b):
                kind, i = use
                if kind in ("out", "max"):
                    return
                act.wait_ge(pj_full, u + 1)
                if kind in ("ctx", "y"):
                    a(tT[0][:, i, :], pj[:], ACT.Copy).then_inc(pj_hi, 1)
                elif kind in ("q", "k"):
                    dst, where = (q_tok, Q_HIGH) if kind == "q" else (k_tok, K_HIGH)
                    a(dst[:, 2 * i, :, where, :], twice(pj, 0), ACT.Copy)
                    a(dst[:, 2 * i + 1, :, where, :], twice(pj, 1), ACT.Copy).then_inc(pj_hi, 1)
                elif kind == "v":
                    a(flat(v_tok[:, 2 * i:2 * i + 2]), pj[:], ACT.Copy).then_inc(pj_out_act, 1)
                else:
                    dst = q_rows if kind == "q_rows" else k_rows
                    a(dst[:, i, :], pj[:], ACT.Copy).then_inc(pj_out_act, 1)

            def spread_v(m, g):
                act.wait_ge(cleared, 1)
                a(diagonal(g, 0), v_tok[:, :, 4 * g:4 * g + 4, :], ACT.Copy).then_inc(v_hi, 1)

            def exp(n, kt):
                act.wait_ge(s_full, 4 * n + kt + 1)
                if not known(n, 0) and kt % 2 == 0:
                    act.wait_ge(p_lo, 2 * n - 1 + kt // 2)
                a(prob[:, kt, :], ps_s[:, kt % 2, :], ACT.Exp).then_inc(exp_done, 1)

            def prob_high(n, par, half):
                if not (isinstance(n, int) and n < 2) and half == 0:
                    act.wait_ge(values_done, n - 1)
                act.wait_ge(exp_done, 4 * n + 2 * half + 2)
                two = slice(2 * half, 2 * half + 2)
                a(flat(pT[0][:, par, two]), flat(prob[:, two]), ACT.Copy).then_inc(p_hi, 1)

            def group_sums(m):
                act.wait_ge(values_done, 4 * m + 4)
                if not known(m, 0):
                    act.wait_ge(o_lo, m)
                a(o_norm[:], ps_z[:], ACT.Copy).then_inc(sums_out, 1)

            def group_high(m, g):
                act.wait_ge(o_norm_done, m + 1)
                a(oT[0][:, g, :], o_norm[:], ACT.Copy).then_inc(o_hi, 1)

            act.wait_ge(w_scaled, 1)
            a(flat(w_qkv[0][:]), flat(w_in), ACT.Copy).then_inc(w_hi, 1)
            act.wait_ge(wo_load, 16 * 8)
            stage = w_in.rearrange("p a c n -> p (a c) n")
            a(flat(w_o[0][:]), flat(stage[:, 0:G1, :]), ACT.Copy).then_inc(wo_hi, 1)
            for u, use in enumerate(PREPARE):
                side(use, u, 0)
            out_of_bank(act, None, V_USE)
            for g in range(3):
                spread_v(g, g)

            def batch(b):
                last = known(b, B - 1)
                u = pj_start(b)

                def sides(some):
                    nonlocal u
                    for use in some:
                        side(use, u, b + 1)
                        u += 1

                for h in range(H1):
                    n, par = H1 * b + h, h % 2
                    early_uses, late_uses, end_uses = halves(uses(b, h))
                    m, g = G1 * b + h // 4 - 1, (h // 4 - 1) % G1
                    if h % 4 == 1 and not (known(b, 0) and h == 1):
                        group_sums(m)
                    exp(n, 0)
                    exp(n, 1)
                    if h % 4 == 2 and not (known(b, 0) and h == 2):
                        group_high(m, g)
                    sides(early_uses)
                    prob_high(n, par, 0)
                    exp(n, 2)
                    exp(n, 3)
                    sides(late_uses)
                    prob_high(n, par, 1)
                    if h == 1:
                        spread_v(G1 * b + 3, 3)
                    if h in V_STEP and not last:
                        spread_v(G1 * b + 4 + V_STEP[h], V_STEP[h])
                    sides(end_uses)
            run(act, batch)
            group_sums(G1 * B - 1)
            group_high(G1 * B - 1, 3)

        @block.vector
        def _(dve):
            ve = nc.vector

            def lo(out, ps, hi):
                return ve.tensor_tensor(out, ps, hi.bitcast(F32), ALU.subtract)

            def side(use, u, b):
                kind, i = use
                if kind in BY_ACT:
                    return
                if kind in ("ctx", "y", "q", "k"):
                    dve.wait_ge(pj_hi, hi_index(use, b) + 1)
                else:
                    dve.wait_ge(pj_full, u + 1)
                if kind in ("ctx", "y"):
                    last = lo(tT[1][:, i, :], pj[:], tT[0][:, i, :])
                elif kind in ("q", "k"):
                    dst, high, low = (q_tok, Q_HIGH, Q_LOW) if kind == "q" else (k_tok, K_HIGH, K_LOW)
                    for t in range(2):
                        last = lo(dst[:, 2 * i + t, :, low, :], twice(pj, t), dst[:, 2 * i + t, :, high, :])
                elif kind == "max":
                    last = ve.tensor_copy(max_rows[32 * i:32 * i + 8, :], pj[0:8, :])
                else:
                    part = flat(x_acc[:, 2 * i:2 * i + 2, :])
                    last = ve.scalar_tensor_tensor(part, pj[:], tg[:, 1:2], part, ALU.mult, ALU.add)
                last.then_inc(pj_out, 1)

            def set_rows(b):
                ve.tensor_copy(row_now[:], pick_cols(route_row, b, TB)).then_inc(rows_set, 1)
                ve.tensor_copy(w_now[:], pick_cols(route_w, b, TB)).then_inc(rows_set, 1)

            def add_experts(b):
                dve.wait_ge(x_load, 16 * b + 16)
                dve.wait_ge(fetch_done, 16 * TB * (b + 1))
                for t in range(TB):
                    ve.scalar_tensor_tensor(x_in[:, t, :], y[:, t, :], w_now[:, t:t + 1], x_in[:, t, :], ALU.mult, ALU.add).then_inc(x2_done, 1)
                dve.wait_ge(x2_done, TB * b + TB)
                statistics(dve, ve, x_in, stats, mv, var, TB, b, bn_done, aggr_done, stats_ready)

            def normalise(b):
                dve.wait_ge(rstd_ready, b + 1)
                for t in range(TB):
                    ve.tensor_scalar(y[:, t, :], x_in[:, t, :], mv[:, t, 0:1], rstd[:, t:t + 1], ALU.subtract, ALU.mult).then_inc(y_ready, 1)

            def spread_v(m, g):
                dve.wait_ge(v_hi, m + 1)
                lo(diagonal(g, 1), v_tok[:, :, 4 * g:4 * g + 4, :], diagonal(g, 0)).then_inc(v_lo, 1)

            def maximum(n, h, qt):
                dve.wait_ge(m_full, 4 * n + qt + 1)
                ve.tensor_reduce(neg_max[:, h // 4 % 2, qt, h % 4:h % 4 + 1], ps_m[:, qt % 2, :], AX.X, ALU.max, negate=True).then_inc(max_done, 1)

            def split_maxima(m, slot):
                dve.wait_ge(max_done, 16 * m + 16)
                ve.tensor_copy(max_parts[:, :, 0, :], neg_max[:, slot]).then_inc(parts_hi, 1)
                dve.wait_ge(parts_hi, m + 1)
                lo(max_parts[:, :, 1, :], neg_max[:, slot], max_parts[:, :, 0, :]).then_inc(parts_lo, 1)

            def prob_low(n, par, half):
                dve.wait_ge(p_hi, 2 * n + half + 1)
                two = slice(2 * half, 2 * half + 2)
                lo(flat(pT[1][:, par, two]), flat(prob[:, two]), flat(pT[0][:, par, two])).then_inc(p_lo, 1)

            def invert_sums(m, quarter):
                if quarter == 0:
                    dve.wait_ge(sums_out, m + 1)
                q = slice(quarter * P, (quarter + 1) * P)
                ve.reciprocal(o_norm[:, q], o_norm[:, q]).then_inc(inv_done, 1)

            def group_norm(m, g):
                dve.wait_ge(inv_done, 4 * m + 4)
                ve.tensor_tensor(o_norm[:], ps_v[:, g % 2], o_norm[:], ALU.mult).then_inc(o_norm_done, 1)

            def group_low(m, g):
                dve.wait_ge(o_hi, m + 1)
                lo(oT[1][:, g, :], o_norm[:], oT[0][:, g, :]).then_inc(o_lo, 1)

            def keep_x2(b):
                if not known(b, 0):
                    dve.wait_ge(stored, 16 * b)
                ve.tensor_copy(x_acc[:], x_in[:]).then_inc(acc_set, 1)

            for at in (0, 32):
                rows = slice(at, at + 8)
                ve.tensor_tensor(select[rows], last_axis(K.ident[rows, at:at + 4], P), last_axis(K.ident[rows, at + 4:at + 8], P), ALU.add).then_inc(tables, 1)
            ve.memset(one_cols[:, 0:96].bitcast(F32), 0.0).then_inc(tables, 1)
            ve.memset(one_cols[:, 96:128].bitcast(F32), 1.0).then_inc(tables, 1)
            ve.memset(one_cols[:, 128:].bitcast(F32), 0.0).then_inc(tables, 1)
            dve.wait_ge(w_load, 48)
            ve.tensor_scalar(flat(w_in[:, 1]), flat(w_in[:, 1]), DH1 ** -0.5, None, ALU.mult).then_inc(w_scaled, 1)
            dve.wait_ge(w_hi, 1)
            lo(flat(w_qkv[1][:]), flat(w_in), flat(w_qkv[0][:])).then_inc(w_lo, 1)
            set_rows(0)
            add_experts(0)
            normalise(0)
            dve.wait_ge(wo_hi, 1)
            stage = w_in.rearrange("p a c n -> p (a c) n")
            lo(flat(w_o[1][:]), flat(stage[:, 0:G1, :]), flat(w_o[0][:])).then_inc(wo_lo, 1)
            for u, use in enumerate(PREPARE):
                side(use, u, 0)
            for g in range(3):
                spread_v(g, g)
            for n in range(AHEAD):
                for qt in range(TB):
                    maximum(n, n, qt)
                if n == 3:
                    split_maxima(0, 0)
            side(("max", 0), len(PREPARE), 0)

            def batch(b):
                first, last = known(b, 0), known(b, B - 1)
                u = pj_start(b)

                def sides(some):
                    nonlocal u
                    for use in some:
                        side(use, u, b + 1)
                        u += 1

                for h in range(H1):
                    n, par = H1 * b + h, h % 2
                    ahead = not (last and h + AHEAD >= H1)
                    early_uses, late_uses, end_uses = halves(uses(b, h))
                    m, g = G1 * b + h // 4 - 1, (h // 4 - 1) % G1
                    invert = h % 4 == 1 and not (first and h == 1)
                    if h == 0 and not last:
                        set_rows(b + 1)
                    for half in range(2):
                        if ahead:
                            maximum(n + AHEAD, h + AHEAD, 2 * half)
                            maximum(n + AHEAD, h + AHEAD, 2 * half + 1)
                        if h == 2 and half == 0 and not first:
                            dve.wait_ge(acc_set, b)
                        if h % 4 == 2 and half == 0 and not (first and h == 2):
                            group_low(m, g)
                        if invert:
                            invert_sums(m, 2 * half)
                        sides(late_uses if half else early_uses)
                        prob_low(n, par, half)
                        if invert:
                            invert_sums(m, 2 * half + 1)
                    if invert:
                        group_norm(m, g)
                    if h == 1:
                        spread_v(G1 * b + 3, 3)
                    if h == 3:
                        keep_x2(b)
                    if not last:
                        if h in V_STEP:
                            spread_v(G1 * b + 4 + V_STEP[h], V_STEP[h])
                        if h == 4:
                            add_experts(b + 1)
                        elif h == 5:
                            normalise(b + 1)
                    if h % 4 == 2 and not (last and h == H1 - 2):
                        split_maxima(G1 * b + h // 4 + 1, (h // 4 + 1) % 2)
                    sides(end_uses)
                end[0] = u
            end = [0]
            run(dve, batch)
            for quarter in range(4):
                invert_sums(G1 * B - 1, quarter)
            group_norm(G1 * B - 1, 3)
            group_low(G1 * B - 1, 3)
            for half in range(2):
                side(("out", half), end[0] + half, B)

        @block.tensor
        def _(pe):
            t_ = nc.tensor

            def side(use, b):
                kind, i = use
                if kind in ("ctx", "y"):
                    src = c_in if kind == "ctx" else y
                    if i == 0:
                        if kind == "ctx":
                            pe.wait_ge(c_load, 16 * b + 16)
                        else:
                            pe.wait_ge(y_ready, TB * b + TB)
                    for t in range(TB):
                        last = t_.transpose(pj[:, t * P:(t + 1) * P], src[:, t, i * P:(i + 1) * P], K.ident[:])
                elif kind in ("q", "k", "v"):
                    w = "qkv".index(kind)
                    for t in range(2):
                        rows = slice((2 * i + t) * P, (2 * i + t + 1) * P)
                        for c in range(DC):
                            last = mm3(t_, pj[:, t * D:(t + 1) * D], tT[0][:, c, rows], tT[1][:, c, rows],
                                       w_qkv[0][:, w, c], w_qkv[1][:, w, c], c == 0, c == DC - 1)
                elif kind in ("q_rows", "k_rows"):
                    src = q_tok if kind == "q_rows" else k_tok
                    for t in range(TB):
                        last = t_.transpose(pj[:, t * P:(t + 1) * P].bitcast(F32R), flat(src[:, t, 2 * i:2 * i + 2]), K.ident_r[:])
                elif kind == "max":
                    for t in range(TB):
                        last = t_.transpose(pj[0:8, t * P:(t + 1) * P].bitcast(F32R), flat(max_parts[:, t]), K.ident_r[:])
                else:
                    for t in range(2):
                        q = slice((2 * i + t) * P, (2 * i + t + 1) * P)
                        for g in range(G1):
                            last = mm3(t_, pj[:, t * D:(t + 1) * D], oT[0][:, g, q], oT[1][:, g, q], w_o[0][:, g], w_o[1][:, g], g == 0, g == G1 - 1)
                last.then_inc(pj_full, 1)

            def head_rows(h):
                return slice(64 * (h % 2), 64 * (h % 2) + 64), h % H1 // 2

            def for_maximum(n, h, qt):
                if not (isinstance(n, int) and 4 * n + qt < 2):
                    pe.wait_ge(max_done, 4 * n + qt - 1)
                rows, p = head_rows(h)
                t_.matmul(ps_m[:, qt % 2, :], q_rows[rows, p, qt * P:(qt + 1) * P], k_rows[rows, p, :], start=True, stop=True).then_inc(m_full, 1)

            def scores(n, h, kt):
                if not (isinstance(n, int) and 4 * n + kt < 2):
                    pe.wait_ge(exp_done, 4 * n + kt - 1)
                rows, p = head_rows(h)
                slot = slice(32 * (h // 4 % 2), 32 * (h // 4 % 2) + 8)
                t_.matmul(ps_s[:, kt % 2, :], k_rows[rows, p, kt * P:(kt + 1) * P], q_rows[rows, p, :], start=True, stop=False)
                t_.matmul(ps_s[:, kt % 2, :], select[slot, h % 4, :], max_rows[slot, :], start=False, stop=True).then_inc(s_full, 1)

            def values(n, h, half):
                pe.wait_ge(p_lo, 2 * n + half + 1)
                for kt in (2 * half, 2 * half + 1):
                    for part in range(2):
                        ends = dict(start=h % 4 == 0 and kt == 0 and part == 0, stop=h % 4 == 3 and kt == KT1 - 1 and part == 1)
                        right = pT[part][:, h % 2, kt, :]
                        t_.matmul(ps_v[:, h // 4 % 2], v_cols[:, kt, h * P:(h + 1) * P], right, **ends)
                        last = t_.matmul(ps_z[:], one_cols[:, 96 - 32 * (h % 4):224 - 32 * (h % 4)], right, **ends)
                if half == 1:
                    last.then_inc(values_done, 1)

            def values_first(b, h, m):
                if h == 13:
                    pe.wait_ge(v_lo, G1 * b + 4)
                elif h == 1:
                    pe.wait_ge(v_lo, G1 * b + 3)
                if h % 4 == 1 and not known(m, 0):
                    pe.wait_ge(sums_out, m)
                    if not known(m, 1):
                        pe.wait_ge(o_norm_done, m - 1)

            pe.wait_ge(tables, 5)
            pe.wait_ge(w_lo, 1)
            for u, use in enumerate(PREPARE):
                if u:
                    out_of_bank(pe, None, u - 1)
                side(use, 0)
            pe.wait_ge(wo_lo, 1)
            out_of_bank(pe, None, len(PREPARE) - 1)
            for n in range(AHEAD):
                for qt in range(TB):
                    for_maximum(n, n, qt)
            pe.wait_ge(parts_lo, 1)
            side(("max", 0), 0)

            def batch(b):
                first, last = known(b, 0), known(b, B - 1)
                i = 0
                for h in range(H1):
                    n = H1 * b + h
                    ahead = not (last and h + AHEAD >= H1)
                    early_uses, late_uses, end_uses = halves(uses(b, h))
                    if h % 4 == 0:
                        out_of_bank(pe, b, i - 1)

                    def sides(some):
                        nonlocal i
                        for use in some:
                            out_of_bank(pe, b, i - 1)
                            if use[0] == "max":
                                pe.wait_ge(parts_lo, G1 * b + h // 4 + 2)
                            elif use == ("out", 0):
                                pe.wait_ge(o_lo, G1 * b)
                            side(use, b + 1)
                            i += 1

                    for half in range(2):
                        scores(n, h, 2 * half)
                        scores(n, h, 2 * half + 1)
                        if ahead:
                            for_maximum(n + AHEAD, h + AHEAD, 2 * half)
                            for_maximum(n + AHEAD, h + AHEAD, 2 * half + 1)
                        sides(late_uses if half else early_uses)
                        if not (first and h == 0):
                            if half == 0:
                                values_first(b, h, G1 * b + (h - 1) // 4)
                            values(n - 1, (h - 1) % H1, half)
                    sides(end_uses)
            run(pe, batch)
            n = H1 * B - 1
            values(n, H1 - 1, 0)
            values(n, H1 - 1, 1)
            pe.wait_ge(o_lo, G1 * B)
            for half in range(2):
                if half:
                    pe.wait_ge(pj_out, dve_start(B - 1) + len(whole(B - 1)) + 1)
                side(("out", half), B)


E1, F1 = 8, 512
EA = E1 + 1
FT1 = F1 // P


def layer1_gate(nc, x3_dram, wg_d, bias_d, K, tg, zT, weight):
    with ExitStack() as ctx:
        def sb(name, shape, dt=F32):
            return ctx.enter_context(nc.sbuf_tensor("g_" + name, shape, dt))

        def sem(name):
            return ctx.enter_context(nc.semaphore("g_" + name))

        wg = sb("wg", [P, DC, E1])
        gate_bias = sb("gate_bias", [P, E1])
        x = sb("x", [P, TB, D])
        y = sb("y", [P, TB, D])
        yT = sb("yT", [P, DC, S])
        stats, mv = sb("stats", [P, TB, 6]), sb("mv", [P, TB, 2])
        var, rstd = sb("var", [P, TB]), sb("rstd", [P, TB])
        neg_max, total, inverse, best = (sb(n, [P, TB]) for n in ("neg_max", "total", "inverse", "best"))
        rel, ex, scores, biased, first, one, two = (sb(n, [P, TB, E1]) for n in ("rel", "ex", "scores", "biased", "first", "one", "two"))
        ps_t = ctx.enter_context(nc.psum_tensor("g_T", [P, 2, DC, BANK], F32))
        ps_l = ctx.enter_context(nc.psum_tensor("g_logits", [P, BANK], F32))

        loaded, x_load = sem("loaded"), sem("x_load")
        bn_done, aggr_done, stats_ready, rstd_ready = sem("bn"), sem("aggr"), sem("stats_ready"), sem("rstd")
        y_ready, t_full, t_out, l_full = sem("y_ready"), sem("t_full"), sem("t_out"), sem("l_full")
        rel_ready, exp_done, z_hi, z_lo, step = sem("rel"), sem("exp"), sem("z_hi"), sem("z_lo"), sem("step")
        weight_set = sem("weight_set")
        STEPS = 21
        xv = x3_dram.rearrange("b (t p) d -> p b t d", p=P)
        block = ctx.enter_context(nc.Block())

        @block.sync
        def _(sp):
            nc.sync.dma_start(x[:], xv[:, 0]).then_inc(x_load, 16)
            nc.sync.dma_start(wg[:], wg_d.rearrange("(c p) e -> p c e", p=P)).then_inc(loaded, 16)
            nc.sync.dma_start(gate_bias[:], bias_d.rearrange("(o d) -> o d", o=1).to_broadcast([P, E1])).then_inc(loaded, 16)
            with sp.Fori(1, B) as b:
                sp.wait_ge(y_ready, TB * b)
                nc.sync.dma_start(x[:], pick4(xv, b)).then_inc(x_load, 16)

        @block.gpsimd
        def _(pool):
            def batch(b):
                pool.wait_ge(stats_ready, 2 * b + 2)
                nc.gpsimd.tensor_tensor(rstd[:], var[:], K.neg_half[:].to_broadcast([P, TB]), ALU.pow).then_inc(rstd_ready, 1)
            each_batch(pool, batch)

        @block.scalar
        def _(act):
            def batch(b):
                if not known(b, 0):
                    act.wait_ge(z_lo, b)
                for c in range(DC):
                    act.wait_ge(t_full, DC * b + c + 1)
                    nc.scalar.activation(yT[:, c, :], ps_t[:, 0, c, :], ACT.Copy).then_inc(t_out, 1)
                act.wait_ge(rel_ready, b + 1)
                nc.scalar.activation(flat(ex[:]), flat(rel[:]), ACT.Exp).then_inc(exp_done, 1)
            each_batch(act, batch)

        @block.tensor
        def _(pe):
            t_ = nc.tensor
            pe.wait_ge(loaded, 32)
            def batch(b):
                pe.wait_ge(y_ready, TB * b + TB)
                for c in range(DC):
                    for t in range(TB):
                        last = t_.transpose(ps_t[:, 0, c, t * P:(t + 1) * P], y[:, t, c * P:(c + 1) * P], K.ident[:])
                    last.then_inc(t_full, 1)
                pe.wait_ge(t_out, DC * b + DC)
                for t in range(TB):
                    for c in range(DC):
                        last = t_.matmul(ps_l[:, t * E1:(t + 1) * E1], yT[:, c, t * P:(t + 1) * P], wg[:, c, :],
                                         start=c == 0, stop=c == DC - 1)
                last.then_inc(l_full, 1)
            each_batch(pe, batch)

        @block.vector
        def _(dve):
            ve = nc.vector
            ve.tensor_copy(weight[:, E1, :], tg[:, 3:4].to_broadcast([P, NT])).then_inc(weight_set, 1)
            logits = ps_l[:, 0:TB * E1].rearrange("p (t e) -> p t e", e=E1)
            dve.wait_ge(loaded, 32)
            def batch(b):
                k = [0]

                def then(instruction):
                    k[0] += 1
                    instruction.then_inc(step, 1)
                    dve.wait_ge(step, STEPS * b + k[0])

                def first_maximum(values, hot):
                    then(ve.tensor_reduce(neg_max[:], values[:], AX.X, ALU.max, negate=True))
                    then(ve.tensor_tensor(first[:], values[:], last_axis(neg_max[:], E1), ALU.add))
                    then(ve.tensor_scalar(first[:], first[:], 0.0, float(-FAR), ALU.is_equal, ALU.mult))
                    then(ve.tensor_tensor(first[:], first[:], mid_axis(K.iota[:, 0:E1], TB), ALU.add))
                    then(ve.tensor_reduce(best[:], first[:], AX.X, ALU.min))
                    then(ve.tensor_scalar(best[:], best[:], float(FAR), None, ALU.add))
                    then(ve.tensor_tensor(hot[:], mid_axis(K.iota[:, 0:E1], TB), last_axis(best[:], E1), ALU.is_equal))

                dve.wait_ge(x_load, 16 * b + 16)
                statistics(dve, ve, x, stats, mv, var, TB, b, bn_done, aggr_done, stats_ready)
                dve.wait_ge(rstd_ready, b + 1)
                for t in range(TB):
                    ve.tensor_scalar(y[:, t, :], x[:, t, :], mv[:, t, 0:1], rstd[:, t:t + 1], ALU.subtract, ALU.mult).then_inc(y_ready, 1)
                dve.wait_ge(t_out, DC * b + DC)
                part = bass.ds(S * b, S) if not isinstance(b, int) else slice(S * b, S * b + S)
                ve.tensor_scalar(zT[0][:, :, part], yT[:], 1.0, None, ALU.mult).then_inc(z_hi, 1)
                dve.wait_ge(z_hi, b + 1)
                ve.tensor_tensor(zT[1][:, :, part], yT[:], zT[0][:, :, part].bitcast(F32), ALU.subtract).then_inc(z_lo, 1)
                dve.wait_ge(l_full, b + 1)
                then(ve.tensor_reduce(neg_max[:], logits, AX.X, ALU.max, negate=True))
                ve.tensor_tensor(rel[:], logits, last_axis(neg_max[:], E1), ALU.add).then_inc(rel_ready, 1)
                dve.wait_ge(exp_done, b + 1)
                then(ve.tensor_reduce(total[:], ex[:], AX.X, ALU.add))
                then(ve.reciprocal(inverse[:], total[:]))
                then(ve.tensor_tensor(scores[:], ex[:], last_axis(inverse[:], E1), ALU.mult))
                then(ve.tensor_tensor(biased[:], scores[:], mid_axis(gate_bias[:], TB), ALU.add))
                first_maximum(biased, one)
                then(ve.scalar_tensor_tensor(biased[:], one[:], -3.0e38, biased[:], ALU.mult, ALU.add))
                first_maximum(biased, two)
                then(ve.tensor_tensor(one[:], one[:], two[:], ALU.add))
                cols = weight[:, 0:E1, pick_range(b, TB)]
                ve.scalar_tensor_tensor(cols, one[:].rearrange("p t e -> p e t"), tg[:, 3:4],
                                        scores[:].rearrange("p t e -> p e t"), ALU.mult, ALU.mult).then_inc(weight_set, 1)
                assert k[0] == STEPS, k[0]
            each_batch(dve, batch)


def pick_range(b, n):
    return slice(n * b, n * b + n) if isinstance(b, int) else bass.ds(n * b, n)


def layer1_experts(nc, x3_dram, w1_d, w3_d, w2_d, zT, weight, out_dram):
    with ExitStack() as ctx:
        def sb(name, shape, dt=F32):
            return ctx.enter_context(nc.sbuf_tensor("m_" + name, shape, dt))

        def sem(name):
            return ctx.enter_context(nc.semaphore("m_" + name))

        w_in = sb("w_in", [P, 3, DC * F1])
        w = [sb("w_hi", [P, 2, 3, DC * F1], F32R), sb("w_lo", [P, 2, 3, DC * F1], F32R)]
        acc = sb("acc", [P, NT, D])
        act_h = sb("act_h", [P, 2, S])
        g = sb("g", [P, 2, S])
        hT = [sb("hT_hi", [P, 2, FT1, S], F32R), sb("hT_lo", [P, 2, FT1, S], F32R)]
        ps_h = ctx.enter_context(nc.psum_tensor("m_h", [P, 2, 2, BANK], F32))
        ps_o = ctx.enter_context(nc.psum_tensor("m_o", [P, TB, D], F32))

        x_load, w_load, w_hi, w_lo = sem("x_load"), sem("w_load"), sem("w_hi"), sem("w_lo")
        h_full, silu_done = sem("h_full"), sem("silu_done")
        g_ready = sem("g_ready")
        h_out = sem("h_out")
        o_full, acc_done, stored = sem("o_full"), sem("acc_done"), sem("stored")

        views = [w1_d.rearrange("e (c p) f -> p e c f", p=P), w3_d.rearrange("e (c p) f -> p e c f", p=P),
                 w2_d.rearrange("e (k p) m -> p e k m", p=P)]

        def experts(eng, expert):
            expert(0, 0)
            with eng.Fori(0, E1 // 2) as k:
                expert(2 * k + 1, 1)
                expert(2 * k + 2, 0)

        def batches(eng, e, slot, step):
            step(e, 0, 0, slot)
            step(e, 1, 1, slot)
            with eng.Fori(1, B // 2) as i:
                step(e, 2 * i, 0, slot)
                step(e, 2 * i + 1, 1, slot)

        block = ctx.enter_context(nc.Block())

        @block.sync
        def _(sp):
            def load(e):
                for j in range(3):
                    view = views[j]
                    src = view[:, e] if isinstance(e, int) else pick4(view, e)
                    n = src.shape[1]
                    nc.sync.dma_start(w_in[:, j].rearrange("p (c f) -> p c f", c=n), src).then_inc(w_load, 16)
            load(0)
            nc.sync.dma_start(acc[:], x3_dram.rearrange("b (t p) d -> p (b t) d", p=P)).then_inc(x_load, 16)
            with sp.Fori(1, EA) as e:
                sp.wait_ge(w_lo, 3 * e)
                load(e)
            ov = out_dram.rearrange("b (t p) d -> p b t d", p=P)
            for b in range(B):
                sp.wait_ge(acc_done, TB * (B * E1 + b + 1))
                nc.sync.dma_start(ov[:, b], acc[:, TB * b:TB * b + TB, :]).then_inc(stored, 16)
            sp.wait_ge(stored, 16 * B)

        @block.scalar
        def _(act):
            def split(e, slot):
                for j in range(3):
                    act.wait_ge(w_load, 48 * e + 48)
                    if not known(e, 0) and not known(e, 1):
                        act.wait_ge(o_full, B * e - B)
                    nc.scalar.activation(w[0][:, slot, j], w_in[:, j], ACT.Copy).then_inc(w_hi, 1)

            def step(e, b, par, slot):
                n = B * e + b
                for f in range(FT1):
                    act.wait_ge(h_full, FT1 * n + f + 1)
                    if not known(n, 0) or f >= 2:
                        act.wait_ge(g_ready, 2 * (FT1 * n + f - 1))
                    nc.scalar.activation(act_h[:, f % 2], ps_h[:, f % 2, 0], ACT.Silu).then_inc(silu_done, 1)

            split(0, 0)
            expert_s(act, step, split, 0, 0)
            with act.Fori(0, E1 // 2 - 1) as k:
                expert_s(act, step, split, 2 * k + 1, 1)
                expert_s(act, step, split, 2 * k + 2, 0)
            expert_s(act, step, split, E1 - 1, 1)
            expert_s(act, step, None, E1, 0)

        @block.gpsimd
        def _(pool):
            def lows(e, slot):
                for j in range(3):
                    pool.wait_ge(w_hi, 3 * e + j + 1)
                    nc.gpsimd.tensor_tensor(w[1][:, slot, j], w_in[:, j], w[0][:, slot, j].bitcast(F32), ALU.subtract).then_inc(w_lo, 1)

            def step(e, b, par, slot):
                n = B * e + b
                for f in range(FT1):
                    pool.wait_ge(g_ready, 2 * (FT1 * n + f + 1))
                    nc.gpsimd.tensor_tensor(hT[1][:, par, f], g[:, f % 2], hT[0][:, par, f].bitcast(F32), ALU.subtract).then_inc(h_out, 1)
            lows(0, 0)
            expert_s(pool, step, lows, 0, 0)
            with pool.Fori(0, E1 // 2 - 1) as k:
                expert_s(pool, step, lows, 2 * k + 1, 1)
                expert_s(pool, step, lows, 2 * k + 2, 0)
            expert_s(pool, step, lows, E1 - 1, 1)
            expert_s(pool, step, None, E1, 0)

        @block.vector
        def _(dve):
            ve = nc.vector
            dve.wait_ge(x_load, 16)

            def combine(e, b, n):
                dve.wait_ge(o_full, n + 1)
                if not known(n, 0):
                    dve.wait_ge(acc_done, TB * n)
                for t in range(TB):
                    at = TB * b + t
                    ve.scalar_tensor_tensor(pick(acc[:], at), ps_o[:, t, :], pick_cols(weight_flat, NT * e + at, 1), pick(acc[:], at),
                                            ALU.mult, ALU.add).then_inc(acc_done, 1)

            weight_flat = flat(weight[:])

            def step(e, b, par, slot):
                n = B * e + b
                for f in range(FT1):
                    dve.wait_ge(silu_done, FT1 * n + f + 1)
                    if f == 0 and not early(n, 2):
                        dve.wait_ge(o_full, n - 1)
                    ve.tensor_tensor(hT[0][:, par, f], act_h[:, f % 2], ps_h[:, f % 2, 1], ALU.mult).then_inc(g_ready, 1)
                    if not known(n, 0) or f >= 2:
                        dve.wait_ge(h_out, FT1 * n + f - 1)
                    ve.tensor_tensor(g[:, f % 2], act_h[:, f % 2], ps_h[:, f % 2, 1], ALU.mult).then_inc(g_ready, 1)
                if not known(n, 0):
                    if known(b, 0):
                        combine(e - 1, B - 1, n - 1)
                    else:
                        combine(e, b - 1, n - 1)

            experts(dve, lambda e, slot: batches(dve, e, slot, step))
            combine(E1, B - 1, B * EA - 1)

        @block.tensor
        def _(pe):
            t_ = nc.tensor

            def first_products(e, b, slot):
                n = B * e + b
                if known(b, 0):
                    pe.wait_ge(w_lo, 3 * e + 3)
                for f in range(FT1):
                    if not known(n, 0) or f >= 2:
                        pe.wait_ge(g_ready, 2 * (FT1 * n + f - 1))
                    for j in range(2):
                        for c in range(DC):
                            ws = slice(c * F1 + f * P, c * F1 + (f + 1) * P)
                            z = [part[:, c, pick_range(b, S)] for part in zT]
                            last = mm3(t_, ps_h[:, f % 2, j], w[0][:, slot, j, ws], w[1][:, slot, j, ws], z[0], z[1],
                                       c == 0, c == DC - 1)
                    last.then_inc(h_full, 1)

            def second_product(n, par, slot):
                pe.wait_ge(h_out, FT1 * n + FT1)
                if not known(n, 0):
                    pe.wait_ge(acc_done, TB * n)
                for t in range(TB):
                    rs = slice(t * P, (t + 1) * P)
                    for f in range(FT1):
                        last = mm3(t_, ps_o[:, t, :], hT[0][:, par, f, rs], hT[1][:, par, f, rs],
                                   w[0][:, slot, 2, f * D:(f + 1) * D], w[1][:, slot, 2, f * D:(f + 1) * D], f == 0, f == FT1 - 1)
                last.then_inc(o_full, 1)

            def step(e, b, par, slot):
                first_products(e, b, slot)
                n = B * e + b
                if not known(n, 0):
                    second_product(n - 1, 1 - par, 1 - slot if known(b, 0) else slot)

            experts(pe, lambda e, slot: batches(pe, e, slot, step))
            second_product(B * EA - 1, 1, 0)


def expert_s(eng, step, split, e, slot):
    step(e, 0, 0, slot)
    step(e, 1, 1, slot)
    if split:
        split(e + 1, 1 - slot)
    with eng.Fori(1, B // 2) as i:
        step(e, 2 * i, 0, slot)
        step(e, 2 * i + 1, 1, slot)


class Constants:

    def __init__(self, nc, ctx):
        def sb(name, shape, dt=F32):
            return ctx.enter_context(nc.sbuf_tensor("k_" + name, shape, dt))

        self.ident = sb("ident", [P, P])
        self.ident_r = sb("ident_r", [P, P], F32R)
        self.ones = sb("ones", [P, P])
        self.before = sb("before", [P, P])
        self.iota = sb("iota", [P, E0])
        self.neg_half = sb("neg_half", [P, 1])
        self.pool_scratch = sb("pool_scratch", [P, 1])
        self.iota_i = sb("iota_i", [P, E0], I32)

    def fill(self, nc, ctx):
        step = ctx.enter_context(nc.semaphore("k_step"))
        with nc.Block() as block:
            @block.gpsimd
            def _(pool):
                g = nc.gpsimd
                g.memset(self.ident[:], 0.0).then_inc(step, 1)
                g.memset(self.ones[:], 1.0).then_inc(step, 1)
                g.memset(self.before[:], 1.0).then_inc(step, 1)
                g.memset(self.neg_half[:], -0.5).then_inc(step, 1)
                g.iota(self.iota_i[:], pattern=[[1, E0]], base=0, channel_multiplier=0).then_inc(step, 1)
                pool.wait_ge(step, 5)
                g.affine_select(out=self.ident[:], in_=self.ident[:], compare_op=ALU.not_equal, fill=1.0, base=0,
                                pattern=[[-1, P]], channel_multiplier=1).then_inc(step, 1)
                g.affine_select(out=self.before[:], in_=self.before[:], compare_op=ALU.is_gt, fill=0.0, base=0,
                                pattern=[[1, P]], channel_multiplier=-1).then_inc(step, 1)
                g.tensor_copy(self.iota[:], self.iota_i[:]).then_inc(step, 1)
                pool.wait_ge(step, 8)
                g.tensor_copy(self.ident_r[:], self.ident[:]).then_inc(step, 1)
                pool.wait_ge(step, 9)


def clear(nc, tables):
    with ExitStack() as ctx:
        zero = ctx.enter_context(nc.sbuf_tensor("z_zero", [P, 4096], F32))
        z, done = ctx.enter_context(nc.semaphore("z_z")), ctx.enter_context(nc.semaphore("z_done"))
        with nc.Block() as block:
            @block.vector
            def _(dve):
                nc.vector.memset(zero[:], 0.0).then_inc(z, 1)

            @block.sync
            def _(sp):
                sp.wait_ge(z, 1)
                n = 0
                for table in tables:
                    v = table.rearrange("(p r) d -> p (r d)", p=P)
                    for at in range(0, v.shape[1], 4096):
                        w = min(4096, v.shape[1] - at)
                        nc.sync.dma_start(v[:, at:at + w], zero[:, 0:w]).then_inc(done, 16)
                        n += 16
                sp.wait_ge(done, n)


def flamingo(nc, t_in, out):
    with ExitStack() as ctx:
        def dram(name, shape):
            return nc.dram_tensor(name, shape, F32).ap()

        K = Constants(nc, ctx)
        tg = ctx.enter_context(nc.sbuf_tensor("tg", [P, 4], F32))
        x1, x3 = dram("x1_dram", (B, S, D)), dram("x3_dram", (B, S, D))
        rows_in, rows_out = dram("rows_in_dram", (E0 * C0, D)), dram("rows_out_dram", (E0 * C0, D))
        K.fill(nc, ctx)
        clear(nc, [rows_in])
        layer0_attention(nc, tuple(t_in[n] for n in (
            "x", "ctx_1024", "g_xattn", "g_ffn", "L0_xattn_gamma_media", "L0_xattn_beta_media", "L0_xattn_gamma_lat",
            "L0_xattn_beta_lat", "L0_xattn_Wq", "L0_xattn_bq", "L0_xattn_Wkv", "L0_xattn_bkv", "L0_xattn_Wo", "L0_xattn_bo")),
            K.ident, tg, x1)
        with ExitStack() as routed:
            route_row = routed.enter_context(nc.sbuf_tensor("route_row", [P, NT], I32))
            route_w = routed.enter_context(nc.sbuf_tensor("route_w", [P, NT], F32))
            layer0_route(nc, x1, t_in["L0_ffn_Wg"], rows_in, K, tg, route_row, route_w)
            layer0_experts(nc, rows_in, t_in["L0_ffn_w1"], t_in["L0_ffn_w2"], rows_out, K)
            layer1_attention(nc, x1, t_in["ctx_1024"], t_in["L1_xattn_w_q"], t_in["L1_xattn_w_k"], t_in["L1_xattn_w_v"],
                             t_in["L1_xattn_w_o"], route_row, route_w, rows_out, tg, x3, K)
        zT = [ctx.enter_context(nc.sbuf_tensor("zT_hi", [P, DC, B * S], F32R)),
              ctx.enter_context(nc.sbuf_tensor("zT_lo", [P, DC, B * S], F32R))]
        weight = ctx.enter_context(nc.sbuf_tensor("weight", [P, EA, NT], F32))
        layer1_gate(nc, x3, t_in["L1_ffn_gate_w"], t_in["L1_ffn_gate_bias"], K, tg, zT, weight)
        layer1_experts(nc, x3, t_in["w1_all"], t_in["w3_all"], t_in["w2_all"], zT, weight, out)



def kernel(**inputs):
    import concourse.bacc as bacc
    from concourse.bass_utils import run_bass_kernel_spmd

    arrays = {k: np.asarray(v) for k, v in inputs.items()}
    for j in (1, 2, 3):
        experts, shared = arrays.pop(f"L1_ffn_w{j}"), arrays.pop(f"L1_ffn_sw{j}")
        arrays[f"w{j}_all"] = np.concatenate([experts, shared[None]]).transpose(0, 2, 1)
    for name in ("L1_xattn_w_q", "L1_xattn_w_k", "L1_xattn_w_v", "L1_xattn_w_o", "L1_ffn_gate_w"):
        arrays[name] = arrays[name].T
    arrays = {k: np.ascontiguousarray(v) for k, v in arrays.items()}

    nc = bacc.Bacc("TRN2", target_bir_lowering=False, num_devices=1)
    t_in = {k: nc.dram_tensor(k + "_in", v.shape, mybir.dt.from_np(v.dtype), kind="ExternalInput").ap() for k, v in arrays.items()}
    out = nc.dram_tensor("out", (B, S, D), F32, kind="ExternalOutput").ap()
    flamingo(nc, t_in, out)
    r = run_bass_kernel_spmd(nc, [{k + "_in": v for k, v in arrays.items()}], core_ids=[0])
    return r.results[0]["out"]
```

```python
from contextlib import ExitStack

import numpy as np
import concourse.bass as bass
from concourse import mybir

ALU = mybir.AluOpType
ACT = mybir.ActivationFunctionType
AX = mybir.AxisListType
F32 = mybir.dt.float32
F32R = mybir.dt.float32r
I32 = mybir.dt.int32

P = 128
B, S, D = 8, 512, 256
TB = S // P
NT = B * TB
DC = D // P
BANK = 512
EPS = 1e-5

H0, DH0 = 8, 128
INNER = H0 * DH0
KV0 = 2 * S
KT0 = KV0 // P


def mm3(pe, out, l_hi, l_lo, r_hi, r_lo, start, stop):
    pe.matmul(out, l_hi, r_hi, start=start, stop=False)
    pe.matmul(out, l_hi, r_lo, start=False, stop=False)
    return pe.matmul(out, l_lo, r_hi, start=False, stop=stop)


def known(v, value):
    return isinstance(v, int) and v == value


def flat(ap):
    n = len(ap.shape) - 1
    names = "abcd"[:n]
    return ap.rearrange(f"p {' '.join(names)} -> p ({' '.join(names)})") if n > 1 else ap


def pick(ap, i):
    one = ap[:, i:i + 1] if isinstance(i, int) else ap[:, bass.ds(i, 1)]
    return one.rearrange("p o n -> p (o n)")


def layer0_attention(nc, t_in, ident, tg, x1_dram, tables):
    with ExitStack() as ctx:
        def sb(name, shape, dt=F32):
            return ctx.enter_context(nc.sbuf_tensor("a_" + name, shape, dt))

        def sem(name):
            return ctx.enter_context(nc.semaphore("a_" + name))

        w_stage = sb("w_stage", [P, 2, 2, DC, DH0])
        wqk = [sb("wqk_hi", [P, 2, 2, DC, DH0], F32R), sb("wqk_lo", [P, 2, 2, DC, DH0], F32R)]
        wv = [sb("wv_hi", [P, DC, INNER], F32R), sb("wv_lo", [P, DC, INNER], F32R)]
        wo = [sb("wo_hi", [P, H0, D], F32R), sb("wo_lo", [P, H0, D], F32R)]
        cols = sb("cols", [P, 4, DC])
        bias = sb("bias", [P, H0, 3])
        qk_bias = sb("qk_bias", [P, 2, 2])
        v_bias = sb("v_bias", [P, 1])
        tbo = sb("tbo", [P, D])
        x_in = sb("x_in", [P, 2 * TB, D])
        y = sb("y", [P, 2 * TB, D])
        stats = sb("stats", [P, 2 * TB, 6])
        mv = sb("mv", [P, 2 * TB, 2])
        var = sb("var", [P, 2 * TB])
        rstd = sb("rstd", [P, 2 * TB])
        vtmp = sb("vtmp", [P, TB])
        consts = sb("consts", [P, 4])
        x_acc = sb("x_acc", [P, TB, D])
        kvT = [sb("kvT_hi", [P, DC, KV0], F32R), sb("kvT_lo", [P, DC, KV0], F32R)]
        zero = sb("zero", [P, 1024])
        qT = [sb("qT_hi", [P, 2, S], F32R), sb("qT_lo", [P, 2, S], F32R)]
        kT = [sb("kT_hi", [P, 2, KV0], F32R), sb("kT_lo", [P, 2, KV0], F32R)]
        v = [sb("v_hi", [P, KT0, 2 * DH0], F32R), sb("v_lo", [P, KT0, 2 * DH0], F32R)]
        neg_max = sb("neg_max", [P, TB])
        row_sum = sb("row_sum", [P, 2, TB])
        inv_sum = sb("inv_sum", [P, 2, TB])
        prob = sb("prob", [P, TB, KV0])
        pT = [sb("pT_hi", [P, KT0, S], F32R), sb("pT_lo", [P, KT0, S], F32R)]
        inv_row = sb("inv_row", [P, S])
        o_norm = sb("o_norm", [P, S])
        oT = [sb("oT_hi", [P, 2, S], F32R), sb("oT_lo", [P, 2, S], F32R)]

        pj = ctx.enter_context(nc.psum_tensor("a_pj", [P, 2, BANK], F32))
        ps_s = ctx.enter_context(nc.psum_tensor("a_scores", [P, 2, KV0], F32))
        ps_t = ctx.enter_context(nc.psum_tensor("a_probT", [P, 2, BANK], F32))

        loaded = sem("loaded")
        cleared = sem("cleared")
        w_load = [sem("w_load_A"), sem("w_load_B")]
        w_split = sem("w_split")
        big_hi = sem("big_hi")
        big_lo = sem("big_lo")
        w_step = sem("w_step")
        consts_set = sem("consts_set")
        set_up = sem("set_up")
        qk_bias_set = sem("qk_bias_set")
        v_bias_set = sem("v_bias_set")
        x_load = sem("x_load")
        stats_ready = sem("stats_ready")
        rstd_ready = sem("rstd_ready")
        y_ready = sem("y_ready")
        ln_step = sem("ln_step")
        pj_full = sem("pj_full")
        pj_out = sem("pj_out")
        hi_done = sem("hi_done")
        s_full = sem("s_full")
        max_done = sem("max_done")
        exp_done = sem("exp_done")
        inv_done = sem("inv_done")
        t_full = sem("t_full")
        t_hi = sem("t_hi")
        t_out = sem("t_out")
        inv_row_done = sem("inv_row_done")
        affine_done = sem("affine_done")
        bn_done = sem("bn_done")
        aggr_done = sem("aggr_done")
        o_hi = sem("o_hi")
        o_lo = sem("o_lo")
        acc_init = sem("acc_init")
        stored = sem("stored")

        (x_d, ctx_d, g_x, g_f, gm, bm, gl, bl, wq_d, bq_d, wkv_d, bkv_d, wo_d, bo_d) = t_in
        xv = x_d.rearrange("b (t p) d -> p b t d", p=P)
        cv = ctx_d.rearrange("b (t p) d -> p b t d", p=P)
        x1v = x1_dram.rearrange("b (t p) d -> p b t d", p=P)
        wq_v = wq_d.rearrange("(c p) (h d) -> p h c d", p=P, d=DH0)
        wk_v = wkv_d[:, 0:INNER].rearrange("(c p) (h d) -> p h c d", p=P, d=DH0)
        wv_v = wkv_d[:, INNER:].rearrange("(c p) n -> p c n", p=P)
        wo_v = wo_d.rearrange("(h p) n -> p h n", p=DH0)
        N_CONST = 12

        def pj_start(b, hp):
            return 7 if known(b, 0) and known(hp, 0) else 3 + 68 * b + 16 * hp

        def hi_start(b, hp):
            return 7 + 44 * b + 10 * hp

        def at(v4, i):
            return v4[:, bass.ds(i, 1)].rearrange("p o t d -> p (o t) d")

        FIN = ("fin", 0)

        def plan(b, hp, par):
            def some(kind, *js):
                return [(kind, j) for j in js]

            if par == 0:
                return [some("qk", 0, 1), [] if known(b, 0) and known(hp, 0) else [FIN], some("qk", 2) + some("v", 0, 1), some("v", 2, 3)]
            out = [] if known(b, 0) and known(hp, 0) else some("out", 0, 1)
            if not known(hp, 3):
                return [out, [FIN], some("qk", 0, 1), some("qk", 2)]
            if known(b, B - 1):
                return [out, [FIN], [], []]
            return [out + some("pro", 0, 1), [FIN], some("pro", 2, 3), some("qk", 0, 1, 2)]

        SCORES = ((0,), (1, 2), (3,), ())

        def width(use):
            return 2 if use == FIN else 1

        def highs(use):
            return use[0] in ("qk", "v", "pro")

        def qk_dst(part, j, par):
            if j == 0:
                return qT[part][:, par]
            return kT[part][:, par, (j - 1) * S:j * S]

        block = ctx.enter_context(nc.Block())

        def batches(eng, pair):
            def batch(b):
                pair(b, 0)
                with eng.Fori(1, 3) as hp:
                    pair(b, hp)
                pair(b, 3)
            batch(0)
            with eng.Fori(1, B - 1) as b:
                batch(b)
            batch(B - 1)

        @block.sync
        def _(sp):
            dma = nc.sync.dma_start
            with nc.allow_non_contiguous_dma(reason="columns of biases, once"):
                for i, a in enumerate((gm, bm, gl, bl)):
                    dma(cols[:, i, :], a.rearrange("(c p) -> p c", p=P)).then_inc(loaded, 16)
                dma(bias[:, :, 0], bq_d.rearrange("(h p) -> p h", p=P)).then_inc(loaded, 16)
                dma(bias[:, :, 1], bkv_d[0:INNER].rearrange("(h p) -> p h", p=P)).then_inc(loaded, 16)
                dma(bias[:, :, 2], bkv_d[INNER:].rearrange("(h p) -> p h", p=P)).then_inc(loaded, 16)
            dma(tbo[:], bo_d.rearrange("(o d) -> o d", o=1).to_broadcast([P, D])).then_inc(loaded, 16)
            dma(tg[:, 0:2], g_x.rearrange("(o d) -> o d", o=1).to_broadcast([P, 2])).then_inc(loaded, 16)
            dma(tg[:, 2:4], g_f.rearrange("(o d) -> o d", o=1).to_broadcast([P, 2])).then_inc(loaded, 16)
            dma(prob[:, 0:2, :], wv_v).then_inc(loaded, 16)
            dma(prob[:, 2:4, :].rearrange("p a (h n) -> p (a h) n", n=D), wo_v).then_inc(loaded, 16)

            def load_tokens(b):
                dma(x_in[:, 0:TB, :], at(cv, b)).then_inc(x_load, 16)
                dma(x_in[:, TB:, :], at(xv, b)).then_inc(x_load, 16)

            def load_w(n, h, par):
                dma(w_stage[:, par, 0], at(wq_v, h)).then_inc(w_load[par], 16)
                dma(w_stage[:, par, 1], at(wk_v, h)).then_inc(w_load[par], 16)

            load_tokens(0)
            load_w(0, 0, 0)
            load_w(1, 1, 1)
            sp.wait_ge(w_split, 1)
            load_w(2, 2, 0)
            sp.wait_ge(w_split, 2)
            load_w(3, 3, 1)
            sp.wait_ge(set_up, 1)
            for table in tables:
                wide = table.rearrange("(p k r) d -> p k (r d)", p=P, r=1024 // D)
                dma(wide, zero[:].rearrange("p (o n) -> p o n", o=1).to_broadcast([P, wide.shape[1], 1024])).then_inc(cleared, 16)

            def batch(b):
                if not known(b, 0):
                    sp.wait_ge(pj_out, pj_start(b, 0) + 11)
                    dma(at(x1v, b - 1), x_acc[:]).then_inc(stored, 16)
                last = known(b, B - 1)
                if not last:
                    sp.wait_ge(acc_init, b + 1)
                    load_tokens(b + 1)
                for hp in range(2 if last else 4):
                    n, h = 8 * b + 2 * hp, (2 * hp + 4) % H0
                    sp.wait_ge(w_split, n + 3)
                    load_w(n + 4, h, 0)
                    sp.wait_ge(w_split, n + 4)
                    load_w(n + 5, h + 1, 1)
            batch(0)
            with sp.Fori(1, B - 1) as b:
                batch(b)
            batch(B - 1)
            sp.wait_ge(pj_out, pj_start(B - 1, 3) + 17)
            dma(x1v[:, B - 1], x_acc[:]).then_inc(stored, 16)
            sp.wait_ge(stored, 16 * B)
            sp.wait_ge(cleared, 16 * len(tables))

        @block.gpsimd
        def _(pool):
            g = nc.gpsimd
            for i, value in enumerate((-0.5, EPS, DH0 ** -0.5, 0.0)):
                g.memset(consts[:, i:i + 1], value).then_inc(consts_set, 1)

            def const(i, shape):
                return consts[:, i:i + 1].to_broadcast(shape)

            def split_w(n, par, after):
                pool.wait_ge(w_load[par], after)
                if not (isinstance(n, int) and n < 2):
                    pool.wait_ge(s_full, 4 * (n - 2) + 1)
                q, every, hi = flat(w_stage[:, par, 0]), flat(w_stage[:, par]), flat(wqk[0][:, par])
                g.tensor_tensor(q, q, const(2, [P, DC * DH0]), ALU.mult).then_inc(w_step, 1)
                pool.wait_ge(w_step, 2 * n + 1)
                g.tensor_tensor(hi, every, const(3, [P, 2 * DC * DH0]), ALU.add).then_inc(w_step, 1)
                pool.wait_ge(w_step, 2 * n + 2)
                g.tensor_tensor(flat(wqk[1][:, par]), every, hi.bitcast(F32), ALU.subtract).then_inc(w_split, 1)

            def inverse_std(b):
                lat = rstd[:, TB:]
                pool.wait_ge(stats_ready, 2 * b + 2)
                g.tensor_tensor(rstd[:], var[:], const(0, [P, 2 * TB]), ALU.pow).then_inc(ln_step, 1)
                pool.wait_ge(ln_step, 5 * b + 1)
                g.tensor_tensor(vtmp[:], lat, lat, ALU.mult).then_inc(ln_step, 1)
                pool.wait_ge(ln_step, 5 * b + 2)
                g.tensor_tensor(vtmp[:], vtmp[:], flat(mv[:, TB:, 1:2]), ALU.mult).then_inc(ln_step, 1)
                pool.wait_ge(ln_step, 5 * b + 3)
                g.tensor_tensor(vtmp[:], vtmp[:], const(1, [P, TB]), ALU.add).then_inc(ln_step, 1)
                pool.wait_ge(ln_step, 5 * b + 4)
                g.tensor_tensor(vtmp[:], vtmp[:], const(0, [P, TB]), ALU.pow).then_inc(ln_step, 1)
                pool.wait_ge(ln_step, 5 * b + 5)
                g.tensor_tensor(lat, lat, vtmp[:], ALU.mult).then_inc(rstd_ready, 1)

            pool.wait_ge(consts_set, 4)
            inverse_std(0)
            split_w(0, 0, 32)
            split_w(1, 1, 32)

            def pair(b, hp):
                n = 8 * b + 2 * hp
                i3 = known(hp, 3)
                if known(b, B - 1) and i3:
                    return
                if i3:
                    inverse_std(b + 1)
                turn = 4 * b + hp
                split_w(n + 2, 0, 32 * turn + 64)
                split_w(n + 3, 1, 32 * turn + 64)
            batches(pool, pair)

        @block.scalar
        def _(act):
            a = nc.scalar.activation
            act.wait_ge(loaded, 16 * N_CONST)
            a(tg[:], tg[:], ACT.Tanh).then_inc(big_hi, 1)
            a(flat(wv[0][:]), flat(prob[:, 0:2, :]), ACT.Copy).then_inc(big_hi, 1)
            a(flat(wo[0][:]), flat(prob[:, 2:4, :]), ACT.Copy).then_inc(big_hi, 1)

            def use_bank(use, u, bank, n, par):
                kind, j = use
                src = pj[:, bank, :]
                if kind == "out":
                    return
                if kind == "qk" and j == 0:
                    act.wait_ge(qk_bias_set, n + 2)
                act.wait_ge(pj_full, u + 1)
                if kind == "qk":
                    i = min(j, 1)
                    a(qk_dst(0, j, 1 - par), src, ACT.Identity, bias=qk_bias[:, 1 - par, i:i + 1]).then_inc(hi_done, 1)
                elif kind == "v":
                    a(flat(v[0][:, 2 * j:2 * j + 2, :]), src, ACT.Copy).then_inc(hi_done, 1)
                elif kind == "pro":
                    c, half = j % 2, j // 2
                    a(kvT[0][:, c, half * S:(half + 1) * S], src, ACT.Identity,
                      bias=cols[:, 2 * half + 1, c:c + 1], scale=cols[:, 2 * half, c:c + 1]).then_inc(hi_done, 1)
                else:
                    a(inv_row[:], src, ACT.Copy).then_inc(inv_row_done, 1)

            def prob_high(n, qt):
                for half in range(2):
                    act.wait_ge(t_full, 8 * n + 2 * qt + half + 1)
                    a(pT[0][:, 4 * half:4 * half + 4, qt * P:(qt + 1) * P],
                      ps_t[:, half, :].rearrange("p (k q) -> p k q", k=4), ACT.Copy).then_inc(t_hi, 1)

            def exp(n, qt, par):
                act.wait_ge(max_done, 4 * n + qt + 1)
                if not known(n, 0):
                    act.wait_ge(t_full, 8 * n + 2 * qt - 6)
                a(prob[:, qt, :], ps_s[:, qt % 2, :], ACT.Exp, bias=neg_max[:, qt:qt + 1],
                  accum_out=row_sum[:, par, qt:qt + 1]).then_inc(exp_done, 1)

            def finish_o(n, par, u):
                act.wait_ge(pj_out, u)
                act.wait_ge(v_bias_set, n + 1)
                a(oT[0][:, par, :], o_norm[:], ACT.Identity, bias=v_bias[:]).then_inc(o_hi, 1)

            for j in range(4):
                use_bank(("pro", j), j, j % 2, 0, 0)
            for j in range(3):
                use_bank(("qk", j), 4 + j, j % 2, -1, 1)

            def step(b, hp, par, u, bank):
                n = 8 * b + 2 * hp + par
                first = known(n, 0)
                for q, todo in enumerate(plan(b, hp, par)):
                    if q == 2 and not first:
                        finish_o(n - 1, 1 - par, u)
                    if todo and todo != [FIN]:
                        use_bank(todo[0], u, bank, n, par)
                    for i, qt in enumerate(SCORES[q]):
                        if i and not first:
                            use_bank(FIN, u, bank, n, par)
                        exp(n, qt, par)
                    for i, use in enumerate(todo):
                        if i:
                            use_bank(use, u, bank, n, par)
                        u, bank = u + width(use), (bank + width(use)) % 2
                    if q:
                        prob_high(n, q - 1)
                    elif not first:
                        prob_high(n - 1, 3)
                return u, bank

            def pair(b, hp):
                u, bank = step(b, hp, 0, pj_start(b, hp), 1)
                step(b, hp, 1, u, bank)

            batches(act, pair)
            n, u = 8 * B - 1, pj_start(B - 1, 3) + 13
            prob_high(n, 3)
            use_bank(FIN, u, u % 2, n, 1)
            finish_o(n, 1, u + 2)

        @block.vector
        def _(dve):
            ve = nc.vector

            def lo(out, ps, hi_ap, bias_ap=None):
                if bias_ap is None:
                    return ve.tensor_tensor(out, ps, hi_ap.bitcast(F32), ALU.subtract)
                return ve.scalar_tensor_tensor(out, ps, bias_ap, hi_ap.bitcast(F32), ALU.add, ALU.subtract)

            def use_bank(use, u, k, bank, n, par, b):
                kind, j = use
                src = pj[:, bank, :]
                if highs(use):
                    dve.wait_ge(hi_done, k + 1)
                elif kind == "out":
                    dve.wait_ge(pj_full, u + 1)
                if kind == "qk":
                    i = min(j, 1)
                    lo(qk_dst(1, j, 1 - par), src, qk_dst(0, j, 1 - par), qk_bias[:, 1 - par, i:i + 1]).then_inc(pj_out, 1)
                elif kind == "v":
                    lo(flat(v[1][:, 2 * j:2 * j + 2, :]), src, flat(v[0][:, 2 * j:2 * j + 2, :])).then_inc(pj_out, 1)
                elif kind == "pro":
                    c, half = j % 2, j // 2
                    ve.tensor_scalar(src, src, cols[:, 2 * half, c:c + 1],
                                     cols[:, 2 * half + 1, c:c + 1], ALU.mult, ALU.add).then_inc(affine_done, 1)
                    dve.wait_ge(affine_done, 4 * b + j + 1)
                    span = slice(half * S, (half + 1) * S)
                    lo(kvT[1][:, c, span], src, kvT[0][:, c, span]).then_inc(pj_out, 1)
                elif kind == "out":
                    if j == 0:
                        dve.wait_ge(pj_out, u)
                        dve.wait_ge(acc_init, b)
                    part = flat(x_acc[:, 2 * j:2 * j + 2, :])
                    ve.scalar_tensor_tensor(part, src, tg[:, 0:1], part, ALU.mult, ALU.add).then_inc(pj_out, 1)
                else:
                    dve.wait_ge(inv_row_done, n)
                    dve.wait_ge(pj_full, u + 2)
                    ve.tensor_tensor(o_norm[:], pj[:, 1 - bank, :], inv_row[:], ALU.mult).then_inc(pj_out, 2)

            def set_qk_bias(h, par):
                ve.tensor_copy(qk_bias[:, par, :], pick(bias[:], h)[:, 0:2]).then_inc(qk_bias_set, 1)

            def set_v_bias(h):
                ve.tensor_copy(v_bias[:], pick(bias[:], h)[:, 2:3]).then_inc(v_bias_set, 1)

            def prob_low(n, qt):
                for half in range(2):
                    dve.wait_ge(t_hi, 8 * n + 2 * qt + half + 1)
                    dst = pT[1][:, 4 * half:4 * half + 4, qt * P:(qt + 1) * P]
                    src = pT[0][:, 4 * half:4 * half + 4, qt * P:(qt + 1) * P]
                    lo(dst, ps_t[:, half, :].rearrange("p (k q) -> p k q", k=4), src).then_inc(t_out, 1)

            def row_max(n, qt):
                dve.wait_ge(s_full, 4 * n + qt + 1)
                ve.tensor_reduce(neg_max[:, qt:qt + 1], ps_s[:, qt % 2, :], AX.X, ALU.max, negate=True).then_inc(max_done, 1)

            def invert_sums(n, par):
                dve.wait_ge(exp_done, 4 * n + 4)
                ve.reciprocal(inv_sum[:, par, :], row_sum[:, par, :]).then_inc(inv_done, 1)

            def o_low(n, par):
                dve.wait_ge(o_hi, n + 1)
                lo(oT[1][:, par, :], o_norm[:], oT[0][:, par, :], v_bias[:]).then_inc(o_lo, 1)

            def statistics(b, part=None):
                T = 2 * TB
                if not part:
                    dve.wait_ge(x_load, 32 * b + 32)
                for t in range(T) if part is None else ((0, 1, 2), (3, 4, 5), (6, 7))[part]:
                    if t:
                        dve.wait_ge(bn_done, T * b + t)
                    ve.bn_stats(stats[:, t, :], x_in[:, t, :]).then_inc(bn_done, 1)
                    if t:
                        ve.bn_aggr(mv[:, t - 1, :], stats[:, t - 1, :]).then_inc(aggr_done, 1)
                if part is not None and part < 2:
                    return
                dve.wait_ge(bn_done, T * b + T)
                dve.wait_ge(aggr_done, T * b + T - 1)
                ve.tensor_scalar(var[:, 0:T - 1], flat(mv[:, 0:T - 1, 1:2]), EPS, None, ALU.add).then_inc(stats_ready, 1)
                ve.bn_aggr(mv[:, T - 1, :], stats[:, T - 1, :]).then_inc(aggr_done, 1)
                dve.wait_ge(aggr_done, T * b + T)
                ve.tensor_scalar(var[:, T - 1:], flat(mv[:, T - 1:, 1:2]), EPS, None, ALU.add).then_inc(stats_ready, 1)

            def normalise(b):
                dve.wait_ge(rstd_ready, b + 1)
                for t in range(2 * TB):
                    last = ve.tensor_scalar(y[:, t, :], x_in[:, t, :], mv[:, t, 0:1], rstd[:, t:t + 1], ALU.subtract, ALU.mult)
                    last.then_inc(y_ready, 1)

            def init_acc(b):
                if not known(b, 0):
                    dve.wait_ge(stored, 16 * b)
                ve.tensor_tensor(x_acc[:], x_in[:, TB:, :], tbo[:].rearrange("p (o d) -> p o d", o=1).to_broadcast([P, TB, D]), ALU.add).then_inc(acc_init, 1)

            ve.memset(zero[:], 0.0).then_inc(set_up, 1)
            statistics(0)
            for i, (w, rows) in enumerate(((wv, slice(0, 2)), (wo, slice(2, 4)))):
                dve.wait_ge(big_hi, i + 2)
                ve.tensor_tensor(flat(w[1][:]), flat(prob[:, rows, :]), flat(w[0][:]).bitcast(F32), ALU.subtract).then_inc(big_lo, 1)
            dve.wait_ge(big_hi, 1)
            ve.tensor_scalar(tbo[:], tbo[:], tg[:, 0:1], None, ALU.mult).then_inc(set_up, 1)
            ve.tensor_scalar(bias[:, :, 0:1], bias[:, :, 0:1], DH0 ** -0.5, None, ALU.mult).then_inc(set_up, 1)
            normalise(0)
            dve.wait_ge(set_up, 3)
            set_qk_bias(0, 0)
            for j in range(4):
                use_bank(("pro", j), j, j, j % 2, 0, 0, 0)
            for j in range(3):
                use_bank(("qk", j), 4 + j, 4 + j, j % 2, -1, 1, 0)

            def step(b, hp, par, u, k, bank):
                n = 8 * b + 2 * hp + par
                first = known(n, 0)
                pair3 = known(hp, 3)
                last = known(b, B - 1) and pair3
                if par == 0 or not last:
                    set_qk_bias(2 * hp + 1 if par == 0 else (0 if pair3 else 2 * hp + 2), 1 - par)
                if not first:
                    if not known(n, 1):
                        dve.wait_ge(o_lo, n - 1)
                    set_v_bias((H0 - 1 if known(hp, 0) else 2 * hp - 1) if par == 0 else 2 * hp)
                    invert_sums(n - 1, 1 - par)
                for q, todo in enumerate(plan(b, hp, par)):
                    for qt in SCORES[q]:
                        row_max(n, qt)
                    if q == 2 and not first and not todo:
                        o_low(n - 1, 1 - par)
                    for i, use in enumerate(todo):
                        use_bank(use, u, k, bank, n, par, b if known(hp, 0) and use[0] == "out" else b + 1)
                        u, k, bank = u + width(use), k + highs(use), (bank + width(use)) % 2
                        if q == 2 and not first and i == 0:
                            o_low(n - 1, 1 - par)
                    if q:
                        prob_low(n, q - 1)
                    elif not first:
                        prob_low(n - 1, 3)
                    if par == 0 and pair3 and not last:
                        if q < 3:
                            statistics(b + 1, q)
                        else:
                            normalise(b + 1)
                if par == 1 and known(hp, 0):
                    init_acc(b)
                return u, k, bank

            def pair(b, hp):
                u, k, bank = step(b, hp, 0, pj_start(b, hp), hi_start(b, hp), 1)
                step(b, hp, 1, u, k, bank)

            batches(dve, pair)
            n, u = 8 * B - 1, pj_start(B - 1, 3) + 13
            dve.wait_ge(o_lo, n)
            set_v_bias(H0 - 1)
            invert_sums(n, 1)
            prob_low(n, 3)
            use_bank(FIN, u, 0, u % 2, n + 1, 0, 0)
            o_low(n, 1)
            for j in range(2):
                use_bank(("out", j), u + 2 + j, 0, (u + j) % 2, n, 1, B)

        @block.tensor
        def _(pe):
            t = nc.tensor

            def free_bank(u):
                if not (isinstance(u, int) and u < 2):
                    pe.wait_ge(pj_out, u - 1)

            def finish(n, par, u, bank, between=None):
                pe.wait_ge(inv_done, n + 1)
                for qt in range(TB):
                    last = t.matmul(pj[:, bank, qt * P:(qt + 1) * P], inv_sum[:, par, qt:qt + 1].to_broadcast([P, P]),
                                    ident[:], is_transpose=True)
                last.then_inc(pj_full, 1)
                free_bank(u + 1)
                pe.wait_ge(t_out, 8 * n + 8)
                for kt in range(KT0):
                    if kt == KT0 // 2 and between:
                        between()
                    d = slice(par * DH0, (par + 1) * DH0)
                    last = mm3(t, pj[:, 1 - bank, :], v[0][:, kt, d], v[1][:, kt, d], pT[0][:, kt, :], pT[1][:, kt, :],
                               kt == 0, kt == KT0 - 1)
                last.then_inc(pj_full, 1)

            def use_bank(use, u, bank, n, par, b, hp, between=None):
                kind, j = use
                dst = pj[:, bank, :]
                if kind == "qk" and j == 0:
                    pe.wait_ge(w_split, n + 2)
                elif kind == "out" and j == 0:
                    pe.wait_ge(o_lo, n - 1)
                elif kind == "pro" and j == 0:
                    pe.wait_ge(y_ready, 8 * b + 8)
                free_bank(u)
                if kind == "qk":
                    span = (slice(S, KV0), slice(0, S), slice(S, KV0))[j]
                    for c in range(DC):
                        last = mm3(t, dst, wqk[0][:, 1 - par, min(j, 1), c], wqk[1][:, 1 - par, min(j, 1), c],
                                   kvT[0][:, c, span], kvT[1][:, c, span], c == 0, c == DC - 1)
                elif kind == "v":
                    for kt in (2 * j, 2 * j + 1):
                        for c in range(DC):
                            two = slice(hp * 256, hp * 256 + 256) if isinstance(hp, int) else bass.ds(hp * 256, 256)
                            last = mm3(t, dst[:, (kt % 2) * 256:(kt % 2) * 256 + 256],
                                       kvT[0][:, c, kt * P:(kt + 1) * P], kvT[1][:, c, kt * P:(kt + 1) * P],
                                       wv[0][:, c, two], wv[1][:, c, two], c == 0, c == DC - 1)
                elif kind == "pro":
                    c, half = j % 2, j // 2
                    for tt in range(TB):
                        last = t.transpose(dst[:, tt * P:(tt + 1) * P], y[:, half * TB + tt, c * P:(c + 1) * P], ident[:])
                elif kind == "out":
                    for tt in (2 * j, 2 * j + 1):
                        for head in range(2):
                            h = 2 * (hp - 1) + head if not known(hp, 0) else H0 - 2 + head
                            q = slice(tt * P, (tt + 1) * P)
                            last = mm3(t, dst[:, (tt % 2) * D:(tt % 2) * D + D], oT[0][:, head, q], oT[1][:, head, q],
                                       pick(wo[0][:], h), pick(wo[1][:], h), head == 0, head == 1)
                else:
                    return finish(n - 1, 1 - par, u, bank, between)
                last.then_inc(pj_full, 1)

            def scores(n, qt, par):
                if not (isinstance(n, int) and 4 * n + qt < 2):
                    pe.wait_ge(exp_done, 4 * n + qt - 1)
                for half in range(2):
                    span = slice(half * S, (half + 1) * S)
                    q = slice(qt * P, (qt + 1) * P)
                    last = mm3(t, ps_s[:, qt % 2, span], qT[0][:, par, q], qT[1][:, par, q], kT[0][:, par, span], kT[1][:, par, span], True, True)
                last.then_inc(s_full, 1)

            def turn(n, qt):
                pe.wait_ge(exp_done, 4 * n + qt + 1)
                for half in range(2):
                    m = 8 * n + 2 * qt + half
                    if not (isinstance(m, int) and m < 2):
                        pe.wait_ge(t_out, m - 1)
                    for k in range(4):
                        kt = 4 * half + k
                        last = t.transpose(ps_t[:, half, k * P:(k + 1) * P], prob[:, qt, kt * P:(kt + 1) * P], ident[:])
                    last.then_inc(t_full, 1)

            for j in range(4):
                use_bank(("pro", j), j, j % 2, 0, 0, 0, 0)
            pe.wait_ge(pj_out, 4)
            for j in range(3):
                use_bank(("qk", j), 4 + j, j % 2, -1, 1, 0, 0)

            def step(b, hp, par, u, bank):
                n = 8 * b + 2 * hp + par
                first = known(n, 0)
                pe.wait_ge(pj_out, u - 4 * par)
                for q, todo in enumerate(plan(b, hp, par)):
                    for qt in SCORES[q][:1 if todo == [FIN] else 2]:
                        scores(n, qt, par)
                    if q == 3 and ("qk", 0) in todo:
                        pe.wait_ge(pj_out, u)
                    for use in todo:
                        use_bank(use, u, bank, n, par, b + 1, hp, lambda: scores(n, 2, par))
                        u, bank = u + width(use), (bank + width(use)) % 2
                    if q:
                        turn(n, q - 1)
                    elif not first:
                        turn(n - 1, 3)
                return u, bank

            def pair(b, hp):
                u, bank = step(b, hp, 0, pj_start(b, hp), 1)
                step(b, hp, 1, u, bank)

            pe.wait_ge(big_lo, 2)
            batches(pe, pair)
            n, u = 8 * B - 1, pj_start(B - 1, 3) + 13
            turn(n, 3)
            free_bank(u)
            finish(n, 1, u, u % 2)
            pe.wait_ge(o_lo, n + 1)
            for j in range(2):
                use_bank(("out", j), u + 2 + j, (u + j) % 2, n, 1, B, 4)


E0, F0 = 16, 1024
C0 = (B * S + E0 - 1) // E0
FT0 = F0 // P
CT0 = C0 // P
FAR = 1 << 20


def statistics(dve, ve, x, stats, mv, var, tiles, done, bn_done, aggr_done, stats_ready):
    T = tiles
    for t in range(T):
        if t:
            dve.wait_ge(bn_done, T * done + t)
        ve.bn_stats(stats[:, t, :], x[:, t, :]).then_inc(bn_done, 1)
        if t:
            ve.bn_aggr(mv[:, t - 1, :], stats[:, t - 1, :]).then_inc(aggr_done, 1)
    dve.wait_ge(bn_done, T * done + T)
    dve.wait_ge(aggr_done, T * done + T - 1)
    ve.tensor_scalar(var[:, 0:T - 1], flat(mv[:, 0:T - 1, 1:2]), EPS, None, ALU.add).then_inc(stats_ready, 1)
    ve.bn_aggr(mv[:, T - 1, :], stats[:, T - 1, :]).then_inc(aggr_done, 1)
    dve.wait_ge(aggr_done, T * done + T)
    ve.tensor_scalar(var[:, T - 1:T], flat(mv[:, T - 1:T, 1:2]), EPS, None, ALU.add).then_inc(stats_ready, 1)


def each_batch(eng, batch):
    batch(0)
    with eng.Fori(1, B) as b:
        batch(b)


def pick4(view, b):
    return view[:, bass.ds(b, 1)].rearrange("p o t d -> p (o t) d")


def pick_cols(table, b, n):
    return table[:, n * b:n * b + n] if isinstance(b, int) else table[:, bass.ds(n * b, n)]


def last_axis(ap, n):
    return ap.rearrange("p (a o) -> p a o", o=1).to_broadcast([ap.shape[0], ap.shape[1], n])


def mid_axis(ap, n):
    return ap.rearrange("p (o a) -> p o a", o=1).to_broadcast([ap.shape[0], n, ap.shape[1]])


def normalise_and_score(nc, name, x_dram, wg_d, E, K, z, logits):
    with ExitStack() as ctx:
        def sb(n, shape, dt=F32):
            return ctx.enter_context(nc.sbuf_tensor(name + n, shape, dt))

        def sem(n):
            return ctx.enter_context(nc.semaphore(name + n))

        wg = sb("wg", [P, DC, E])
        x = sb("x", [P, B, TB, D])
        yT = sb("yT", [P, 2, DC, S])
        stats, mv = sb("stats", [P, 2, TB, 6]), sb("mv", [P, 2, TB, 2])
        var, rstd = sb("var", [P, 2, TB]), sb("rstd", [P, 2, TB])
        ps_t = ctx.enter_context(nc.psum_tensor(name + "T", [P, 2, DC, BANK], F32))
        ps_l = ctx.enter_context(nc.psum_tensor(name + "logit", [P, 2, BANK], F32))
        wg_load, x_load = sem("wg_load"), [sem("x_load0"), sem("x_load1")]
        bn_done, aggr_done, stats_ready, rstd_ready = sem("bn"), sem("aggr"), sem("stats_ready"), sem("rstd")
        z_ready, t_full, t_out = sem("z_ready"), sem("t_full"), sem("t_out")
        l_full, l_out = sem("l_full"), sem("l_out")
        xv = x_dram.rearrange("b (t p) d -> p b t d", p=P)

        def pairs(batch):
            for b in range(B):
                batch(b, b // 2, b % 2)

        block = ctx.enter_context(nc.Block())

        @block.sync
        def _(sp):
            nc.sync.dma_start(wg[:], wg_d.rearrange("(c p) e -> p c e", p=P)).then_inc(wg_load, 16)

            def batch(b, i, par):
                if b >= 2:
                    sp.wait_ge(x_load[par], 16 * i)
                nc.sync.dma_start(x[:, b], xv[:, b]).then_inc(x_load[par], 16)
            pairs(batch)

        @block.gpsimd
        def _(pool):
            def batch(b, i, par):
                pool.wait_ge(stats_ready, 2 * b + 2)
                nc.gpsimd.tensor_tensor(rstd[:, par], var[:, par], K.neg_half[:].to_broadcast([P, TB]), ALU.pow).then_inc(rstd_ready, 1)
            pairs(batch)

        @block.scalar
        def _(act):
            def batch(b, i, par):
                if b >= 2:
                    act.wait_ge(l_full, b - 1)
                for c in range(DC):
                    act.wait_ge(t_full, DC * b + c + 1)
                    nc.scalar.activation(yT[:, par, c, :], ps_t[:, par, c, :], ACT.Copy).then_inc(t_out, 1)
            pairs(batch)

        @block.tensor
        def _(pe):
            t_ = nc.tensor

            def score(b, par):
                pe.wait_ge(t_out, DC * b + DC)
                if b >= 2:
                    pe.wait_ge(l_out, b - 1)
                for t in range(TB):
                    for c in range(DC):
                        last = t_.matmul(ps_l[:, par, t * E:(t + 1) * E], yT[:, par, c, t * P:(t + 1) * P], wg[:, c, :],
                                         start=c == 0, stop=c == DC - 1)
                last.then_inc(l_full, 1)

            def batch(b, i, par):
                pe.wait_ge(z_ready, TB * b + TB)
                if b >= 2:
                    pe.wait_ge(t_out, DC * (b - 1))
                for c in range(DC):
                    for t in range(TB):
                        last = t_.transpose(ps_t[:, par, c, t * P:(t + 1) * P], z[:, TB * b + t, c * P:(c + 1) * P], K.ident[:])
                    last.then_inc(t_full, 1)
                if b:
                    score(b - 1, 1 - par)
            pe.wait_ge(wg_load, 16)
            pairs(batch)
            score(B - 1, 1)

        @block.vector
        def _(dve):
            ve = nc.vector

            def measure(b, i, par):
                dve.wait_ge(x_load[par], 16 * i + 16)
                if b >= 2:
                    dve.wait_ge(z_ready, TB * (b - 1))
                statistics(dve, ve, x[:, b], stats[:, par], mv[:, par], var[:, par], TB, b, bn_done, aggr_done, stats_ready)

            def keep_logits(b, par):
                dve.wait_ge(l_full, b + 1)
                ve.tensor_scalar(logits[:, pick_range(b, TB), :], ps_l[:, par, 0:TB * E].rearrange("p (t e) -> p t e", e=E),
                                 1.0, None, ALU.mult).then_inc(l_out, 1)

            def batch(b, i, par):
                if b < B - 1:
                    measure(b + 1, i + par, 1 - par)
                dve.wait_ge(rstd_ready, b + 1)
                for t in range(TB):
                    ve.tensor_scalar(z[:, TB * b + t, :], x[:, b, t, :], mv[:, par, t, 0:1], rstd[:, par, t:t + 1],
                                     ALU.subtract, ALU.mult).then_inc(z_ready, 1)
                if b >= 2:
                    keep_logits(b - 2, par)
            measure(0, 0, 0)
            pairs(batch)
            keep_logits(B - 2, 0)
            keep_logits(B - 1, 1)


def pick_range(b, n):
    return slice(n * b, n * b + n) if isinstance(b, int) else bass.ds(n * b, n)


def early(e, n):
    return isinstance(e, int) and e < n


def chain(dve, step):
    count = [0]

    def then(instruction):
        count[0] += 1
        instruction.then_inc(step, 1)
        dve.wait_ge(step, count[0])
    return then


def relative(ve, then, logits, peak, rel, E, ready):
    then(ve.tensor_reduce(peak[:], logits[:], AX.X, ALU.max, negate=True))
    ve.tensor_tensor(rel[:], logits[:], last_axis(peak[:], E), ALU.add).then_inc(ready, 1)


def first_zero(ve, then, rel, first, best, hot, K, E):
    then(ve.tensor_scalar(first[:], rel[:], 0.0, float(-FAR), ALU.is_equal, ALU.mult))
    then(ve.tensor_tensor(first[:], first[:], mid_axis(K.iota[:, 0:E], NT), ALU.add))
    then(ve.tensor_reduce(best[:], first[:], AX.X, ALU.min))
    then(ve.tensor_scalar(best[:], best[:], float(FAR), None, ALU.add))
    return ve.tensor_tensor(hot[:], mid_axis(K.iota[:, 0:E], NT), last_axis(best[:], E), ALU.is_equal)


def places(ve, then, in_tile, in_tiles, a, b):
    then(ve.tensor_copy(a[:], in_tiles))
    d = 1
    while d < NT:
        then(ve.tensor_tensor(b[:, d:], a[:, d:], a[:, 0:NT - d], ALU.add))
        then(ve.tensor_copy(b[:, 0:d], a[:, 0:d]))
        a, b = b, a
        d *= 2
    then(ve.tensor_tensor(b[:, 1:], in_tile[:, 1:], a[:, 0:NT - 1], ALU.add))
    then(ve.tensor_copy(b[:, 0:1], in_tile[:, 0:1]))
    return b, a


def layer0_route(nc, x1_dram, wg_d, K, tg, z, row_i, route_row, route_w):
    with ExitStack() as ctx:
        def sb(name, shape, dt=F32):
            return ctx.enter_context(nc.sbuf_tensor("r_" + name, shape, dt))

        def sem(name):
            return ctx.enter_context(nc.semaphore("r_" + name))

        logits, rel, ex, first, chosen, a, b = (sb(n, [P, NT, E0]) for n in ("logits", "rel", "ex", "first", "chosen", "sums_a", "sums_b"))
        peak, total, gate, best, loc, valid, row, off = (sb(n, [P, NT]) for n in ("peak", "total", "gate", "best", "loc", "valid", "row", "off"))
        normalise_and_score(nc, "rn_", x1_dram, wg_d, E0, K, z, logits)

        ps_c = ctx.enter_context(nc.psum_tensor("r_in_tile", [P, BANK], F32))
        ps_n = ctx.enter_context(nc.psum_tensor("r_in_tiles", [P, BANK], F32))
        rel_ready, exp_done, chosen_ready, counted, step = (
            sem(n) for n in ("rel", "exp", "chosen", "counted", "step"))
        block = ctx.enter_context(nc.Block())

        @block.scalar
        def _(act):
            act.wait_ge(rel_ready, 1)
            nc.scalar.activation(flat(ex[:]), flat(rel[:]), ACT.Exp).then_inc(exp_done, 1)

        @block.tensor
        def _(pe):
            pe.wait_ge(chosen_ready, 1)
            nc.tensor.matmul(ps_c[:, 0:NT * E0], K.before[:], flat(chosen[:]), start=True, stop=True)
            nc.tensor.matmul(ps_n[:, 0:NT * E0], K.ones[:], flat(chosen[:]), start=True, stop=True).then_inc(counted, 1)

        @block.vector
        def _(dve):
            ve = nc.vector
            then = chain(dve, step)
            relative(ve, then, logits, peak, rel, E0, rel_ready)
            dve.wait_ge(rel_ready, 1)
            first_zero(ve, then, rel, first, best, chosen, K, E0).then_inc(chosen_ready, 1)
            dve.wait_ge(chosen_ready, 1)
            dve.wait_ge(exp_done, 1)
            then(ve.tensor_reduce(total[:], ex[:], AX.X, ALU.add))
            then(ve.reciprocal(gate[:], total[:]))
            dve.wait_ge(counted, 1)
            view = [ps[:, 0:NT * E0].rearrange("p (t e) -> p t e", e=E0) for ps in (ps_c, ps_n)]
            place, _ = places(ve, then, view[0], view[1], a, b)
            then(ve.tensor_tensor(place[:], place[:], chosen[:], ALU.mult))
            then(ve.tensor_reduce(loc[:], place[:], AX.X, ALU.add))
            then(ve.tensor_scalar(valid[:], loc[:], float(C0), None, ALU.is_lt))
            then(ve.scalar_tensor_tensor(row[:], best[:], float(C0), loc[:], ALU.mult, ALU.add))
            then(ve.tensor_scalar(off[:], valid[:], float(-FAR), float(FAR), ALU.mult, ALU.add))
            then(ve.tensor_tensor(row_i[:], row[:], off[:], ALU.add))
            then(ve.tensor_scalar(loc[:], loc[:], float(C0 - 1), None, ALU.min))
            then(ve.scalar_tensor_tensor(route_row[:], best[:], float(C0), loc[:], ALU.mult, ALU.add))
            then(ve.scalar_tensor_tensor(route_w[:], gate[:], tg[:, 2:3], valid[:], ALU.mult, ALU.mult))


def e_at(view, e):
    return view[:, e] if isinstance(e, int) else pick4(view, e)


def layer0_experts(nc, z, row_i, d_in, w1_d, w2_d, d_out, K):
    with ExitStack() as ctx:
        def sb(name, shape, dt=F32):
            return ctx.enter_context(nc.sbuf_tensor("e_" + name, shape, dt))

        def sem(name):
            return ctx.enter_context(nc.semaphore("e_" + name))

        def psum(name, banks):
            return ctx.enter_context(nc.psum_tensor("e_" + name, [P, banks, BANK], F32))

        HB = FT0 // 2
        w1_in, w2_in = sb("w1_in", [P, 2, DC, F0]), sb("w2_in", [P, 2, FT0, D])
        w1 = [sb("w1_hi", [P, 2, DC, F0], F32R), sb("w1_lo", [P, 2, DC, F0], F32R)]
        w2 = [sb("w2_hi", [P, 2, FT0, D], F32R), sb("w2_lo", [P, 2, FT0, D], F32R)]
        rows = sb("rows", [P, 2, CT0, D])
        rT = [sb("rT_hi", [P, 2, DC, C0], F32R), sb("rT_lo", [P, 2, DC, C0], F32R)]
        hT = [sb("hT_hi", [P, 2, FT0, C0], F32R), sb("hT_lo", [P, 2, FT0, C0], F32R)]
        res = sb("res", [P, 2, CT0, D])
        ps_h, ps_t, ps_o = psum("h", HB), psum("t", 1), psum("o", 1)

        w1_load, w2_load, row_load, stored = ([sem(f"{n}{p}") for p in range(2)] for n in ("w1_load", "w2_load", "row_load", "stored"))
        w1_hi, w1_lo, w2_hi, w2_lo = sem("w1_hi"), sem("w1_lo"), sem("w2_hi"), sem("w2_lo")
        t_full, t_hi, t_out = sem("t_full"), sem("t_hi"), sem("t_out")
        h_full, h_hi, h_out = sem("h_full"), sem("h_hi"), sem("h_out")
        o_full, o_out = sem("o_full"), sem("o_out")

        w1_v = w1_d.rearrange("e (c p) f -> p e c f", p=P)
        w2_v = w2_d.rearrange("e (k p) m -> p e k m", p=P)
        in_v = d_in.rearrange("(e t p) d -> p e t d", p=P, t=CT0)
        out_v = d_out.rearrange("(e t p) d -> p e t d", p=P, t=CT0)

        def steps(eng, step):
            step(0, 0, 0)
            step(1, 0, 1)
            with eng.Fori(1, E0 // 2 - 1) as i:
                step(2 * i, i, 0)
                step(2 * i + 1, i, 1)
            step(E0 - 2, E0 // 2 - 1, 0)
            step(E0 - 1, E0 // 2 - 1, 1)

        block = ctx.enter_context(nc.Block())

        scattered = sem("scattered")

        @block.sync
        def _(sp):
            def load_w1(e, par):
                nc.sync.dma_start(w1_in[:, par], e_at(w1_v, e)).then_inc(w1_load[par], 16)

            def step(e, i, par):
                if known(e, 0):
                    load_w1(0, 0)
                    sp.wait_ge(scattered, 16 * NT)
                if not early(e, 2):
                    sp.wait_ge(t_full, e - 1)
                nc.sync.dma_start(rows[:, par], e_at(in_v, e)).then_inc(row_load[par], 16)
                if not early(e, 2):
                    sp.wait_ge(w1_lo, e - 1)
                if not known(e, 0):
                    load_w1(e, par)
                if not early(e, 2):
                    sp.wait_ge(w2_lo, e - 1)
                nc.sync.dma_start(w2_in[:, par], e_at(w2_v, e)).then_inc(w2_load[par], 16)
            steps(sp, step)

        @block.gpsimd
        def _(pool):
            def store(e, par):
                pool.wait_ge(o_out, e + 1)
                nc.gpsimd.dma_start(e_at(out_v, e), res[:, par]).then_inc(stored[par], 16)

            def scatter(tiles):
                for t in tiles:
                    nc.gpsimd.indirect_dma_start(d_in, bass.IndirectOffsetOnAxis(ap=row_i[:, t:t + 1], axis=0), z[:, t, :], None,
                                                 bounds_check=E0 * C0 - 1, oob_is_err=False).then_inc(scattered, 16)

            def step(e, i, par):
                if known(e, 1):
                    scatter(range(NT // 2, NT))
                pool.wait_ge(w1_hi, e + 1)
                nc.gpsimd.tensor_tensor(flat(w1[1][:, par]), flat(w1_in[:, par]), flat(w1[0][:, par]).bitcast(F32), ALU.subtract).then_inc(w1_lo, 1)
                if not early(e, 2):
                    store(e - 2, par)
            scatter(range(NT // 2))
            steps(pool, step)
            store(E0 - 2, 0)
            store(E0 - 1, 1)
            pool.wait_ge(stored[0], 8 * E0)
            pool.wait_ge(stored[1], 8 * E0)

        @block.scalar
        def _(act):
            a = nc.scalar.activation

            def split_w1(e, i, par):
                act.wait_ge(w1_load[par], 16 * i + 16)
                if not early(e, 2):
                    act.wait_ge(h_full, HB * e - HB)
                a(flat(w1[0][:, par]), flat(w1_in[:, par]), ACT.Copy).then_inc(w1_hi, 1)

            def split_w2(e, i, par):
                act.wait_ge(w2_load[par], 16 * i + 16)
                if not early(e, 2):
                    act.wait_ge(o_full, e - 1)
                a(flat(w2[0][:, par]), flat(w2_in[:, par]), ACT.Copy).then_inc(w2_hi, 1)

            def rows_hi(e, par):
                act.wait_ge(t_full, e + 1)
                a(flat(rT[0][:, par]), ps_t[:, 0, :], ACT.Copy).then_inc(t_hi, 1)

            def step(e, i, par):
                if not early(e, 2):
                    act.wait_ge(o_full, e - 1)
                for j in range(HB):
                    act.wait_ge(h_full, HB * e + j + 1)
                    a(flat(hT[0][:, par, 2 * j:2 * j + 2]), ps_h[:, j, :], ACT.Relu).then_inc(h_hi, 1)
                if not known(e, E0 - 1):
                    rows_hi(e + 1, 1 - par)
                    split_w1(e + 1, i + par, 1 - par)
                split_w2(e, i, par)

            split_w1(0, 0, 0)
            rows_hi(0, 0)
            steps(act, step)

        @block.vector
        def _(dve):
            ve = nc.vector

            def rows_lo(e, par):
                dve.wait_ge(t_hi, e + 1)
                ve.tensor_tensor(flat(rT[1][:, par]), ps_t[:, 0, :], flat(rT[0][:, par]).bitcast(F32), ALU.subtract).then_inc(t_out, 1)

            def result(e, i, par):
                dve.wait_ge(o_full, e + 1)
                if not early(e, 2):
                    dve.wait_ge(stored[par], 16 * i)
                ve.tensor_copy(flat(res[:, par]), ps_o[:, 0, :]).then_inc(o_out, 1)

            def step(e, i, par):
                for j in range(HB):
                    dve.wait_ge(h_hi, HB * e + j + 1)
                    part = slice(2 * j, 2 * j + 2)
                    ve.scalar_tensor_tensor(flat(hT[1][:, par, part]), ps_h[:, j, :], 0.0, flat(hT[0][:, par, part]).bitcast(F32),
                                            ALU.max, ALU.subtract).then_inc(h_out, 1)
                if not known(e, E0 - 1):
                    rows_lo(e + 1, 1 - par)
                dve.wait_ge(w2_hi, e + 1)
                ve.tensor_tensor(flat(w2[1][:, par]), flat(w2_in[:, par]), flat(w2[0][:, par]).bitcast(F32), ALU.subtract).then_inc(w2_lo, 1)
                if not known(e, 0):
                    result(e - 1, i if par else i - 1, 1 - par)

            rows_lo(0, 0)
            steps(dve, step)
            result(E0 - 1, E0 // 2 - 1, 1)

        @block.tensor
        def _(pe):
            t_ = nc.tensor

            def turn_rows(e, i, par):
                pe.wait_ge(row_load[par], 16 * i + 16)
                if not known(e, 0):
                    pe.wait_ge(t_out, e)
                for c in range(DC):
                    for t in range(CT0):
                        last = t_.transpose(ps_t[:, 0, c * C0 + t * P:c * C0 + (t + 1) * P], rows[:, par, t, c * P:(c + 1) * P], K.ident[:])
                last.then_inc(t_full, 1)

            def first_product(e, par):
                pe.wait_ge(t_out, e + 1)
                pe.wait_ge(w1_lo, e + 1)
                for j in range(HB):
                    if not known(e, 0):
                        pe.wait_ge(h_out, HB * (e - 1) + j + 1)
                    for f in (2 * j, 2 * j + 1):
                        for c in range(DC):
                            fs = slice(f * P, (f + 1) * P)
                            last = mm3(t_, ps_h[:, j, (f % 2) * C0:(f % 2 + 1) * C0], w1[0][:, par, c, fs], w1[1][:, par, c, fs],
                                       rT[0][:, par, c], rT[1][:, par, c], c == 0, c == DC - 1)
                    last.then_inc(h_full, 1)

            def second_product(e, par):
                pe.wait_ge(h_out, HB * e + HB)
                pe.wait_ge(w2_lo, e + 1)
                if not known(e, 0):
                    pe.wait_ge(o_out, e)
                for t in range(CT0):
                    rs = slice(t * P, (t + 1) * P)
                    for f in range(FT0):
                        last = mm3(t_, ps_o[:, 0, t * D:(t + 1) * D], hT[0][:, par, f, rs], hT[1][:, par, f, rs],
                                   w2[0][:, par, f], w2[1][:, par, f], f == 0, f == FT0 - 1)
                last.then_inc(o_full, 1)

            def step(e, i, par):
                first_product(e, par)
                if not known(e, E0 - 1):
                    turn_rows(e + 1, i + par, 1 - par)
                if not known(e, 0):
                    second_product(e - 1, 1 - par)

            turn_rows(0, 0, 0)
            steps(pe, step)
            second_product(E0 - 1, 1)


H1, DH1 = 16, 16
G1 = H1 // 4
PAIRS = H1 // 2
KT1 = S // P
VPAD = H1 * P + P
AHEAD = 5


def layer1_attention(nc, x1_dram, ctx_d, wqT_d, wkT_d, wvT_d, woT_d, route_row, route_w, d_out, tg, x3_dram, K):
    with ExitStack() as ctx:
        def sb(name, shape, dt=F32):
            return ctx.enter_context(nc.sbuf_tensor("c_" + name, shape, dt))

        def sem(name):
            return ctx.enter_context(nc.semaphore("c_" + name))

        prob = sb("prob", [P, KT1, S])
        w_in = prob[:, 0:3, :].rearrange("p a (c n) -> p a c n", c=DC)
        w_qkv = [sb("w_hi", [P, 3, DC, D], F32R), sb("w_lo", [P, 3, DC, D], F32R)]
        w_o = [sb("wo_hi", [P, G1, D], F32R), sb("wo_lo", [P, G1, D], F32R)]
        x_in, x_acc = sb("x_in", [P, TB, D]), sb("x_acc", [P, TB, D])
        y = sb("y", [P, TB, D])
        c_in = sb("c_in", [P, TB, D])
        v_tok = c_in[:].rearrange("p t (h d) -> p t h d", h=H1)
        row_now, w_now = sb("row_now", [P, TB], I32), sb("w_now", [P, TB])
        stats, mv = sb("stats", [P, TB, 6]), sb("mv", [P, TB, 2])
        var, rstd = sb("var", [P, TB]), sb("rstd", [P, TB])
        tT = [sb("tT_hi", [P, DC, S], F32R), sb("tT_lo", [P, DC, S], F32R)]
        q_tok = sb("q_tok", [P, TB, H1, 4, DH1], F32R)
        k_tok = sb("k_tok", [P, TB, H1, 4, DH1], F32R)
        q_rows = sb("q_rows", [P, PAIRS, S], F32R)
        k_rows = sb("k_rows", [P, PAIRS, S], F32R)
        v_cols = sb("v_cols", [P, KT1, VPAD], F32R)
        neg_max = sb("neg_max", [P, 2, TB, 4])
        max_parts = sb("max_parts", [P, TB, 2, 4], F32R)
        max_rows = sb("max_rows", [40, S], F32R)
        select = sb("select", [40, 4, P], F32R)
        one_cols = sb("one_cols", [P, 7 * 32], F32R)
        pT = [sb("pT_hi", [P, 2, KT1, S], F32R), sb("pT_lo", [P, 2, KT1, S], F32R)]
        o_norm = sb("o_norm", [P, S])
        oT = [sb("oT_hi", [P, G1, S], F32R), sb("oT_lo", [P, G1, S], F32R)]

        ps_m = ctx.enter_context(nc.psum_tensor("c_max", [P, 2, BANK], F32))
        ps_s = ctx.enter_context(nc.psum_tensor("c_scores", [P, 2, BANK], F32))
        ps_v = ctx.enter_context(nc.psum_tensor("c_values", [P, 2, BANK], F32))
        ps_z = ctx.enter_context(nc.psum_tensor("c_sums", [P, BANK], F32))
        pj = ctx.enter_context(nc.psum_tensor("c_pj", [P, BANK], F32))

        w_load, w_hi, w_lo = sem("w_load"), sem("w_hi"), sem("w_lo")
        cleared, set_up = sem("cleared"), sem("set_up")
        x_load, c_load, rows_set, fetch_done, x2_done = (sem(n) for n in ("x_load", "c_load", "rows_set", "fetch_done", "x2_done"))
        bn_done, aggr_done, stats_ready, rstd_ready, y_ready = (sem(n) for n in ("bn", "aggr", "stats", "rstd", "y"))
        pj_full = sem("pj_full")
        pj_hi = sem("pj_hi")
        pj_out = sem("pj_out")
        pj_out_act = sem("pj_out_act")
        v_hi, v_lo = sem("v_hi"), sem("v_lo")
        m_full, max_done, parts_hi, parts_lo = sem("m_full"), sem("max_done"), sem("parts_hi"), sem("parts_lo")
        s_full, exp_done, p_hi = sem("s_full"), sem("exp_done"), sem("p_hi")
        p_lo = [sem("p_lo0"), sem("p_lo1")]
        values_done, sums_out, inv_done, o_norm_done, o_hi, o_lo = (
            sem(n) for n in ("values_done", "sums_out", "inv_done", "o_norm_done", "o_hi", "o_lo"))
        acc_set, stored = sem("acc_set"), sem("stored")

        xv = x1_dram.rearrange("b (t p) d -> p b t d", p=P)
        cv = ctx_d.rearrange("b (t p) d -> p b t d", p=P)
        x3v = x3_dram.rearrange("b (t p) d -> p b t d", p=P)

        PLAN = {3: [("ctx", 0), ("ctx", 1)], 4: [("k", 0), ("k", 1)], 5: [("v", 0), ("v", 1)],
                6: [("y", 0), ("y", 1)], 7: [("q", 0), ("q", 1)]}
        PLAN.update({8 + p: [("q_rows", p), ("k_rows", p)] for p in range(PAIRS)})
        PREPARE = [use for h in sorted(PLAN) for use in PLAN[h]]
        HIGHS = [use for use in PREPARE if use[0] in ("ctx", "k", "y", "q")]
        BY_ACT = ("v", "q_rows", "k_rows")
        ACT_USES = sum(use[0] in BY_ACT for use in PREPARE)
        V_STEP = {10: 0, 11: 1, 14: 2}

        def uses(b, h):
            found = [("max", (h // 4 + 1) % 2)] if h % 4 == 3 and not (known(b, B - 1) and h == H1 - 1) else []
            if h == 2 and not known(b, 0):
                found += [("out", 0), ("out", 1)]
            return found + ([] if known(b, B - 1) else PLAN.get(h, []))

        ALL = len(PREPARE) + G1 + 2

        def pj_start(b):
            return len(PREPARE) + 1 if known(b, 0) else ALL * b + len(PREPARE) + 1 - 2

        def dve_start(b):
            return len(PREPARE) + 1 - ACT_USES if known(b, 0) else (ALL - ACT_USES) * b + len(PREPARE) + 1 - 2 - ACT_USES

        def halves(todo):
            first = 0 if todo and todo[0][0] == "out" else 1
            return todo[:first], todo[first:first + 1], todo[first + 1:]

        def whole(b):
            return [use for h in range(H1) for use in uses(b, h)]

        def out_of_bank(eng, b, i):
            seq = PREPARE if b is None else whole(b)
            by_act = sum(use[0] in BY_ACT for use in seq[:i + 1])
            if seq[i][0] in BY_ACT if i >= 0 else not known(b, 0):
                eng.wait_ge(pj_out_act, by_act if b is None else ACT_USES * b + (ACT_USES + by_act))
            else:
                eng.wait_ge(pj_out, i + 1 - by_act if b is None else dve_start(b) + (i + 1 - by_act))

        V_USE = max(i for i, use in enumerate(PREPARE) if use[0] == "v")

        def hi_index(use, b):
            return len(HIGHS) * b + HIGHS.index(use)

        def b_at(view, b):
            return view[:, b] if isinstance(b, int) else pick4(view, b)

        def run(eng, batch):
            batch(0)
            with eng.Fori(1, B - 1) as b:
                batch(b)
            batch(B - 1)

        def diagonal(g, part):
            wide = v_cols[:, :, g * 4 * P:g * 4 * P + 4 * (P + 2 * DH1)].rearrange("p k (j c) -> p k j c", j=4)
            return wide[:, :, :, part * DH1:(part + 1) * DH1]

        block = ctx.enter_context(nc.Block())

        Q_HIGH, Q_LOW = slice(0, 4, 2), slice(1, 4, 2)
        K_HIGH, K_LOW = slice(0, 2), slice(2, 4)

        def twice(two_tiles, t):
            return two_tiles[:, t * D:(t + 1) * D].rearrange("p (h o d) -> p h o d", h=H1, o=1).to_broadcast([P, H1, 2, DH1])

        @block.sync
        def _(sp):
            dma = nc.sync.dma_start
            for i, w in enumerate((wqT_d, wkT_d, wvT_d)):
                dma(w_in[:, i], w.rearrange("(c p) n -> p c n", p=P)).then_inc(w_load, 16)
            dma(x_in[:], xv[:, 0]).then_inc(x_load, 16)
            dma(c_in[:], cv[:, 0]).then_inc(c_load, 16)
            sp.wait_ge(w_lo, 1)
            wo_v = woT_d.rearrange("(g j d) n -> j d g n", g=G1, j=4)
            stage = w_in.rearrange("p a c n -> p (a c) n")
            for j in range(4):
                for part in range(2):
                    dma(stage[32 * j + 16 * part:32 * j + 16 * part + 16, 0:G1, :], wo_v[j]).then_inc(w_load, 16)

            def batch(b):
                if not known(b, B - 1):
                    sp.wait_ge(v_lo, G1 * b + G1)
                    dma(c_in[:], b_at(cv, b + 1)).then_inc(c_load, 16)
                if not known(b, 0):
                    out_of_bank(sp, b, 1)
                    dma(b_at(x3v, b - 1), x_acc[:]).then_inc(stored, 16)
                if not known(b, B - 1):
                    sp.wait_ge(acc_set, b + 1)
                    dma(x_in[:], b_at(xv, b + 1)).then_inc(x_load, 16)
            run(sp, batch)
            sp.wait_ge(pj_out, dve_start(B - 1) + len(whole(B - 1)) + 2)
            dma(x3v[:, B - 1], x_acc[:]).then_inc(stored, 16)
            sp.wait_ge(stored, 16 * B)

        @block.gpsimd
        def _(pool):
            g = nc.gpsimd
            g.memset(v_cols[:].bitcast(F32), 0.0).then_inc(cleared, 1)

            def fetch(b, t):
                if t == 0:
                    pool.wait_ge(rows_set, 2 * b + 2)
                    g.tensor_tensor(K.pool_scratch[:], K.neg_half[:], K.neg_half[:], ALU.mult).then_inc(cleared, 1)
                g.indirect_dma_start(y[:, t, :], None, d_out, bass.IndirectOffsetOnAxis(ap=row_now[:, t:t + 1], axis=0)).then_inc(fetch_done, 16)

            def inverse_std(b):
                pool.wait_ge(stats_ready, 2 * b + 2)
                g.tensor_tensor(rstd[:], var[:], K.neg_half[:].to_broadcast([P, TB]), ALU.pow).then_inc(rstd_ready, 1)

            def prob_low(n, par):
                pool.wait_ge(p_hi, 2 * n + 2)
                g.tensor_tensor(flat(pT[1][:, par, 2:4]), flat(prob[:, 2:4]), flat(pT[0][:, par, 2:4]).bitcast(F32), ALU.subtract).then_inc(p_lo[1], 1)

            for t in range(TB):
                fetch(0, t)
            inverse_std(0)

            def batch(b):
                for h in range(H1):
                    if h == 5 and not known(b, B - 1):
                        inverse_std(b + 1)
                    prob_low(H1 * b + h, h % 2)
                    if h < TB and not known(b, B - 1):
                        fetch(b + 1, h)
            run(pool, batch)

        @block.scalar
        def _(act):
            a = nc.scalar.activation

            def side(use, u, b):
                kind, i = use
                if kind in ("out", "max"):
                    return
                act.wait_ge(pj_full, u + 1)
                if kind in ("ctx", "y"):
                    a(tT[0][:, i, :], pj[:], ACT.Copy).then_inc(pj_hi, 1)
                elif kind in ("q", "k"):
                    dst, where = (q_tok, Q_HIGH) if kind == "q" else (k_tok, K_HIGH)
                    a(dst[:, 2 * i, :, where, :], twice(pj, 0), ACT.Copy)
                    a(dst[:, 2 * i + 1, :, where, :], twice(pj, 1), ACT.Copy).then_inc(pj_hi, 1)
                elif kind == "v":
                    a(flat(v_tok[:, 2 * i:2 * i + 2]), pj[:], ACT.Copy).then_inc(pj_out_act, 1)
                else:
                    dst = q_rows if kind == "q_rows" else k_rows
                    a(dst[:, i, :], pj[:], ACT.Copy).then_inc(pj_out_act, 1)

            def spread_v(m, g):
                act.wait_ge(cleared, 1)
                a(diagonal(g, 0), v_tok[:, :, 4 * g:4 * g + 4, :], ACT.Copy).then_inc(v_hi, 1)

            def exp(n, kt):
                act.wait_ge(s_full, 4 * n + kt + 1)
                if not known(n, 0) and kt % 2 == 0:
                    act.wait_ge(p_lo[kt // 2], n)
                a(prob[:, kt, :], ps_s[:, kt % 2, :], ACT.Exp).then_inc(exp_done, 1)

            def prob_high(n, par, half):
                if not (isinstance(n, int) and n < 2) and half == 0:
                    act.wait_ge(values_done, n - 1)
                act.wait_ge(exp_done, 4 * n + 2 * half + 2)
                two = slice(2 * half, 2 * half + 2)
                a(flat(pT[0][:, par, two]), flat(prob[:, two]), ACT.Copy).then_inc(p_hi, 1)

            def group_sums(m):
                act.wait_ge(values_done, 4 * m + 4)
                if not known(m, 0):
                    act.wait_ge(o_lo, m)
                a(o_norm[:], ps_z[:], ACT.Copy).then_inc(sums_out, 1)

            def group_high(m, g):
                act.wait_ge(o_norm_done, m + 1)
                a(oT[0][:, g, :], o_norm[:], ACT.Copy).then_inc(o_hi, 1)

            act.wait_ge(set_up, 6)
            a(flat(w_qkv[0][:]), flat(w_in), ACT.Copy).then_inc(w_hi, 1)
            act.wait_ge(w_load, 16 * (3 + 8))
            stage = w_in.rearrange("p a c n -> p (a c) n")
            a(flat(w_o[0][:]), flat(stage[:, 0:G1, :]), ACT.Copy).then_inc(w_hi, 1)
            for u, use in enumerate(PREPARE):
                side(use, u, 0)
            out_of_bank(act, None, V_USE)
            for g in range(3):
                spread_v(g, g)

            def batch(b):
                last = known(b, B - 1)
                u = pj_start(b)

                def sides(some):
                    nonlocal u
                    for use in some:
                        side(use, u, b + 1)
                        u += 1

                for h in range(H1):
                    n, par = H1 * b + h, h % 2
                    early_uses, late_uses, end_uses = halves(uses(b, h))
                    m, g = G1 * b + h // 4 - 1, (h // 4 - 1) % G1
                    if h % 4 == 1 and not (known(b, 0) and h == 1):
                        group_sums(m)
                    exp(n, 0)
                    exp(n, 1)
                    if h % 4 == 2 and not (known(b, 0) and h == 2):
                        group_high(m, g)
                    sides(early_uses)
                    prob_high(n, par, 0)
                    exp(n, 2)
                    exp(n, 3)
                    sides(late_uses)
                    prob_high(n, par, 1)
                    if h == 1:
                        spread_v(G1 * b + 3, 3)
                    if h in V_STEP and not last:
                        spread_v(G1 * b + 4 + V_STEP[h], V_STEP[h])
                    sides(end_uses)
            run(act, batch)
            group_sums(G1 * B - 1)
            group_high(G1 * B - 1, 3)

        @block.vector
        def _(dve):
            ve = nc.vector

            def lo(out, ps, hi):
                return ve.tensor_tensor(out, ps, hi.bitcast(F32), ALU.subtract)

            def side(use, u, b):
                kind, i = use
                if kind in BY_ACT:
                    return
                if kind in ("ctx", "y", "q", "k"):
                    dve.wait_ge(pj_hi, hi_index(use, b) + 1)
                else:
                    dve.wait_ge(pj_full, u + 1)
                if kind in ("ctx", "y"):
                    last = lo(tT[1][:, i, :], pj[:], tT[0][:, i, :])
                elif kind in ("q", "k"):
                    dst, high, low = (q_tok, Q_HIGH, Q_LOW) if kind == "q" else (k_tok, K_HIGH, K_LOW)
                    for t in range(2):
                        last = lo(dst[:, 2 * i + t, :, low, :], twice(pj, t), dst[:, 2 * i + t, :, high, :])
                elif kind == "max":
                    last = ve.tensor_copy(max_rows[32 * i:32 * i + 8, :], pj[0:8, :])
                else:
                    part = flat(x_acc[:, 2 * i:2 * i + 2, :])
                    last = ve.scalar_tensor_tensor(part, pj[:], tg[:, 1:2], part, ALU.mult, ALU.add)
                last.then_inc(pj_out, 1)

            def set_rows(b):
                ve.tensor_copy(row_now[:], pick_cols(route_row, b, TB)).then_inc(rows_set, 1)
                ve.tensor_copy(w_now[:], pick_cols(route_w, b, TB)).then_inc(rows_set, 1)

            def add_experts(b):
                dve.wait_ge(x_load, 16 * b + 16)
                dve.wait_ge(fetch_done, 16 * TB * (b + 1))
                for t in range(TB):
                    ve.scalar_tensor_tensor(x_in[:, t, :], y[:, t, :], w_now[:, t:t + 1], x_in[:, t, :], ALU.mult, ALU.add).then_inc(x2_done, 1)
                dve.wait_ge(x2_done, TB * b + TB)
                statistics(dve, ve, x_in, stats, mv, var, TB, b, bn_done, aggr_done, stats_ready)

            def normalise(b):
                dve.wait_ge(rstd_ready, b + 1)
                for t in range(TB):
                    ve.tensor_scalar(y[:, t, :], x_in[:, t, :], mv[:, t, 0:1], rstd[:, t:t + 1], ALU.subtract, ALU.mult).then_inc(y_ready, 1)

            def spread_v(m, g):
                dve.wait_ge(v_hi, m + 1)
                lo(diagonal(g, 1), v_tok[:, :, 4 * g:4 * g + 4, :], diagonal(g, 0)).then_inc(v_lo, 1)

            def maximum(n, h, qt):
                dve.wait_ge(m_full, 4 * n + qt + 1)
                ve.tensor_reduce(neg_max[:, h // 4 % 2, qt, h % 4:h % 4 + 1], ps_m[:, qt % 2, :], AX.X, ALU.max, negate=True).then_inc(max_done, 1)

            def split_maxima(m, slot):
                dve.wait_ge(max_done, 16 * m + 16)
                ve.tensor_copy(max_parts[:, :, 0, :], neg_max[:, slot]).then_inc(parts_hi, 1)
                dve.wait_ge(parts_hi, m + 1)
                lo(max_parts[:, :, 1, :], neg_max[:, slot], max_parts[:, :, 0, :]).then_inc(parts_lo, 1)

            def prob_low(n, par):
                dve.wait_ge(p_hi, 2 * n + 1)
                lo(flat(pT[1][:, par, 0:2]), flat(prob[:, 0:2]), flat(pT[0][:, par, 0:2])).then_inc(p_lo[0], 1)

            def invert_sums(m, quarter):
                if quarter == 0:
                    dve.wait_ge(sums_out, m + 1)
                q = slice(quarter * P, (quarter + 1) * P)
                ve.reciprocal(o_norm[:, q], o_norm[:, q]).then_inc(inv_done, 1)

            def group_norm(m, g):
                dve.wait_ge(inv_done, 4 * m + 4)
                ve.tensor_tensor(o_norm[:], ps_v[:, g % 2], o_norm[:], ALU.mult).then_inc(o_norm_done, 1)

            def group_low(m, g):
                dve.wait_ge(o_hi, m + 1)
                lo(oT[1][:, g, :], o_norm[:], oT[0][:, g, :]).then_inc(o_lo, 1)

            def keep_x2(b):
                if not known(b, 0):
                    dve.wait_ge(stored, 16 * b)
                ve.tensor_copy(x_acc[:], x_in[:]).then_inc(acc_set, 1)

            for at in (0, 32):
                rows = slice(at, at + 8)
                ve.tensor_tensor(select[rows], last_axis(K.ident[rows, at:at + 4], P), last_axis(K.ident[rows, at + 4:at + 8], P), ALU.add).then_inc(set_up, 1)
            ve.memset(one_cols[:, 0:96].bitcast(F32), 0.0).then_inc(set_up, 1)
            ve.memset(one_cols[:, 96:128].bitcast(F32), 1.0).then_inc(set_up, 1)
            ve.memset(one_cols[:, 128:].bitcast(F32), 0.0).then_inc(set_up, 1)
            dve.wait_ge(w_load, 48)
            ve.tensor_scalar(flat(w_in[:, 1]), flat(w_in[:, 1]), DH1 ** -0.5, None, ALU.mult).then_inc(set_up, 1)
            dve.wait_ge(w_hi, 1)
            lo(flat(w_qkv[1][:]), flat(w_in), flat(w_qkv[0][:])).then_inc(w_lo, 1)
            set_rows(0)
            add_experts(0)
            normalise(0)
            dve.wait_ge(w_hi, 2)
            stage = w_in.rearrange("p a c n -> p (a c) n")
            lo(flat(w_o[1][:]), flat(stage[:, 0:G1, :]), flat(w_o[0][:])).then_inc(w_lo, 1)
            for u, use in enumerate(PREPARE):
                side(use, u, 0)
            for g in range(3):
                spread_v(g, g)
            for n in range(AHEAD):
                for qt in range(TB):
                    maximum(n, n, qt)
                if n == 3:
                    split_maxima(0, 0)
            side(("max", 0), len(PREPARE), 0)

            def batch(b):
                first, last = known(b, 0), known(b, B - 1)
                u = pj_start(b)

                def sides(some):
                    nonlocal u
                    for use in some:
                        side(use, u, b + 1)
                        u += 1

                for h in range(H1):
                    n, par = H1 * b + h, h % 2
                    ahead = not (last and h + AHEAD >= H1)
                    early_uses, late_uses, end_uses = halves(uses(b, h))
                    m, g = G1 * b + h // 4 - 1, (h // 4 - 1) % G1
                    invert = h % 4 == 1 and not (first and h == 1)
                    if h == 0 and not last:
                        set_rows(b + 1)
                    for half in range(2):
                        if ahead:
                            maximum(n + AHEAD, h + AHEAD, 2 * half)
                            maximum(n + AHEAD, h + AHEAD, 2 * half + 1)
                        if h == 2 and half == 0 and not first:
                            dve.wait_ge(acc_set, b)
                        if h % 4 == 2 and half == 0 and not (first and h == 2):
                            group_low(m, g)
                        if invert:
                            invert_sums(m, 2 * half)
                        sides(late_uses if half else early_uses)
                        if half == 0:
                            prob_low(n, par)
                        if invert:
                            invert_sums(m, 2 * half + 1)
                    if invert:
                        group_norm(m, g)
                    if h == 1:
                        spread_v(G1 * b + 3, 3)
                    if h == 3:
                        keep_x2(b)
                    if not last:
                        if h in V_STEP:
                            spread_v(G1 * b + 4 + V_STEP[h], V_STEP[h])
                        if h == 4:
                            add_experts(b + 1)
                        elif h == 5:
                            normalise(b + 1)
                    if h % 4 == 2 and not (last and h == H1 - 2):
                        split_maxima(G1 * b + h // 4 + 1, (h // 4 + 1) % 2)
                    sides(end_uses)
                end[0] = u
            end = [0]
            run(dve, batch)
            for quarter in range(4):
                invert_sums(G1 * B - 1, quarter)
            group_norm(G1 * B - 1, 3)
            group_low(G1 * B - 1, 3)
            for half in range(2):
                side(("out", half), end[0] + half, B)

        @block.tensor
        def _(pe):
            t_ = nc.tensor

            def side(use, b):
                kind, i = use
                if kind in ("ctx", "y"):
                    src = c_in if kind == "ctx" else y
                    if i == 0:
                        if kind == "ctx":
                            pe.wait_ge(c_load, 16 * b + 16)
                        else:
                            pe.wait_ge(y_ready, TB * b + TB)
                    for t in range(TB):
                        last = t_.transpose(pj[:, t * P:(t + 1) * P], src[:, t, i * P:(i + 1) * P], K.ident[:])
                elif kind in ("q", "k", "v"):
                    w = "qkv".index(kind)
                    for t in range(2):
                        rows = slice((2 * i + t) * P, (2 * i + t + 1) * P)
                        for c in range(DC):
                            last = mm3(t_, pj[:, t * D:(t + 1) * D], tT[0][:, c, rows], tT[1][:, c, rows],
                                       w_qkv[0][:, w, c], w_qkv[1][:, w, c], c == 0, c == DC - 1)
                elif kind in ("q_rows", "k_rows"):
                    src = q_tok if kind == "q_rows" else k_tok
                    for t in range(TB):
                        last = t_.transpose(pj[:, t * P:(t + 1) * P].bitcast(F32R), flat(src[:, t, 2 * i:2 * i + 2]), K.ident_r[:])
                elif kind == "max":
                    for t in range(TB):
                        last = t_.transpose(pj[0:8, t * P:(t + 1) * P].bitcast(F32R), flat(max_parts[:, t]), K.ident_r[:])
                else:
                    for t in range(2):
                        q = slice((2 * i + t) * P, (2 * i + t + 1) * P)
                        for g in range(G1):
                            last = mm3(t_, pj[:, t * D:(t + 1) * D], oT[0][:, g, q], oT[1][:, g, q], w_o[0][:, g], w_o[1][:, g], g == 0, g == G1 - 1)
                last.then_inc(pj_full, 1)

            def head_rows(h):
                return slice(64 * (h % 2), 64 * (h % 2) + 64), h % H1 // 2

            def for_maximum(n, h, qt):
                if not (isinstance(n, int) and 4 * n + qt < 2):
                    pe.wait_ge(max_done, 4 * n + qt - 1)
                rows, p = head_rows(h)
                t_.matmul(ps_m[:, qt % 2, :], q_rows[rows, p, qt * P:(qt + 1) * P], k_rows[rows, p, :], start=True, stop=True).then_inc(m_full, 1)

            def scores(n, h, kt):
                if not (isinstance(n, int) and 4 * n + kt < 2):
                    pe.wait_ge(exp_done, 4 * n + kt - 1)
                rows, p = head_rows(h)
                slot = slice(32 * (h // 4 % 2), 32 * (h // 4 % 2) + 8)
                t_.matmul(ps_s[:, kt % 2, :], k_rows[rows, p, kt * P:(kt + 1) * P], q_rows[rows, p, :], start=True, stop=False)
                t_.matmul(ps_s[:, kt % 2, :], select[slot, h % 4, :], max_rows[slot, :], start=False, stop=True).then_inc(s_full, 1)

            def values(n, h, half):
                pe.wait_ge(p_lo[half], n + 1)
                for kt in (2 * half, 2 * half + 1):
                    for part in range(2):
                        ends = dict(start=h % 4 == 0 and kt == 0 and part == 0, stop=h % 4 == 3 and kt == KT1 - 1 and part == 1)
                        right = pT[part][:, h % 2, kt, :]
                        t_.matmul(ps_v[:, h // 4 % 2], v_cols[:, kt, h * P:(h + 1) * P], right, **ends)
                        last = t_.matmul(ps_z[:], one_cols[:, 96 - 32 * (h % 4):224 - 32 * (h % 4)], right, **ends)
                if half == 1:
                    last.then_inc(values_done, 1)

            def values_first(b, h, m):
                if h == 13:
                    pe.wait_ge(v_lo, G1 * b + 4)
                elif h == 1:
                    pe.wait_ge(v_lo, G1 * b + 3)
                if h % 4 == 1 and not known(m, 0):
                    pe.wait_ge(sums_out, m)
                    if not known(m, 1):
                        pe.wait_ge(o_norm_done, m - 1)

            pe.wait_ge(set_up, 5)
            pe.wait_ge(w_lo, 1)
            for u, use in enumerate(PREPARE):
                if u:
                    out_of_bank(pe, None, u - 1)
                side(use, 0)
            pe.wait_ge(w_lo, 2)
            out_of_bank(pe, None, len(PREPARE) - 1)
            for n in range(AHEAD):
                for qt in range(TB):
                    for_maximum(n, n, qt)
            pe.wait_ge(parts_lo, 1)
            side(("max", 0), 0)

            def batch(b):
                first, last = known(b, 0), known(b, B - 1)
                i = 0
                for h in range(H1):
                    n = H1 * b + h
                    ahead = not (last and h + AHEAD >= H1)
                    early_uses, late_uses, end_uses = halves(uses(b, h))
                    if h % 4 == 0:
                        out_of_bank(pe, b, i - 1)

                    def sides(some):
                        nonlocal i
                        for use in some:
                            out_of_bank(pe, b, i - 1)
                            if use[0] == "max":
                                pe.wait_ge(parts_lo, G1 * b + h // 4 + 2)
                            elif use == ("out", 0):
                                pe.wait_ge(o_lo, G1 * b)
                            side(use, b + 1)
                            i += 1

                    for half in range(2):
                        scores(n, h, 2 * half)
                        scores(n, h, 2 * half + 1)
                        if ahead:
                            for_maximum(n + AHEAD, h + AHEAD, 2 * half)
                            for_maximum(n + AHEAD, h + AHEAD, 2 * half + 1)
                        sides(late_uses if half else early_uses)
                        if not (first and h == 0):
                            if half == 0:
                                values_first(b, h, G1 * b + (h - 1) // 4)
                            values(n - 1, (h - 1) % H1, half)
                    sides(end_uses)
            run(pe, batch)
            n = H1 * B - 1
            values(n, H1 - 1, 0)
            values(n, H1 - 1, 1)
            pe.wait_ge(o_lo, G1 * B)
            for half in range(2):
                if half:
                    pe.wait_ge(pj_out, dve_start(B - 1) + len(whole(B - 1)) + 1)
                side(("out", half), B)


E1, F1 = 8, 512
TOP = 2
R1 = 512
NR = (TOP * B * S + E1 * (R1 - 1)) // R1
RT = R1 // P
FT1 = F1 // P


def layer1_gate(nc, x3_dram, wg_d, bias_d, K, tg, z, rows, weight, tile_expert):
    with ExitStack() as ctx:
        def sb(name, shape, dt=F32):
            return ctx.enter_context(nc.sbuf_tensor("g_" + name, shape, dt))

        def sem(name):
            return ctx.enter_context(nc.semaphore("g_" + name))

        J = B * S // R1
        gate_bias = sb("gate_bias", [P, E1])
        logits, rel, ex, scores, biased, first, one, two, both, a, b, picked = (sb(n, [P, NT, E1]) for n in (
            "logits", "rel", "ex", "scores", "biased", "first", "one", "two", "both", "sums_a", "sums_b", "picked"))
        peak, total, inverse, best, rank, offset = (sb(n, [P, NT]) for n in ("peak", "total", "inverse", "best", "rank", "offset"))
        base, ends = sb("base", [P, E1]), sb("ends", [P, E1])
        tiles_of = sb("tiles_of", [P, E1])
        over = sb("over", [P, E1, J])
        until = sb("until", [P, NR, E1])
        numbers = sb("numbers", [P, NR])
        starts = sb("starts", [P, J])
        found = sb("found", [P, NR])
        normalise_and_score(nc, "gn_", x3_dram, wg_d, E1, K, z, logits)

        ps_c = ctx.enter_context(nc.psum_tensor("g_in_tile", [P, BANK], F32))
        ps_n = ctx.enter_context(nc.psum_tensor("g_in_tiles", [P, BANK], F32))
        loaded, rel_ready, exp_done, chosen_ready, counted, step = (
            sem(n) for n in ("loaded", "rel", "exp", "chosen", "counted", "step"))
        block = ctx.enter_context(nc.Block())

        @block.sync
        def _(sp):
            nc.sync.dma_start(gate_bias[:], bias_d.rearrange("(o d) -> o d", o=1).to_broadcast([P, E1])).then_inc(loaded, 16)

        @block.scalar
        def _(act):
            act.wait_ge(rel_ready, 1)
            nc.scalar.activation(flat(ex[:]), flat(rel[:]), ACT.Exp).then_inc(exp_done, 1)

        @block.tensor
        def _(pe):
            pe.wait_ge(chosen_ready, 1)
            nc.tensor.matmul(ps_c[:, 0:NT * E1], K.before[:], flat(both[:]), start=True, stop=True)
            nc.tensor.matmul(ps_n[:, 0:NT * E1], K.ones[:], flat(both[:]), start=True, stop=True).then_inc(counted, 1)

        @block.vector
        def _(dve):
            ve = nc.vector
            then = chain(dve, step)
            relative(ve, then, logits, peak, rel, E1, rel_ready)
            for j in range(0, NR, E0):
                n = min(E0, NR - j)
                then(ve.tensor_scalar(numbers[:, j:j + n], K.iota[:, 0:n], float(j), None, ALU.add))
            then(ve.tensor_scalar(starts[:], numbers[:, 0:J], float(R1), None, ALU.mult))
            dve.wait_ge(loaded, 16)
            dve.wait_ge(exp_done, 1)
            then(ve.tensor_reduce(total[:], ex[:], AX.X, ALU.add))
            then(ve.reciprocal(inverse[:], total[:]))
            then(ve.tensor_tensor(scores[:], ex[:], last_axis(inverse[:], E1), ALU.mult))
            then(ve.tensor_tensor(biased[:], scores[:], mid_axis(gate_bias[:], NT), ALU.add))
            for hot in (one, two):
                then(ve.tensor_reduce(peak[:], biased[:], AX.X, ALU.max, negate=True))
                then(ve.tensor_tensor(rel[:], biased[:], last_axis(peak[:], E1), ALU.add))
                then(first_zero(ve, then, rel, first, best, hot, K, E1))
                if hot is one:
                    then(ve.scalar_tensor_tensor(flat(biased[:]), flat(one[:]), -3.0e38, flat(biased[:]), ALU.mult, ALU.add))
            ve.tensor_tensor(both[:], one[:], two[:], ALU.add).then_inc(chosen_ready, 1)
            for c, hot in enumerate((one, two)):
                then(ve.tensor_tensor(picked[:], hot[:], scores[:], ALU.mult))
                then(ve.tensor_reduce(total[:], picked[:], AX.X, ALU.add))
                then(ve.tensor_scalar(weight[:, c, :], total[:], tg[:, 3:4], None, ALU.mult))
            dve.wait_ge(counted, 1)
            view = [ps[:, 0:NT * E1].rearrange("p (t e) -> p t e", e=E1) for ps in (ps_c, ps_n)]
            place, sums = places(ve, then, view[0], view[1], a, b)
            then(ve.tensor_tensor(over[:], last_axis(sums[:, NT - 1, :], J), mid_axis(starts[:], E1), ALU.is_gt))
            then(ve.tensor_reduce(tiles_of[:], over[:], AX.X, ALU.add))
            then(ve.memset(base[:, 0:1], 0.0))
            for e in range(E1):
                then(ve.tensor_tensor(ends[:, e:e + 1], base[:, e:e + 1], tiles_of[:, e:e + 1], ALU.add))
                if e < E1 - 1:
                    then(ve.tensor_copy(base[:, e + 1:e + 2], ends[:, e:e + 1]))
            then(ve.tensor_tensor(until[:], last_axis(numbers[:], E1), mid_axis(ends[:], NR), ALU.is_ge))
            then(ve.tensor_reduce(found[:], until[:], AX.X, ALU.add))
            then(ve.tensor_scalar(tile_expert[:], found[:], float(E1 - 1), None, ALU.min))
            for c, hot in enumerate((one, two)):
                then(ve.tensor_tensor(picked[:], hot[:], place[:], ALU.mult))
                then(ve.tensor_reduce(rank[:], picked[:], AX.X, ALU.add))
                then(ve.tensor_tensor(picked[:], hot[:], mid_axis(base[:], NT), ALU.mult))
                then(ve.tensor_reduce(offset[:], picked[:], AX.X, ALU.add))
                then(ve.scalar_tensor_tensor(rows[:, c, :], offset[:], float(R1), rank[:], ALU.mult, ALU.add))


def layer1_experts(nc, K, x3_dram, w1_d, w3_d, w2_d, shared, z, rows, tile_expert, tg, rows_in, rows_out):
    with ExitStack() as ctx:
        def sb(name, shape, dt=F32):
            return ctx.enter_context(nc.sbuf_tensor("m_" + name, shape, dt))

        def sem(name):
            return ctx.enter_context(nc.semaphore("m_" + name))

        WN = DC * F1
        w_in = sb("w_in", [P, 3, WN])
        w = [sb("w_hi", [P, 2, 3, WN], F32R), sb("w_lo", [P, 2, 3, WN], F32R)]
        row_in = sb("row_in", [P, RT, D])
        rT = [sb("rT_hi", [P, 2, DC, R1], F32R), sb("rT_lo", [P, 2, DC, R1], F32R)]
        act_h = sb("act_h", [P, 2, R1])
        g = sb("g", [P, 2, R1])
        hT = [sb("hT_hi", [P, 2, FT1, R1], F32R), sb("hT_lo", [P, 2, FT1, R1], F32R)]
        res = sb("res", [P, RT, D])
        x = sb("x", [P, TB, D])
        ps_h = ctx.enter_context(nc.psum_tensor("m_h", [P, 2, 2, BANK], F32))
        ps_o = ctx.enter_context(nc.psum_tensor("m_o", [P, RT, D], F32))
        ps_t = ctx.enter_context(nc.psum_tensor("m_t", [P, DC, BANK], F32))

        x_load = sem("x_load")
        w_load, w_hi, w_lo = sem("w_load"), sem("w_hi"), sem("w_lo")
        w2_load, w2_hi, w2_lo = sem("w2_load"), sem("w2_hi"), sem("w2_lo")
        scattered, row_load, t_full, t_hi, t_out = (sem(n) for n in ("scattered", "row_load", "t_full", "t_hi", "t_out"))
        h_full, silu_done = sem("h_full"), sem("silu_done")
        g_ready = sem("g_ready")
        h_out = sem("h_out")
        o_full, o_out, stored = sem("o_full"), sem("o_out"), sem("stored")
        LAST = B + NR - 1

        views = [v.rearrange("e (c p) f -> p e c f", p=P) for v in (w1_d, w3_d, w2_d)]
        shared_views = [v.rearrange("(c p) f -> p c f", p=P) for v in shared]
        in_v = rows_in.rearrange("(j t p) d -> p j t d", t=RT, p=P)
        out_v = rows_out.rearrange("(j t p) d -> p j t d", t=RT, p=P)
        xv = x3_dram.rearrange("b (t p) d -> p b t d", p=P)

        def tiles(eng, step):
            step(B, 0)
            with eng.Fori(0, (NR - 3) // 2) as i:
                step(2 * i + (B + 1), 1)
                step(2 * i + (B + 2), 0)
            step(LAST - 1, 1)
            step(LAST, 0)

        assert NR % 2 == 1 and B % 2 == 0

        def weights_of(n):
            return 0 if isinstance(n, int) and n < B else n - (B - 1)

        block = ctx.enter_context(nc.Block())

        @block.sync
        def _(sp):
            dma = nc.sync.dma_start

            def load(j, src):
                dma(w_in[:, j].rearrange("p (c f) -> p c f", c=src.shape[1]), src).then_inc(w2_load if j == 2 else w_load, 16)

            def step(n):
                m = weights_of(n)
                j = n - (B - 1)
                at = slice(j, j + 1) if isinstance(j, int) else bass.ds(j, 1)
                e = sp.value_load(tile_expert[0:1, at], min_val=0, max_val=E1 - 1)
                sp.wait_ge(w_lo, 2 * m + 2)
                for i in range(2):
                    load(i, pick4(views[i], e))
                sp.wait_ge(w2_lo, m + 1)
                load(2, pick4(views[2], e))
                if known(n, B - 1):
                    sp.wait_ge(scattered, 16 * TOP * NT)
                else:
                    sp.wait_ge(t_full, n + 1)
                dma(row_in[:], in_v[:, j] if isinstance(j, int) else pick4(in_v, j)).then_inc(row_load, 16)

            def store(n):
                sp.wait_ge(o_out, n + 1)
                if isinstance(n, int) and n < B:
                    dst = xv[:, n]
                else:
                    dst = out_v[:, n - B] if isinstance(n, int) else pick4(out_v, n - B)
                dma(dst, res[:]).then_inc(stored, 16)

            for j in range(3):
                load(j, shared_views[j])
            for b in range(B):
                if b:
                    store(b - 1)
                dma(x[:], xv[:, b]).then_inc(x_load, 16)
            step(B - 1)
            step(B)
            store(B - 1)
            with sp.Fori(B + 1, LAST) as n:
                step(n)
                store(n - 1)
            store(LAST - 1)
            store(LAST)
            sp.wait_ge(stored, 16 * (LAST + 1))

        @block.gpsimd
        def _(pool):
            def lows(m, slot, some=(0, 1)):
                for j in some:
                    pool.wait_ge(w_hi, 2 * m + j + 1)
                    nc.gpsimd.tensor_tensor(w[1][:, slot, j], w_in[:, j], w[0][:, slot, j].bitcast(F32), ALU.subtract).then_inc(w_lo, 1)

            def scatter(i):
                for c in range(TOP):
                    nc.gpsimd.indirect_dma_start(rows_in, bass.IndirectOffsetOnAxis(ap=rows[:, c, i:i + 1], axis=0), z[:, i, :], None,
                                                 bounds_check=NR * R1 - 1, oob_is_err=False).then_inc(scattered, 16)

            def step(n, par, between=None, after=None):
                for f in range(FT1):
                    if between:
                        between(f)
                    pool.wait_ge(g_ready, 2 * FT1 * n + (2 * f + 2))
                    nc.gpsimd.tensor_tensor(hT[1][:, par, f], g[:, f % 2], hT[0][:, par, f].bitcast(F32), ALU.subtract).then_inc(h_out, 1)
                    if after and f >= FT1 - 2:
                        after(f - (FT1 - 2))

            lows(0, 0)
            for b in range(B):
                step(b, b % 2, lambda f: scatter(TB * b + f))
            lows(1, 1)

            def tile(n, par):
                step(n, par, after=None if known(n, LAST) else lambda j: lows(n - (B - 2), par, (j,)))
            tiles(pool, tile)

        @block.scalar
        def _(act):
            a = nc.scalar.activation

            def split(m, slot, some=(0, 1)):
                for j in some:
                    act.wait_ge(w_load, 32 * m + 32)
                    a(w[0][:, slot, j], w_in[:, j], ACT.Copy).then_inc(w_hi, 1)

            def split_w2(m, slot, n):
                act.wait_ge(w2_load, 16 * m + 16)
                if not known(n, 0):
                    act.wait_ge(o_full, n - 1)
                a(w[0][:, slot, 2], w_in[:, 2], ACT.Copy).then_inc(w2_hi, 1)

            def rows_hi(n, par):
                act.wait_ge(t_full, n + 1)
                for c in range(DC):
                    a(rT[0][:, par, c], ps_t[:, c, :], ACT.Copy).then_inc(t_hi, 1)

            def step(n, par, after=None):
                for f in range(FT1):
                    act.wait_ge(h_full, FT1 * n + f + 1)
                    if not known(n, 0) or f >= 2:
                        act.wait_ge(g_ready, 2 * FT1 * n + (2 * f - 2))
                    a(act_h[:, f % 2], ps_h[:, f % 2, 0], ACT.Silu).then_inc(silu_done, 1)
                    if after and f >= FT1 - 2:
                        after(f - (FT1 - 2))

            split(0, 0)
            split_w2(0, 0, 0)
            rows_hi(0, 0)
            for b in range(B):
                step(b, b % 2)
                if b < B - 1:
                    rows_hi(b + 1, (b + 1) % 2)
            split(1, 1)
            rows_hi(B, 0)

            def tile(n, par):
                split_w2(n - (B - 1), 1 - par, n)
                step(n, par, None if known(n, LAST) else lambda j: split(n - (B - 2), par, (j,)))
                if not known(n, LAST):
                    rows_hi(n + 1, 1 - par)
            tiles(act, tile)

        @block.vector
        def _(dve):
            ve = nc.vector

            def lo(out, value, hi):
                return ve.tensor_tensor(out, value, hi.bitcast(F32), ALU.subtract)

            def w2_low(m, slot):
                dve.wait_ge(w2_hi, m + 1)
                lo(w[1][:, slot, 2], w_in[:, 2], w[0][:, slot, 2]).then_inc(w2_lo, 1)

            def rows_lo(n, par):
                for c in range(DC):
                    dve.wait_ge(t_hi, DC * n + c + 1)
                    lo(rT[1][:, par, c], ps_t[:, c, :], rT[0][:, par, c]).then_inc(t_out, 1)

            def result(n):
                dve.wait_ge(o_full, n + 1)
                if isinstance(n, int) and n < B:
                    dve.wait_ge(x_load, 16 * n + 16)
                    if n:
                        dve.wait_ge(stored, 16 * n)
                    ve.scalar_tensor_tensor(flat(res[:]), flat(ps_o[:]), tg[:, 3:4], flat(x[:]), ALU.mult, ALU.add).then_inc(o_out, 1)
                else:
                    dve.wait_ge(stored, 16 * n)
                    ve.tensor_copy(flat(res[:]), flat(ps_o[:])).then_inc(o_out, 1)

            def step(n, par):
                for f in range(FT1):
                    dve.wait_ge(silu_done, FT1 * n + f + 1)
                    if f == 0 and not early(n, 2):
                        dve.wait_ge(o_full, n - 1)
                    ve.tensor_tensor(hT[0][:, par, f], act_h[:, f % 2], ps_h[:, f % 2, 1], ALU.mult).then_inc(g_ready, 1)
                    if not known(n, 0) or f >= 2:
                        dve.wait_ge(h_out, FT1 * n + f - 1)
                    ve.tensor_tensor(g[:, f % 2], act_h[:, f % 2], ps_h[:, f % 2, 1], ALU.mult).then_inc(g_ready, 1)

            w2_low(0, 0)
            rows_lo(0, 0)
            for b in range(B):
                step(b, b % 2)
                if b < B - 1:
                    rows_lo(b + 1, (b + 1) % 2)
                if b:
                    result(b - 1)
            rows_lo(B, 0)

            def tile(n, par):
                w2_low(n - (B - 1), 1 - par)
                step(n, par)
                if not known(n, LAST):
                    rows_lo(n + 1, 1 - par)
                result(n - 1)
            tiles(dve, tile)
            result(LAST)

        @block.tensor
        def _(pe):
            t_ = nc.tensor

            def first_products(n, par, slot):
                m = weights_of(n)
                pe.wait_ge(w_lo, 2 * m + 2)
                pe.wait_ge(t_out, DC * n + DC)
                for f in range(FT1):
                    if not known(n, 0) or f >= 2:
                        pe.wait_ge(g_ready, 2 * FT1 * n + (2 * f - 2))
                    for j in range(2):
                        for c in range(DC):
                            ws = slice(c * F1 + f * P, c * F1 + (f + 1) * P)
                            last = mm3(t_, ps_h[:, f % 2, j], w[0][:, slot, j, ws], w[1][:, slot, j, ws], rT[0][:, par, c], rT[1][:, par, c],
                                       c == 0, c == DC - 1)
                    last.then_inc(h_full, 1)

            def second_product(n, par, slot, m):
                pe.wait_ge(h_out, FT1 * n + FT1)
                pe.wait_ge(w2_lo, m + 1)
                if not known(n, 0):
                    pe.wait_ge(o_out, n)
                for t in range(RT):
                    rs = slice(t * P, (t + 1) * P)
                    for f in range(FT1):
                        last = mm3(t_, ps_o[:, t, :], hT[0][:, par, f, rs], hT[1][:, par, f, rs],
                                   w[0][:, slot, 2, f * D:(f + 1) * D], w[1][:, slot, 2, f * D:(f + 1) * D], f == 0, f == FT1 - 1)
                last.then_inc(o_full, 1)

            def turn_rows(n):
                if isinstance(n, int) and n < B:
                    src = z[:, TB * n:TB * n + TB]
                else:
                    src = row_in
                    pe.wait_ge(row_load, 16 * (n - B) + 16)
                if not known(n, 0):
                    pe.wait_ge(t_out, DC * n)
                for c in range(DC):
                    for t in range(RT):
                        last = t_.transpose(ps_t[:, c, t * P:(t + 1) * P], src[:, t, c * P:(c + 1) * P], K.ident[:])
                last.then_inc(t_full, 1)

            turn_rows(0)
            for b in range(B):
                first_products(b, b % 2, 0)
                if b < B - 1:
                    turn_rows(b + 1)
                if b:
                    second_product(b - 1, (b - 1) % 2, 0, 0)
            turn_rows(B)

            def tile(n, par):
                first_products(n, par, 1 - par)
                if not known(n, LAST):
                    turn_rows(n + 1)
                second_product(n - 1, 1 - par, 0 if known(n, B) else par, weights_of(n - 1))
            tiles(pe, tile)
            second_product(LAST, 0, 1, weights_of(LAST))


def layer1_gather(nc, x3_dram, rows, weight, rows_out, out_dram):
    with ExitStack() as ctx:
        def sb(name, shape, dt=F32):
            return ctx.enter_context(nc.sbuf_tensor("f_" + name, shape, dt))

        def sem(name):
            return ctx.enter_context(nc.semaphore("f_" + name))

        acc = sb("acc", [P, NT, D])
        parts = sb("parts", [P, NT, TOP, D])
        x_load, added, stored = sem("x_load"), sem("added"), sem("stored")
        fetched = [sem("fetched0"), sem("fetched1")]
        xv = x3_dram.rearrange("b (t p) d -> p b t d", p=P)
        ov = out_dram.rearrange("b (t p) d -> p b t d", p=P)
        block = ctx.enter_context(nc.Block())

        @block.sync
        def _(sp):
            for b in range(B):
                nc.sync.dma_start(acc[:, TB * b:TB * b + TB], xv[:, b]).then_inc(x_load, 16)
            for b in range(B):
                sp.wait_ge(added, TOP * TB * (b + 1))
                nc.sync.dma_start(ov[:, b], acc[:, TB * b:TB * b + TB]).then_inc(stored, 16)
            sp.wait_ge(stored, 16 * B)

        @block.gpsimd
        def _(pool):
            def wait(b):
                pool.wait_ge(fetched[b % 2], 16 * TB * TOP * (b // 2 + 1))

            for t in range(NT):
                if t % TB == 0 and t >= 2 * TB:
                    wait(t // TB - 2)
                for c in range(TOP):
                    nc.gpsimd.indirect_dma_start(parts[:, t, c, :], None, rows_out, bass.IndirectOffsetOnAxis(ap=rows[:, c, t:t + 1], axis=0)).then_inc(fetched[t // TB % 2], 16)
            wait(B - 2)
            wait(B - 1)

        @block.vector
        def _(dve):
            dve.wait_ge(x_load, 16 * B)
            for t in range(NT):
                if t % TB == 0:
                    dve.wait_ge(fetched[t // TB % 2], 16 * TB * TOP * (t // TB // 2 + 1))
                for c in range(TOP):
                    if c:
                        dve.wait_ge(added, TOP * t + c)
                    nc.vector.scalar_tensor_tensor(acc[:, t, :], parts[:, t, c, :], weight[:, c, t:t + 1], acc[:, t, :],
                                                   ALU.mult, ALU.add).then_inc(added, 1)


class Constants:

    def __init__(self, nc, ctx):
        def sb(name, shape, dt=F32):
            return ctx.enter_context(nc.sbuf_tensor("k_" + name, shape, dt))

        self.ident = sb("ident", [P, P])
        self.ident_r = sb("ident_r", [P, P], F32R)
        self.ones = sb("ones", [P, P])
        self.before = sb("before", [P, P])
        self.iota = sb("iota", [P, E0])
        self.neg_half = sb("neg_half", [P, 1])
        self.pool_scratch = sb("pool_scratch", [P, 1])
        self.iota_i = sb("iota_i", [P, E0], I32)

    def fill(self, nc, ctx):
        step = ctx.enter_context(nc.semaphore("k_step"))
        with nc.Block() as block:
            @block.gpsimd
            def _(pool):
                g = nc.gpsimd
                g.memset(self.ident[:], 0.0).then_inc(step, 1)
                g.memset(self.ones[:], 1.0).then_inc(step, 1)
                g.memset(self.before[:], 1.0).then_inc(step, 1)
                g.memset(self.neg_half[:], -0.5).then_inc(step, 1)
                g.iota(self.iota_i[:], pattern=[[1, E0]], base=0, channel_multiplier=0).then_inc(step, 1)
                pool.wait_ge(step, 5)
                g.affine_select(out=self.ident[:], in_=self.ident[:], compare_op=ALU.not_equal, fill=1.0, base=0,
                                pattern=[[-1, P]], channel_multiplier=1).then_inc(step, 1)
                g.affine_select(out=self.before[:], in_=self.before[:], compare_op=ALU.is_gt, fill=0.0, base=0,
                                pattern=[[1, P]], channel_multiplier=-1).then_inc(step, 1)
                g.tensor_copy(self.iota[:], self.iota_i[:]).then_inc(step, 1)
                pool.wait_ge(step, 8)
                g.tensor_copy(self.ident_r[:], self.ident[:]).then_inc(step, 1)
                pool.wait_ge(step, 9)


def flamingo(nc, t_in, out):
    with ExitStack() as ctx:
        def dram(name, shape):
            return nc.dram_tensor(name, shape, F32).ap()

        K = Constants(nc, ctx)
        tg = ctx.enter_context(nc.sbuf_tensor("tg", [P, 4], F32))
        x1, x3 = dram("x1_dram", (B, S, D)), dram("x3_dram", (B, S, D))
        rows0_in, rows0_out = dram("rows0_in_dram", (E0 * C0, D)), dram("rows0_out_dram", (E0 * C0, D))
        rows1_in, rows1_out = dram("rows1_in_dram", (NR * R1, D)), dram("rows1_out_dram", (NR * R1, D))
        K.fill(nc, ctx)
        layer0_attention(nc, tuple(t_in[n] for n in (
            "x", "ctx_1024", "g_xattn", "g_ffn", "L0_xattn_gamma_media", "L0_xattn_beta_media", "L0_xattn_gamma_lat",
            "L0_xattn_beta_lat", "L0_xattn_Wq", "L0_xattn_bq", "L0_xattn_Wkv", "L0_xattn_bkv", "L0_xattn_Wo", "L0_xattn_bo")),
            K.ident, tg, x1, (rows0_in, rows1_in))
        with ExitStack() as routed:
            route_row = routed.enter_context(nc.sbuf_tensor("route_row", [P, NT], I32))
            route_w = routed.enter_context(nc.sbuf_tensor("route_w", [P, NT], F32))
            with ExitStack() as normalised:
                z = normalised.enter_context(nc.sbuf_tensor("z0", [P, NT, D], F32))
                row_i = normalised.enter_context(nc.sbuf_tensor("row_i", [P, NT], I32))
                layer0_route(nc, x1, t_in["L0_ffn_Wg"], K, tg, z, row_i, route_row, route_w)
                layer0_experts(nc, z, row_i, rows0_in, t_in["L0_ffn_w1"], t_in["L0_ffn_w2"], rows0_out, K)
            layer1_attention(nc, x1, t_in["ctx_1024"], t_in["L1_xattn_w_q"], t_in["L1_xattn_w_k"], t_in["L1_xattn_w_v"],
                             t_in["L1_xattn_w_o"], route_row, route_w, rows0_out, tg, x3, K)
        rows = ctx.enter_context(nc.sbuf_tensor("rows", [P, TOP, NT], I32))
        weight = ctx.enter_context(nc.sbuf_tensor("weight", [P, TOP, NT], F32))
        tile_expert = ctx.enter_context(nc.sbuf_tensor("tile_expert", [P, NR], I32))
        with ExitStack() as normalised:
            z = normalised.enter_context(nc.sbuf_tensor("z", [P, NT, D], F32))
            layer1_gate(nc, x3, t_in["L1_ffn_gate_w"], t_in["L1_ffn_gate_bias"], K, tg, z, rows, weight, tile_expert)
            layer1_experts(nc, K, x3, t_in["L1_ffn_w1"], t_in["L1_ffn_w3"], t_in["L1_ffn_w2"],
                           (t_in["L1_ffn_sw1"], t_in["L1_ffn_sw3"], t_in["L1_ffn_sw2"]), z, rows, tile_expert, tg, rows1_in, rows1_out)
        layer1_gather(nc, x3, rows, weight, rows1_out, out)



def kernel(**inputs):
    import concourse.bacc as bacc
    from concourse.bass_utils import run_bass_kernel_spmd

    arrays = {k: np.asarray(v) for k, v in inputs.items()}
    for name in arrays:
        if name.startswith(("L1_xattn_w", "L1_ffn_w", "L1_ffn_sw")) or name == "L1_ffn_gate_w":
            arrays[name] = arrays[name].swapaxes(-1, -2)
    arrays = {k: np.ascontiguousarray(v) for k, v in arrays.items()}

    nc = bacc.Bacc("TRN2", target_bir_lowering=False, num_devices=1)
    t_in = {k: nc.dram_tensor(k + "_in", v.shape, mybir.dt.from_np(v.dtype), kind="ExternalInput").ap() for k, v in arrays.items()}
    out = nc.dram_tensor("out", (B, S, D), F32, kind="ExternalOutput").ap()
    flamingo(nc, t_in, out)
    r = run_bass_kernel_spmd(nc, [{k + "_in": v for k, v in arrays.items()}], core_ids=[0])
    return r.results[0]["out"]
```
